# Optimizing a Trainium2 kernel written in Bass

```python
import numpy as np
import jax
import jax.numpy as jnp

def _softmax(x, axis=-1):
    return jax.nn.softmax(x, axis=axis)

def _gelu(x):
    return jax.nn.gelu(x, approximate=True)

def _silu(x):
    return jax.nn.silu(x)

def _sigmoid(x):
    return jax.nn.sigmoid(x)

def _layernorm(x, axis=-1, eps=1e-05):
    m = jnp.mean(x, axis=axis, keepdims=True)
    v = jnp.var(x, axis=axis, keepdims=True)
    return (x - m) / jnp.sqrt(v + eps)

def _scatter_add(tgt, idx, src, axis=0):
    return tgt.at[idx].add(src)

def _segment_sum(src, seg, n):
    return jax.ops.segment_sum(src, seg, n)
kernel_name = 'mk_seq_postln_d1_jaxref_r4_b77ff8'

def setup_inputs(seed: int=0):
    np.random.seed(seed)
    _w = jnp.asarray

    def _L0_attn_setup():
        import jax, jax.numpy as jnp
        import numpy as np
        D_MODEL = 256
        D_STATE = 64
        D_CONV = 4
        EXPAND = 2
        HEADDIM = 64
        D_INNER = EXPAND * D_MODEL
        NHEADS = D_INNER // HEADDIM
        NGROUPS = 1
        CONV_DIM = D_INNER + 2 * NGROUPS * D_STATE
        D_IN_PROJ = 2 * D_INNER + 2 * NGROUPS * D_STATE + NHEADS
        BATCH, SEQLEN = (4, 512)

        def _mamba2_forward(x, W_in, conv_w, conv_b, dt_bias, A_log, D, norm_w, W_out):
            Bsz, L, _ = x.shape
            zxbcdt = x @ W_in
            z = zxbcdt[..., :D_INNER]
            xBC = zxbcdt[..., D_INNER:D_INNER + CONV_DIM]
            dt = zxbcdt[..., D_INNER + CONV_DIM:]
            dt = jax.nn.softplus(dt + dt_bias)
            xp = jnp.pad(xBC, ((0, 0), (D_CONV - 1, 0), (0, 0)))
            xc = sum((xp[:, k:k + L, :] * conv_w[:, k] for k in range(D_CONV)))
            xBC = jax.nn.silu(xc + conv_b)
            xh = xBC[..., :D_INNER].reshape(Bsz, L, NHEADS, HEADDIM)
            Bm = xBC[..., D_INNER:D_INNER + D_STATE]
            Cm = xBC[..., D_INNER + D_STATE:]
            A = -jnp.exp(A_log)

            def step(h, inp):
                dt_t, x_t, B_t, C_t = inp
                dA = jnp.exp(dt_t * A)
                h = h * dA[..., None, None] + (dt_t[..., None] * x_t)[..., None] * B_t[:, None, None, :]
                y_t = jnp.einsum('bhpn,bn->bhp', h, C_t)
                return (h, y_t)
            h0 = jnp.zeros((Bsz, NHEADS, HEADDIM, D_STATE), dtype=x.dtype)
            inputs = (jnp.moveaxis(dt, 1, 0), jnp.moveaxis(xh, 1, 0), jnp.moveaxis(Bm, 1, 0), jnp.moveaxis(Cm, 1, 0))
            _, ys = jax.lax.scan(step, h0, inputs)
            y = jnp.moveaxis(ys, 0, 1) + xh * D[None, None, :, None]
            y = y.reshape(Bsz, L, D_INNER)
            y = y * jax.nn.silu(z)
            y = y * jax.lax.rsqrt(jnp.mean(y * y, axis=-1, keepdims=True) + 1e-05) * norm_w
            return y @ W_out
        key = jax.random.key(seed)
        ks = jax.random.split(key, 8)
        x = jax.random.normal(ks[0], (BATCH, SEQLEN, D_MODEL), dtype=jnp.float32)
        W_in = jax.random.normal(ks[1], (D_MODEL, D_IN_PROJ), dtype=jnp.float32) * 0.02
        conv_w = jax.random.normal(ks[2], (CONV_DIM, D_CONV), dtype=jnp.float32) * 0.2
        conv_b = jnp.zeros((CONV_DIM,), dtype=jnp.float32)
        dt = jnp.exp(jax.random.uniform(ks[3], (NHEADS,)) * (np.log(0.1) - np.log(0.001)) + np.log(0.001))
        dt_bias = dt + jnp.log(-jnp.expm1(-dt))
        A_log = jnp.log(jax.random.uniform(ks[4], (NHEADS,), minval=1.0, maxval=16.0))
        D = jnp.ones((NHEADS,), dtype=jnp.float32)
        norm_w = jnp.ones((D_INNER,), dtype=jnp.float32)
        W_out = jax.random.normal(ks[5], (D_INNER, D_MODEL), dtype=jnp.float32) * 0.02
        return {'x': x, 'W_in': W_in, 'conv_w': conv_w, 'conv_b': conv_b, 'dt_bias': dt_bias, 'A_log': A_log, 'D': D, 'norm_w': norm_w, 'W_out': W_out}
    _L0_attn_in = _L0_attn_setup()

    def _L0_ffn_setup():
        import jax, jax.numpy as jnp
        import numpy as np
        H, I, E_ROUTED, TOP_K = (256, 704, 7, 2)
        B, S = (4, 512)

        def _expert(h, g, u, d):
            return jnp.einsum('...i,hi->...h', jax.nn.silu(h @ g.T) * (h @ u.T), d)
        key = jax.random.key(seed)
        ks = jax.random.split(key, 10)
        sc = 0.02
        return {'x': jax.random.normal(ks[0], (B, S, H), dtype=jnp.float32), 'sg': jax.random.normal(ks[1], (I, H), dtype=jnp.float32) * sc, 'su': jax.random.normal(ks[2], (I, H), dtype=jnp.float32) * sc, 'sd': jax.random.normal(ks[3], (H, I), dtype=jnp.float32) * sc, 'rg': jax.random.normal(ks[4], (E_ROUTED, I, H), dtype=jnp.float32) * sc, 'ru': jax.random.normal(ks[5], (E_ROUTED, I, H), dtype=jnp.float32) * sc, 'rd': jax.random.normal(ks[6], (E_ROUTED, H, I), dtype=jnp.float32) * sc, 'wr': jax.random.normal(ks[7], (E_ROUTED, H), dtype=jnp.float32) * sc, 'rb': jnp.zeros((E_ROUTED,), dtype=jnp.float32)}
    _L0_ffn_in = _L0_ffn_setup()
    _d = {'L0_attn_x': _L0_attn_in['x'], 'L0_attn_W_in': _L0_attn_in['W_in'], 'L0_attn_conv_w': _L0_attn_in['conv_w'], 'L0_attn_conv_b': _L0_attn_in['conv_b'], 'L0_attn_dt_bias': _L0_attn_in['dt_bias'], 'L0_attn_A_log': _L0_attn_in['A_log'], 'L0_attn_D': _L0_attn_in['D'], 'L0_attn_norm_w': _L0_attn_in['norm_w'], 'L0_attn_W_out': _L0_attn_in['W_out'], 'L0_ffn_sg': _L0_ffn_in['sg'], 'L0_ffn_su': _L0_ffn_in['su'], 'L0_ffn_sd': _L0_ffn_in['sd'], 'L0_ffn_rg': _L0_ffn_in['rg'], 'L0_ffn_ru': _L0_ffn_in['ru'], 'L0_ffn_rd': _L0_ffn_in['rd'], 'L0_ffn_wr': _L0_ffn_in['wr'], 'L0_ffn_rb': _L0_ffn_in['rb']}
    _x0 = _d['L0_attn_x']
    _d['L0_attn_x'] = jax.random.normal(jax.random.fold_in(jax.random.key(seed), 1), (4, 1024, 256), dtype=_x0.dtype)
    del _x0
    return _d

def reference(L0_attn_x, L0_attn_W_in, L0_attn_conv_w, L0_attn_conv_b, L0_attn_dt_bias, L0_attn_A_log, L0_attn_D, L0_attn_norm_w, L0_attn_W_out, L0_ffn_sg, L0_ffn_su, L0_ffn_sd, L0_ffn_rg, L0_ffn_ru, L0_ffn_rd, L0_ffn_wr, L0_ffn_rb):

    def _L0_attn_ref(x, W_in, conv_w, conv_b, dt_bias, A_log, D, norm_w, W_out):
        import jax, jax.numpy as jnp
        import numpy as np
        D_MODEL = 256
        D_STATE = 64
        D_CONV = 4
        EXPAND = 2
        HEADDIM = 64
        D_INNER = EXPAND * D_MODEL
        NHEADS = D_INNER // HEADDIM
        NGROUPS = 1
        CONV_DIM = D_INNER + 2 * NGROUPS * D_STATE
        D_IN_PROJ = 2 * D_INNER + 2 * NGROUPS * D_STATE + NHEADS
        BATCH, SEQLEN = (4, 512)

        def _mamba2_forward(x, W_in, conv_w, conv_b, dt_bias, A_log, D, norm_w, W_out):
            Bsz, L, _ = x.shape
            zxbcdt = x @ W_in
            z = zxbcdt[..., :D_INNER]
            xBC = zxbcdt[..., D_INNER:D_INNER + CONV_DIM]
            dt = zxbcdt[..., D_INNER + CONV_DIM:]
            dt = jax.nn.softplus(dt + dt_bias)
            xp = jnp.pad(xBC, ((0, 0), (D_CONV - 1, 0), (0, 0)))
            xc = sum((xp[:, k:k + L, :] * conv_w[:, k] for k in range(D_CONV)))
            xBC = jax.nn.silu(xc + conv_b)
            xh = xBC[..., :D_INNER].reshape(Bsz, L, NHEADS, HEADDIM)
            Bm = xBC[..., D_INNER:D_INNER + D_STATE]
            Cm = xBC[..., D_INNER + D_STATE:]
            A = -jnp.exp(A_log)

            def step(h, inp):
                dt_t, x_t, B_t, C_t = inp
                dA = jnp.exp(dt_t * A)
                h = h * dA[..., None, None] + (dt_t[..., None] * x_t)[..., None] * B_t[:, None, None, :]
                y_t = jnp.einsum('bhpn,bn->bhp', h, C_t)
                return (h, y_t)
            h0 = jnp.zeros((Bsz, NHEADS, HEADDIM, D_STATE), dtype=x.dtype)
            inputs = (jnp.moveaxis(dt, 1, 0), jnp.moveaxis(xh, 1, 0), jnp.moveaxis(Bm, 1, 0), jnp.moveaxis(Cm, 1, 0))
            _, ys = jax.lax.scan(step, h0, inputs)
            y = jnp.moveaxis(ys, 0, 1) + xh * D[None, None, :, None]
            y = y.reshape(Bsz, L, D_INNER)
            y = y * jax.nn.silu(z)
            y = y * jax.lax.rsqrt(jnp.mean(y * y, axis=-1, keepdims=True) + 1e-05) * norm_w
            return y @ W_out
        return _mamba2_forward(x, W_in, conv_w, conv_b, dt_bias, A_log, D, norm_w, W_out)

    def _L0_ffn_ref(x, sg, su, sd, rg, ru, rd, wr, rb):
        import jax, jax.numpy as jnp
        import numpy as np
        H, I, E_ROUTED, TOP_K = (256, 704, 7, 2)
        B, S = (4, 512)

        def _expert(h, g, u, d):
            return jnp.einsum('...i,hi->...h', jax.nn.silu(h @ g.T) * (h @ u.T), d)
        shared_out = _expert(x, sg, su, sd)
        logits = x @ wr.T + rb
        probs = jax.nn.softmax(logits, axis=-1)
        scores, idx = jax.lax.top_k(probs, TOP_K)
        scores = scores / scores.sum(axis=-1, keepdims=True)
        w = jnp.sum(scores[..., None] * jax.nn.one_hot(idx, E_ROUTED, dtype=x.dtype), axis=-2)
        out = shared_out
        for e in range(E_ROUTED):
            out = out + w[..., e:e + 1] * _expert(x, rg[e], ru[e], rd[e])
        return out
    x = L0_attn_x
    x = _layernorm(x + _L0_attn_ref(x, L0_attn_W_in, L0_attn_conv_w, L0_attn_conv_b, L0_attn_dt_bias, L0_attn_A_log, L0_attn_D, L0_attn_norm_w, L0_attn_W_out), axis=-1)
    x = _layernorm(x + _L0_ffn_ref(x, L0_ffn_sg, L0_ffn_su, L0_ffn_sd, L0_ffn_rg, L0_ffn_ru, L0_ffn_rd, L0_ffn_wr, L0_ffn_rb), axis=-1)
    return x

_drawn_inputs = setup_inputs


def setup_inputs(seed=0):
    import zlib

    import numpy as np

    out = dict(_drawn_inputs(seed))
    spreads = {'L0_attn_conv_b': (0.0, 0.1),
     'L0_attn_D': (1.0, 0.2),
     'L0_attn_norm_w': (1.0, 0.2),
     'L0_ffn_rb': (0.0, 0.8)}
    factors = {'L0_attn_dt_bias': 8.0,
     'L0_attn_A_log': 8.0,
     'L0_ffn_rg': 2.866,
     'L0_ffn_ru': 2.843,
     'L0_ffn_rd': 2.832,
     'L0_ffn_wr': 3.413}
    for name, (base, spread) in spreads.items():
        noise = np.random.default_rng([zlib.crc32(name.encode()), seed]).standard_normal(out[name].shape)
        drawn = base * np.exp(spread * noise) if base else spread * noise
        out[name] = jnp.asarray(drawn.astype(out[name].dtype))
    for name, factor in factors.items():
        out[name] = (out[name] * factor).astype(out[name].dtype)
    return out
```

```python
from contextlib import ExitStack

import numpy as np

import concourse.bass as bass
from concourse import mybir

F32 = mybir.dt.float32
F32R = mybir.dt.float32r
U32 = mybir.dt.uint32
I32 = mybir.dt.int32
ALU = mybir.AluOpType
ACT = mybir.ActivationFunctionType
AX_X = mybir.AxisListType.X

P = 128
BATCH, SEQ, DM = 4, 1024, 256
T = BATCH * SEQ
KT = DM // P
DI = 512
NST = 64
NH = 8
HD = DI // NH
NCONV = 4
NPROJ = 2 * DI + 2 * NST + NH
Z0, X0, BC0, DT0 = 0, DI, 2 * DI, 2 * DI + 2 * NST
Q = 128
NC = 4
BLK = NC * Q
NBLK = T // BLK
MX = DI // P
EPS = 1e-5

NE = 7
FF = 704
NCH = 6
TILE = 256
BIAS = 2
CAP = T + TILE
R0 = T
DUMMY = R0 + NE * CAP
NROWS = DUMMY + TILE
NTR = (2 * T + NE * (TILE - 1)) // TILE
NTR += NTR % 2
NTS = T // TILE
GU = 11 * P
DN = NCH * DM
WROW = KT * GU + DN


class Block:

    def __init__(self, b, par):
        self.b, self.par = b, par

    def next(self):
        return Block(self.b, 1) if self.par == 0 else Block(self.b + 1, 0)

    def prev(self):
        return Block(self.b, 0) if self.par else Block(self.b - 1, 1)

    def count(self, per, n):
        return self.b * (2 * per) + (self.par * per + n)


def count(k, per, n):
    v = k.count(per, n + BIAS)
    return max(v, BIAS) if isinstance(v, int) else v


def landed(k, loads):
    return (k.b + 1) * (16 * loads)


def sent(k, dmas):
    return k.b * (16 * dmas) + 16


class Steps:

    def __init__(self, per=0):
        self.per, self.n, self.k = per, 0, None

    def begin(self, k):
        self.k, self.n = k, 0

    def made(self, n):
        self.n += n
        return self.n if self.k is None else count(self.k, self.per, self.n)

    def end(self):
        assert self.n == self.per, (self.n, self.per)


def program(nc, x, xT, W_in, conv_w, conv_b, dt_bias, A_log, Dh, norm_w, W_out, experts, wr, rb, consts,
            xs, ys, out):
    with ExitStack() as ctx:
        keep = ctx.enter_context
        pos_all = keep(nc.sbuf_tensor("pos_all", [P, 2 * T // P], F32))
        pos_y = keep(nc.sbuf_tensor("pos_y", [P, 2 * T // P], U32))
        share_all = keep(nc.sbuf_tensor("share_all", [P, 2 * T // P], F32))
        base = keep(nc.sbuf_tensor("base", [P, NE], F32))
        cst = keep(nc.sbuf_tensor("cst", [P, NCONST], F32))
        table = keep(nc.sbuf_tensor("table", [1, 2, NTR], I32))
        pads = keep(nc.sbuf_tensor("pads", [1, NE], I32))
        zero = keep(nc.sbuf_tensor("zero", [P, 2 * DM], F32))
        mixer(nc, x, xT, W_in, conv_w, conv_b, dt_bias, A_log, Dh, norm_w, W_out, wr, rb, consts, xs,
              pos_all, share_all, base, cst)
        route(nc, xs, base, cst, table, pads, zero, pos_all, pos_y)
        moe(nc, experts, xs, ys, out, pos_y, share_all, cst, table)


C_ID = 0
C_INCL = C_ID + P
C_GTR = C_INCL + P
C_LESS = C_GTR + P
C_ONE = C_LESS + P
C_TIE = C_ONE + P
C_REG = C_TIE + NE * NE
C_T16 = C_REG + NE
C_TJ = C_T16 + NE * NTS
C_E = C_TJ + NE * NTR
NCONST = C_E + NE * NTR


def constants():
    c = np.zeros((P, NCONST), np.float32)
    k, t = np.arange(P)[:, None], np.arange(P)[None, :]
    for at, m in ((C_ID, k == t), (C_INCL, k <= t), (C_GTR, k > t), (C_LESS, k < t), (C_ONE, k >= 0)):
        c[:, at:at + P] = m
    i, j = np.arange(NE)[:, None], np.arange(NE)[None, :]
    c[:, C_TIE:C_REG] = (j < i).reshape(-1)
    c[:, C_REG:C_T16] = R0 + CAP * np.arange(NE)
    c[:, C_T16:C_TJ] = np.tile(TILE * np.arange(NTS), NE)
    c[:, C_TJ:C_E] = np.tile(np.arange(NTR), NE)
    c[:, C_E:] = np.repeat(np.arange(NE), NTR)
    return c


PF_USES = 11
DVE_F, DVE_B, POOL_B = 32, 60, 8
SERIES = [1.0 / (2 * i + 1) for i in range(9)]


def mixer(nc, x, xT, W_in, conv_w, conv_b, dt_bias, A_log, Dh, norm_w, W_out, wr, rb, consts, xs,
          pos_all, share_all, base, cst):
    with ExitStack() as ctx:
        def sb(name, shape, dt=F32):
            return ctx.enter_context(nc.sbuf_tensor(name, shape, dt))

        def bank(name):
            return ctx.enter_context(nc.psum_tensor(name, [P, 512], F32))

        def sem(name):
            return ctx.enter_context(nc.semaphore(name))

        def pair(name, shape, dt=F32):
            return [sb(f"{name}{i}", shape, dt) for i in range(2)]

        w_raw = sb("w_raw", [P, KT, NPROJ])
        w_hi = sb("w_hi", [P, KT, NPROJ], F32R)
        w_lo = sb("w_lo", [P, KT, NPROJ], F32R)
        cw = sb("cw", [P, 5, NCONV])
        cb = sb("cb", [P, 5])
        dtb = sb("dtb", [P, NH])
        alog = sb("alog", [P, NH])
        eA = sb("eA", [P, NH])
        Dp = sb("Dp", [P, NH])
        nw = sb("nw", [P, MX])
        wo_raw = sb("wo_raw", [P, MX, DM])
        wo = sb("wo", [P, MX, DM])
        wr_sb = sb("wr_sb", [P, KT, NE])
        rb_sb = sb("rb_sb", [P, NE])
        x_raw = sb("x_raw", [P, KT, BLK])
        x_hi = sb("x_hi", [P, KT, BLK], F32R)
        x_lo = sb("x_lo", [P, KT, BLK], F32R)
        cin = pair("cin", [P, 5, BLK + NCONV - 1])
        conv = sb("conv", [P, 5, BLK])
        xch = pair("xch", [P, MX, BLK])
        BT = pair("BT", [NST, BLK])
        CT = pair("CT", [NST, BLK])
        zs = pair("zs", [P, NC, DI])
        xres = pair("xres", [P, NC, DM])
        dt_raw = sb("dt_raw", [P, NC * NH])
        dt_n = sb("dt_n", [P, NC * NH])
        dt_u = sb("dt_u", [P, NC * NH])
        dt_s = sb("dt_s", [P, NC * NH])
        dt_q = sb("dt_q", [P, NC * NH])
        dt_h = sb("dt_h", [P, NC * NH])
        dt_m = sb("dt_m", [P, NC * NH])
        dts = pair("dts", [P, NC, NH])
        a = pair("a", [P, NC, NH])
        ce = pair("ce", [P, 3, NC, NH])
        x_tok = pair("x_tok", [P, DI])
        B_tok = pair("B_tok", [P, NST])
        am = sb("am", [P, NH, Q])
        E = sb("E", [P, NH, Q])
        Gm = sb("Gm", [P, Q])
        M = pair("M", [P, NH, Q])
        xdt = pair("xdt", [P, DI])
        xw = pair("xw", [P, DI])
        xD = sb("xD", [P, DI])
        t1 = sb("t1", [P, DI])
        yz = pair("yz", [P, DI])
        junk = sb("junk", [P, DI])
        ss = pair("ss", [P, 1])
        rs = pair("rs", [P, 1])
        yT = sb("yT", [P, MX, Q])
        S = sb("S", [NST, DI])
        S2 = sb("S2", [NST, DI])
        r = sb("r", [P, DM])
        st6 = sb("st6", [P, 6])
        mv = sb("mv", [P, 2])
        rln = sb("rln", [P, 1])
        mhalf = sb("mhalf", [P, 1])
        x1 = pair("x1", [P, NC, DM])
        x1T = sb("x1T", [P, NC, KT, Q])
        lg = sb("lg", [P, NC, NE])
        mx = sb("mx", [P, NC])
        pe_ = sb("pe_", [P, NC, NE])
        pr = sb("pr", [P, NC, NE])
        sm = sb("sm", [P, NC])
        gt = sb("gt", [P, NC, NE, NE])
        eq = sb("eq", [P, NC, NE, NE])
        rank = sb("rank", [P, NC, NE])
        oh = sb("oh", [P, 2, NC, NE])
        mask = sb("mask", [P, NC, NE])
        cbase = sb("cbase", [P, NC, NE])
        slot = sb("slot", [P, NC, NE])
        tmp = sb("tmp", [P, 2, NC, NE])
        posf = sb("posf", [P, 2, NC])
        top = sb("top", [P, 2, NC])
        posu = [sb(f"posu{i}", [P, 2, NC], U32) for i in range(2)]

        PF = [bank("PF0"), bank("PF1")]
        PX, PG, PD0, PD1, PY, PI = [bank(n) for n in ("PX", "PG", "PD0", "PD1", "PY", "PI")]

        s_w = sem("s_w")
        s_small = sem("s_small")
        s_xT = sem("s_xT")
        s_xres = [sem("s_xres0"), sem("s_xres1")]
        s_whi, s_wlo, s_eA = sem("s_whi"), sem("s_wlo"), sem("s_eA")
        s_set = sem("s_set")
        s_wo = sem("s_wo")
        s_xhi, s_xlo, s_dtn, s_dtu, s_dt, s_ce = [sem(n) for n in
                                                  ("s_xhi", "s_xlo", "s_dtn", "s_dtu", "s_dt", "s_ce")]
        s_pf, s_pff = sem("s_pf"), sem("s_pff")
        s_conv, s_sil = sem("s_conv"), sem("s_sil")
        s_S0 = sem("s_S0")
        s_hold = sem("s_hold")
        s_mh = sem("s_mh")
        names = ("s_XT s_xt s_Bt s_G s_D s_am s_E s_Gm s_xw s_M s_Y s_yi s_t1 s_ds s_S s_xD s_yz s_ss s_rs "
                 "s_YT s_yT s_O s_r s_mv s_r1 s_x1").split()
        (s_XT, s_xt, s_Bt, s_G, s_D, s_am, s_E, s_Gm, s_xw, s_M, s_Y, s_yi, s_t1, s_ds, s_S, s_xD, s_yz,
         s_ss, s_rs, s_YT, s_yT, s_O, s_r, s_mv, s_r1, s_x1) = [sem(n) for n in names]
        s_RT, s_rT, s_lg, s_lm, s_ex, s_mask, s_rk, s_pos = [sem(n) for n in
            ("s_RT", "s_rT", "s_lg", "s_lm", "s_ex", "s_mask", "s_rk", "s_pos")]
        s_sc, s_scd = sem("s_sc"), sem("s_scd")
        s_xo = [sem("s_xo0"), sem("s_xo1")]
        s_dvf, s_dvb, s_pb = sem("s_dvf"), sem("s_dvb"), sem("s_pb")

        block = ctx.enter_context(nc.Block())

        def loop(eng, front, back):
            front(Block(0, 0))
            with eng.Fori(0, NBLK // 2 - 1) as b:
                front(Block(b, 1))
                back(Block(b, 0))
                front(Block(b + 1, 0))
                back(Block(b, 1))
            last = NBLK // 2 - 1
            front(Block(last, 1))
            back(Block(last, 0))
            back(Block(last, 1))

        def start(eng, *sems):
            for s in sems:
                eng.sem_inc(s, BIAS)

        xT_v = xT
        x_v = x.rearrange("(g p) d -> p g d", p=P)
        xs_v = xs[0:T, :].rearrange("(g p) d -> p g d", p=P)

        @block.sync
        def _(sp):
            for s in s_xo:
                sp.sem_inc(s, 16)
            sp.dma_start(cst[:, :], consts).then_inc(s_small, 16)
            sp.dma_start(w_raw[:, :, :], W_in.rearrange("(a p) n -> p a n", p=P)).then_inc(s_w, 16)
            for dst, src in ((cw[:, :, :], conv_w.rearrange("(m p) k -> p m k", p=P)), (cb[:, :], conv_b),
                             (dtb[:, :], dt_bias), (alog[:, :], A_log), (Dp[:, :], Dh), (nw[:, :], norm_w),
                             (wo_raw[:, :, :], W_out.rearrange("(m p) n -> p m n", p=P)),
                             (wr_sb[:, :, :], wr), (rb_sb[:, :], rb)):
                sp.dma_start(dst, src).then_inc(s_small, 16)

            def front(k):
                sp.wait_ge(s_xhi, count(k, 1, 0))
                sp.sem_inc(s_hold, 1)
                sp.wait_ge(s_xlo, count(k, 1, 0))
                sp.sem_inc(s_hold, 1)
                t0 = k.b * (2 * BLK) + k.par * BLK
                sp.dma_start(x_raw[:, :, :], xT_v[:, :, bass.ds(t0, BLK)]).then_inc(s_xT, 16)
                sp.wait_ge(s_r, count(k, NC, -NC))
                sp.sem_inc(s_hold, 1)
                g0 = k.b * (2 * NC) + k.par * NC
                sp.dma_start(xres[k.par][:, :, :], x_v[:, bass.ds(g0, NC), :]).then_inc(s_xres[k.par], 16)

            def back(k):
                sp.wait_ge(s_x1, count(k, NC, NC))
                sp.sem_inc(s_hold, 1)
                g0 = k.b * (2 * NC) + k.par * NC
                sp.dma_start(xs_v[:, bass.ds(g0, NC), :], x1[k.par][:, :, :]).then_inc(s_xo[k.par], 16)

            loop(sp, front, back)
            for i in range(2):
                sp.wait_ge(s_xo[i], 16 * (NBLK // 2) + 16)

        @block.gpsimd
        def _(pool):
            start(pool, s_scd, s_am, s_xD, s_rs, s_r1, s_pb)
            nc.gpsimd.memset(mhalf[:, :], -0.5).then_inc(s_mh, 1)
            pool.wait_ge(s_mh, 1)
            chain = Steps(POOL_B)
            pool.wait_ge(s_small, 160)

            def front(k):
                pass

            def back(k):
                chain.begin(Block(k.b, k.par))

                def decays(c):
                    pool.wait_ge(s_dt, count(k, 1, 1))
                    pool.wait_ge(s_D, count(k, NC, c))
                    nc.gpsimd.tensor_tensor(
                        am[:, :, :], a[k.par][:, c, :].unsqueeze(2).to_broadcast([P, NH, Q]),
                        cst[:, C_INCL:C_INCL + Q].unsqueeze(1).to_broadcast([P, NH, Q]),
                        ALU.mult).then_inc(s_am, 1)

                def skip(c):
                    pool.wait_ge(s_xt, count(k, NC, c + 1))
                    pool.wait_ge(s_yz, count(k, NC, c))
                    nc.gpsimd.tensor_tensor(
                        xD[:, :].rearrange("p (h d) -> p h d", h=NH),
                        x_tok[c % 2][:, :].rearrange("p (h d) -> p h d", h=NH),
                        Dp[:, :].unsqueeze(2).to_broadcast([P, NH, HD]), ALU.mult).then_inc(s_xD, 1)

                def norms(c):
                    pool.wait_ge(s_ss, count(k, NC, c + 1))
                    pool.wait_ge(s_r, count(k, NC, c - 1))
                    pool.sem_inc(s_hold, 1)
                    nc.gpsimd.tensor_scalar(rs[c % 2][:, :], ss[c % 2][:, :], 1.0 / DI, EPS,
                                                       ALU.mult, ALU.add).then_inc(s_pb, 1)
                    pool.wait_ge(s_pb, chain.made(1))
                    nc.gpsimd.tensor_tensor(rs[c % 2][:, :], rs[c % 2][:, :], mhalf[:, :],
                                            ALU.pow).then_inc(s_rs, 1)
                    pool.wait_ge(s_mv, count(k, NC, c + 1))
                    pool.wait_ge(s_x1, count(k, NC, c))
                    pool.sem_inc(s_hold, 1)
                    nc.gpsimd.tensor_scalar(rln[:, :], mv[:, 1:2], EPS, None, ALU.add).then_inc(s_pb, 1)
                    pool.wait_ge(s_pb, chain.made(1))
                    nc.gpsimd.tensor_tensor(rln[:, :], rln[:, :], mhalf[:, :], ALU.pow).then_inc(s_r1, 1)

                for c in range(NC):
                    decays(c)
                    skip(c)
                    if c:
                        norms(c - 1)
                norms(NC - 1)
                chain.end()
                pool.wait_ge(s_pos, count(k, 1, 1))
                pool.sem_inc(s_hold, 1)
                for i in range(2):
                    for c in range(NC):
                        pool.indirect_dma_start(
                            out=xs, out_offset=bass.IndirectOffsetOnAxis(ap=posu[k.par][:, i, c:c + 1], axis=0),
                            in_=x1[k.par][:, c, :], in_offset=None).then_inc(s_sc, 16)
                pool.wait_ge(s_sc, k.count(16 * 2 * NC, 16 * 2 * NC))
                pool.sem_inc(s_scd, 1)

            loop(pool, front, back)

        @block.scalar
        def _(act):
            start(act, s_xhi, s_dtu, s_ce, s_pff, s_sil, s_xt, s_Bt, s_E, s_ss, s_yT, s_rT, s_ex)
            act.wait_ge(s_w, 16)
            nc.scalar.activation(w_hi[:, :, :], w_raw[:, :, :], ACT.Copy).then_inc(s_whi, 1)
            act.wait_ge(s_small, 160)
            nc.scalar.activation(eA[:, :], alog[:, :], ACT.Exp).then_inc(s_eA, 1)

            def front(k):
                act.wait_ge(s_xT, k.count(16, 16))
                act.wait_ge(s_pf, count(k, PF_USES, 0))
                nc.scalar.activation(x_hi[:, :, :], x_raw[:, :, :], ACT.Copy).then_inc(s_xhi, 1)
                act.wait_ge(s_dt, count(k, 1, 0))
                act.wait_ge(s_pf, count(k, PF_USES, 1))
                nc.scalar.activation(dt_raw[:, :], PF[k.par][:, 0:NC * NH], ACT.Copy).then_inc(s_pff, 1)
                act.wait_ge(s_conv, count(k, 5, 0))
                for u, m in enumerate((4, 0, 1, 2, 3), 1):
                    act.wait_ge(s_pf, count(k, PF_USES, u + 1))
                    nc.scalar.activation(cin[k.par][:, m, NCONV - 1:], PF[(u + k.par) % 2][:, :],
                                         ACT.Copy).then_inc(s_pff, 1)
                act.wait_ge(s_dtn, count(k, 1, 1))
                nc.scalar.activation(dt_u[:, :], dt_n[:, :], ACT.Exp).then_inc(s_dtu, 1)
                act.wait_ge(s_yz, count(k, NC, -NC))
                act.wait_ge(s_S, count(k, NC, -NC))
                act.wait_ge(s_pf, count(k, PF_USES, 7))
                nc.scalar.activation(ce[k.par][:, :, :, :].rearrange("p i c h -> p (i c h)"),
                                     PF[(6 + k.par) % 2][:, 0:3 * NC * NH], ACT.Exp).then_inc(s_pff, 1)
                for c in range(NC):
                    act.wait_ge(s_pf, count(k, PF_USES, 8 + c))
                    nc.scalar.activation(zs[k.par][:, c, :], PF[(7 + c + k.par) % 2][:, :],
                                         ACT.Silu).then_inc(s_pff, 1)
                act.wait_ge(s_XT, count(k, NC, 1 - NC))
                act.wait_ge(s_conv, count(k, 5, 1))
                nc.scalar.activation(BT[k.par][:, :], conv[0:NST, 4, :], ACT.Silu).then_inc(s_sil, 1)
                nc.scalar.activation(CT[k.par][:, :], conv[NST:P, 4, :], ACT.Silu).then_inc(s_sil, 1)
                for m in range(MX):
                    act.wait_ge(s_conv, count(k, 5, m + 2))
                    nc.scalar.activation(xch[k.par][:, m, :], conv[:, m, :], ACT.Silu).then_inc(s_sil, 1)

            def back(k):
                def tokens(c):
                    act.wait_ge(s_XT, count(k, NC, c + 1))
                    act.wait_ge(s_yz, count(k, NC, c - 1))
                    act.wait_ge(s_xD, count(k, NC, c - 1))
                    nc.scalar.activation(x_tok[c % 2][:, :], PX[:, :], ACT.Copy).then_inc(s_xt, 1)
                    act.wait_ge(s_G, count(k, NC, c + 1))
                    act.wait_ge(s_ds, count(k, NC, c - 1))
                    nc.scalar.activation(B_tok[c % 2][:, :], PG[:, Q:Q + NST], ACT.Copy).then_inc(s_Bt, 1)
                    act.wait_ge(s_D, count(k, NC, c + 1))
                    act.wait_ge(s_M, count(k, NC, c))
                    nc.scalar.activation(E[:, 0:4, :].rearrange("p h t -> p (h t)"), PD0[:, :], ACT.Exp)
                    nc.scalar.activation(E[:, 4:8, :].rearrange("p h t -> p (h t)"), PD1[:, :],
                                         ACT.Exp).then_inc(s_E, 1)

                def gated(c):
                    act.wait_ge(s_yz, count(k, NC, c + 1))
                    act.wait_ge(s_rs, count(k, NC, c - 1))
                    nc.scalar.activation(junk[:, :], yz[c % 2][:, :], ACT.Square,
                                         accum_out=ss[c % 2][:, :]).then_inc(s_ss, 1)
                    act.wait_ge(s_YT, count(k, NC, c + 1))
                    act.wait_ge(s_O, count(k, NC, c))
                    nc.scalar.activation(yT[:, :, :].rearrange("p m t -> p (m t)"), PX[:, :],
                                         ACT.Copy).then_inc(s_yT, 1)

                for c in range(NC):
                    tokens(c)
                    if c:
                        gated(c - 1)
                gated(NC - 1)
                for half in range(2):
                    act.wait_ge(s_RT, count(k, 2, half + 1))
                    act.wait_ge(s_lg, count(k, 1, 0))
                    nc.scalar.activation(x1T[:, 2 * half:2 * half + 2, :, :].rearrange("p c a t -> p (c a t)"),
                                         PX[:, :], ACT.Copy).then_inc(s_rT, 1)
                act.wait_ge(s_lm, count(k, 1, 1))
                nc.scalar.activation(pe_[:, :, :], lg[:, :, :], ACT.Exp).then_inc(s_ex, 1)

            loop(act, front, back)

        @block.vector
        def _(dve):
            start(dve, s_xlo, s_dtn, s_dt, s_conv, s_S0, s_Gm, s_xw, s_M, s_t1, s_S, s_yz, s_r, s_mv, s_x1,
                  s_lm, s_mask, s_pos, s_dvf, s_dvb)
            dve.wait_ge(s_whi, 1)
            nc.vector.tensor_tensor(w_lo[:, :, :], w_raw[:, :, :], w_hi[:, :, :].bitcast(F32),
                                    ALU.subtract).then_inc(s_wlo, 1)
            dve.wait_ge(s_small, 160)
            for m in range(MX):
                nc.vector.tensor_scalar(wo[:, m, :], wo_raw[:, m, :], nw[:, m:m + 1], None,
                                        ALU.mult).then_inc(s_wo, 1)
            nc.vector.tensor_copy(base[:, :], cst[:, C_REG:C_REG + NE]).then_inc(s_set, 1)
            dve.wait_ge(s_eA, 1)
            dve.wait_ge(s_set, 1)
            F = Steps(DVE_F)
            B = Steps(DVE_B)
            V = nc.vector

            def front(k):
                F.begin(k)
                dve.wait_ge(s_xhi, count(k, 1, 1))
                V.tensor_tensor(x_lo[:, :, :], x_raw[:, :, :], x_hi[:, :, :].bitcast(F32),
                                ALU.subtract).then_inc(s_xlo, 1)
                halo = cin[k.par][:, :, 0:NCONV - 1]
                if k.par == 0:
                    V.memset(halo, 0.0).then_inc(s_dvf, 1)
                    dve.wait_ge(s_dvf, F.made(1))
                else:
                    V.tensor_copy(halo, cin[0][:, :, BLK:]).then_inc(s_dvf, 1)
                    dve.wait_ge(s_dvf, F.made(1))
                dve.wait_ge(s_pff, count(k, PF_USES, 1))
                heads = [P, NC, NH]
                v3 = lambda t: t[:, :].rearrange("p (c h) -> p c h", c=NC)
                V.tensor_tensor(v3(dt_s), v3(dt_raw), dtb[:, :].unsqueeze(1).to_broadcast(heads), ALU.add).then_inc(s_dvf, 1)
                dve.wait_ge(s_dvf, F.made(1))
                V.tensor_scalar(dt_m[:, :], dt_s[:, :], 0.0, None, ALU.max).then_inc(s_dvf, 1)
                F.made(1)
                V.scalar_tensor_tensor(out=dt_n[:, :], in0=dt_s[:, :], scalar=-1.0, in1=dt_s[:, :],
                                       op0=ALU.mult, op1=ALU.min).then_inc(s_dtn, 1)
                dve.wait_ge(s_dtu, count(k, 1, 1))
                V.tensor_scalar(dt_q[:, :], dt_u[:, :], 2.0, None, ALU.add).then_inc(s_dvf, 1)
                dve.wait_ge(s_dvf, F.made(1))
                V.reciprocal(dt_q[:, :], dt_q[:, :]).then_inc(s_dvf, 1)
                dve.wait_ge(s_dvf, F.made(1))
                V.tensor_tensor(dt_s[:, :], dt_u[:, :], dt_q[:, :], ALU.mult).then_inc(s_dvf, 1)
                dve.wait_ge(s_dvf, F.made(1))
                V.tensor_tensor(dt_q[:, :], dt_s[:, :], dt_s[:, :], ALU.mult).then_inc(s_dvf, 1)
                dve.wait_ge(s_dvf, F.made(1))
                V.tensor_scalar(dt_h[:, :], dt_q[:, :], SERIES[8], None, ALU.mult).then_inc(s_dvf, 1)
                dve.wait_ge(s_dvf, F.made(1))
                for i in range(7, 0, -1):
                    V.scalar_tensor_tensor(out=dt_h[:, :], in0=dt_h[:, :], scalar=SERIES[i],
                                                  in1=dt_q[:, :], op0=ALU.add, op1=ALU.mult).then_inc(s_dvf, 1)
                    dve.wait_ge(s_dvf, F.made(1))
                V.scalar_tensor_tensor(out=dt_h[:, :], in0=dt_h[:, :], scalar=1.0, in1=dt_s[:, :],
                                              op0=ALU.add, op1=ALU.mult).then_inc(s_dvf, 1)
                dve.wait_ge(s_dvf, F.made(1))
                dve.wait_ge(s_am, count(k, NC, -NC))
                V.scalar_tensor_tensor(out=dts[k.par][:, :, :].rearrange("p c h -> p (c h)"),
                                              in0=dt_h[:, :], scalar=2.0, in1=dt_m[:, :],
                                              op0=ALU.mult, op1=ALU.add).then_inc(s_dvf, 1)
                dve.wait_ge(s_dvf, F.made(1))
                V.scalar_tensor_tensor(out=a[k.par][:, :, :], in0=dts[k.par][:, :, :], scalar=-1.0,
                                       in1=eA[:, :].unsqueeze(1).to_broadcast(heads),
                                       op0=ALU.mult, op1=ALU.mult).then_inc(s_dt, 1)
                dve.wait_ge(s_sil, count(k, 6, 0))
                for u, m in enumerate((4, 0, 1, 2, 3)):
                    dve.wait_ge(s_pff, count(k, PF_USES, u + 2))
                    src = cin[k.par][:, m, :]
                    ins = V.tensor_scalar(conv[:, m, :], src[:, 0:BLK], cw[:, m, 0:1], cb[:, m:m + 1],
                                          ALU.mult, ALU.add)
                    for tap in range(1, NCONV):
                        ins.then_inc(s_dvf, 1)
                        dve.wait_ge(s_dvf, F.made(1))
                        ins = V.scalar_tensor_tensor(out=conv[:, m, :], in0=src[:, tap:tap + BLK],
                                                     scalar=cw[:, m, tap:tap + 1], in1=conv[:, m, :],
                                                     op0=ALU.mult, op1=ALU.add)
                    ins.then_inc(s_conv, 1)
                F.end()

            def h64(ap):
                return ap.rearrange("p (h d) -> p h d", h=NH)

            def back(k):
                B.begin(k)
                if k.par == 0:
                    V.memset(S[:, :], 0.0).then_inc(s_S0, 1)

                def weights(c):
                    dve.wait_ge(s_xt, count(k, NC, c + 1))
                    dve.wait_ge(s_Y, count(k, NC, c - 1))
                    V.tensor_tensor(h64(xdt[c % 2][:, :]), h64(x_tok[c % 2][:, :]),
                                           dts[k.par][:, c, :].unsqueeze(2).to_broadcast([P, NH, HD]), ALU.mult).then_inc(s_dvb, 1)
                    dve.wait_ge(s_dvb, B.made(1))
                    if c == 0:
                        dve.wait_ge(s_pff, count(k, PF_USES, 7))
                    dve.wait_ge(s_ds, count(k, NC, c - 1))
                    V.tensor_tensor(h64(xw[c % 2][:, :]), h64(xdt[c % 2][:, :]),
                                    ce[k.par][:, 1, c, :].unsqueeze(2).to_broadcast([P, NH, HD]),
                                    ALU.mult).then_inc(s_xw, 1)
                    dve.wait_ge(s_Bt, count(k, NC, c + 1))
                    V.tensor_tensor(Gm[:, :], PG[:, 0:Q], cst[:, C_INCL:C_INCL + Q], ALU.mult).then_inc(s_Gm, 1)
                    dve.wait_ge(s_Gm, count(k, NC, c + 1))
                    dve.wait_ge(s_E, count(k, NC, c + 1))
                    V.tensor_tensor(M[c % 2][:, :, :], E[:, :, :],
                                    Gm[:, :].unsqueeze(1).to_broadcast([P, NH, Q]), ALU.mult).then_inc(s_M, 1)

                def outputs(c):
                    dve.wait_ge(s_yi, count(k, NC, c + 1))
                    V.tensor_tensor(h64(t1[:, :]), h64(PI[:, :]),
                                    ce[k.par][:, 0, c, :].unsqueeze(2).to_broadcast([P, NH, HD]),
                                    ALU.mult).then_inc(s_t1, 1)
                    V.tensor_tensor(h64(S2[:, :]), h64(S[:, :]),
                                           ce[k.par][0:NST, 2, c, :].unsqueeze(2).to_broadcast([NST, NH, HD]),
                                           ALU.mult).then_inc(s_dvb, 1)
                    dve.wait_ge(s_dvb, B.made(1))
                    dve.wait_ge(s_Y, count(k, NC, c + 1))
                    V.tensor_tensor(t1[:, :], t1[:, :], PY[:, :], ALU.add).then_inc(s_dvb, 1)
                    B.made(1)
                    dve.wait_ge(s_ds, count(k, NC, c + 1))
                    V.tensor_tensor(S[:, :], S2[:, :], PI[0:NST, :], ALU.add).then_inc(s_S, 1)
                    dve.wait_ge(s_dvb, B.made(0))
                    dve.wait_ge(s_xD, count(k, NC, c + 1))
                    V.tensor_tensor(t1[:, :], t1[:, :], xD[:, :], ALU.add).then_inc(s_dvb, 1)
                    dve.wait_ge(s_dvb, B.made(1))
                    dve.wait_ge(s_ss, count(k, NC, c - 1))
                    dve.wait_ge(s_YT, count(k, NC, c - 1))
                    V.tensor_tensor(yz[c % 2][:, :], t1[:, :], zs[k.par][:, c, :], ALU.mult).then_inc(s_yz, 1)

                def finish(c):
                    if c == 0:
                        dve.wait_ge(s_xres[k.par], landed(k, 1))
                        dve.wait_ge(s_scd, count(k, 1, 0))
                        dve.wait_ge(s_xo[k.par], sent(k, 1))
                    dve.wait_ge(s_x1, count(k, NC, c))
                    dve.wait_ge(s_O, count(k, NC, c + 1))
                    dve.wait_ge(s_rs, count(k, NC, c + 1))
                    V.scalar_tensor_tensor(out=r[:, :], in0=PG[:, DM:2 * DM], scalar=rs[c % 2][:, :],
                                           in1=xres[k.par][:, c, :], op0=ALU.mult, op1=ALU.add).then_inc(s_r, 1)
                    dve.wait_ge(s_r, count(k, NC, c + 1))
                    V.bn_stats(st6[:, :], r[:, :]).then_inc(s_dvb, 1)
                    dve.wait_ge(s_dvb, B.made(1))
                    dve.sem_inc(s_hold, 1)
                    V.bn_aggr(mv[:, :], st6[:, :]).then_inc(s_mv, 1)
                    dve.wait_ge(s_r1, count(k, NC, c + 1))
                    V.tensor_scalar(x1[k.par][:, c, :], r[:, :], mv[:, 0:1], rln[:, :], ALU.subtract,
                                    ALU.mult).then_inc(s_x1, 1)

                for c in range(NC):
                    weights(c)
                    outputs(c)
                    if c:
                        finish(c - 1)
                finish(NC - 1)
                router(k)
                B.end()

            def router(k):
                ce4 = [P, NC, NE]
                c44 = [P, NC, NE, NE]
                dve.wait_ge(s_lg, count(k, 1, 1))
                V.tensor_tensor(lg[:, :, :], PG[:, 0:NC * NE].rearrange("p (c e) -> p c e", c=NC),
                                       rb_sb[:, :].unsqueeze(1).to_broadcast(ce4), ALU.add).then_inc(s_dvb, 1)
                dve.wait_ge(s_dvb, B.made(1))
                V.tensor_reduce(mx[:, :], lg[:, :, :], AX_X, ALU.max).then_inc(s_dvb, 1)
                dve.wait_ge(s_dvb, B.made(1))
                V.tensor_tensor(lg[:, :, :], lg[:, :, :], mx[:, :].unsqueeze(2).to_broadcast(ce4),
                                ALU.subtract).then_inc(s_lm, 1)
                dve.wait_ge(s_ex, count(k, 1, 1))
                V.tensor_reduce(sm[:, :], pe_[:, :, :], AX_X, ALU.add).then_inc(s_dvb, 1)
                dve.wait_ge(s_dvb, B.made(1))
                V.reciprocal(sm[:, :], sm[:, :]).then_inc(s_dvb, 1)
                dve.wait_ge(s_dvb, B.made(1))
                V.tensor_tensor(pr[:, :, :], pe_[:, :, :], sm[:, :].unsqueeze(2).to_broadcast(ce4), ALU.mult).then_inc(s_dvb, 1)
                dve.wait_ge(s_dvb, B.made(1))
                for c in range(NC):
                    pj = pr[:, c, :].unsqueeze(1).to_broadcast([P, NE, NE])
                    pi = pr[:, c, :].unsqueeze(2).to_broadcast([P, NE, NE])
                    V.tensor_tensor(gt[:, c, :, :], pj, pi, ALU.is_gt).then_inc(s_dvb, 1)
                    B.made(1)
                    V.tensor_tensor(eq[:, c, :, :], pj, pi, ALU.is_equal).then_inc(s_dvb, 1)
                    dve.wait_ge(s_dvb, B.made(1))
                    V.tensor_tensor(eq[:, c, :, :], eq[:, c, :, :],
                                           cst[:, C_TIE:C_REG].rearrange("p (i j) -> p i j", i=NE), ALU.mult).then_inc(s_dvb, 1)
                    dve.wait_ge(s_dvb, B.made(1))
                    V.tensor_tensor(gt[:, c, :, :], gt[:, c, :, :], eq[:, c, :, :], ALU.add).then_inc(s_dvb, 1)
                    dve.wait_ge(s_dvb, B.made(1))
                V.tensor_reduce(rank[:, :, :].rearrange("p c e -> p (c e)"),
                                       gt[:, :, :, :].rearrange("p c i j -> p (c i) j"), AX_X, ALU.add).then_inc(s_dvb, 1)
                dve.wait_ge(s_dvb, B.made(1))
                for i in range(2):
                    V.tensor_scalar(oh[:, i, :, :], rank[:, :, :], float(i), None, ALU.is_equal).then_inc(s_dvb, 1)
                    dve.wait_ge(s_dvb, B.made(1))
                V.tensor_tensor(mask[:, :, :], oh[:, 0, :, :], oh[:, 1, :, :], ALU.add).then_inc(s_mask, 1)
                for i in range(2):
                    V.tensor_tensor(tmp[:, i, :, :], oh[:, i, :, :], pr[:, :, :], ALU.mult).then_inc(s_dvb, 1)
                    dve.wait_ge(s_dvb, B.made(1))
                V.tensor_reduce(top[:, :, :].rearrange("p i c -> p (i c)"),
                                       tmp[:, :, :, :].rearrange("p i c e -> p (i c) e"), AX_X, ALU.add).then_inc(s_dvb, 1)
                dve.wait_ge(s_dvb, B.made(1))
                V.tensor_tensor(sm[:, :], top[:, 0, :], top[:, 1, :], ALU.add).then_inc(s_dvb, 1)
                dve.wait_ge(s_dvb, B.made(1))
                V.reciprocal(sm[:, :], sm[:, :]).then_inc(s_dvb, 1)
                dve.wait_ge(s_dvb, B.made(1))
                g0 = k.b * (4 * NC) + k.par * 2 * NC
                V.tensor_tensor(
                    share_all[:, bass.ds(g0, 2 * NC)].rearrange("p (i c) -> p i c", i=2), top[:, :, :],
                    sm[:, :].unsqueeze(1).to_broadcast([P, 2, NC]), ALU.mult).then_inc(s_dvb, 1)
                B.made(1)
                dve.wait_ge(s_rk, count(k, 1, 1))
                tot = PG[:, 64:64 + NC * NE].rearrange("p (c e) -> p c e", c=NC)
                V.tensor_copy(cbase[:, 0, :], base[:, :]).then_inc(s_dvb, 1)
                dve.wait_ge(s_dvb, B.made(1))
                for c in range(1, NC):
                    V.tensor_tensor(cbase[:, c, :], cbase[:, c - 1, :], tot[:, c - 1, :], ALU.add).then_inc(s_dvb, 1)
                    dve.wait_ge(s_dvb, B.made(1))
                V.tensor_tensor(base[:, :], cbase[:, NC - 1, :], tot[:, NC - 1, :], ALU.add).then_inc(s_dvb, 1)
                B.made(1)
                V.tensor_tensor(slot[:, :, :], cbase[:, :, :],
                                       PG[:, 32:32 + NC * NE].rearrange("p (c e) -> p c e", c=NC), ALU.add).then_inc(s_dvb, 1)
                dve.wait_ge(s_dvb, B.made(1))
                for i in range(2):
                    V.tensor_tensor(tmp[:, i, :, :], oh[:, i, :, :], slot[:, :, :], ALU.mult).then_inc(s_dvb, 1)
                    dve.wait_ge(s_dvb, B.made(1))
                V.tensor_reduce(posf[:, :, :].rearrange("p i c -> p (i c)"),
                                       tmp[:, :, :, :].rearrange("p i c e -> p (i c) e"), AX_X, ALU.add).then_inc(s_dvb, 1)
                dve.wait_ge(s_dvb, B.made(1))
                V.tensor_copy(pos_all[:, bass.ds(g0, 2 * NC)],
                                       posf[:, :, :].rearrange("p i c -> p (i c)")).then_inc(s_dvb, 1)
                B.made(1)
                V.tensor_copy(posu[k.par][:, :, :], posf[:, :, :]).then_inc(s_pos, 1)

            loop(dve, front, back)

        @block.tensor
        def _(pe):
            start(pe, s_pf, s_XT, s_G, s_D, s_Y, s_yi, s_ds, s_YT, s_O, s_RT, s_lg, s_rk)
            pe.wait_ge(s_small, 160)
            pe.wait_ge(s_wlo, 1)
            pe.wait_ge(s_wo, MX)
            mm = nc.tensor.matmul
            ident = cst[:, C_ID:C_ID + P]

            def product(dst, lhs, rhs, last_sem=None):
                for kt in range(KT):
                    (lh, ll), (rh, rl) = lhs(kt), rhs(kt)
                    mm(dst, lh, rh, start=(kt == 0), stop=False)
                    mm(dst, lh, rl, start=False, stop=False)
                    last = mm(dst, ll, rh, start=False, stop=(kt == KT - 1))
                return last

            def front(k):
                pe.wait_ge(s_xhi, count(k, 1, 1))
                pe.wait_ge(s_xlo, count(k, 1, 1))

                def free(u):
                    pe.wait_ge(s_pff, count(k, PF_USES, u - 1))
                    return PF[(u + k.par) % 2]

                def xw_(kt, c):
                    return x_hi[:, kt, c * Q:(c + 1) * Q], x_lo[:, kt, c * Q:(c + 1) * Q]

                def ww(kt, lo, n):
                    return w_hi[:, kt, lo:lo + n], w_lo[:, kt, lo:lo + n]

                bank = free(0)
                for c in range(NC):
                    last = product(bank[:, c * NH:(c + 1) * NH], lambda kt: xw_(kt, c), lambda kt: ww(kt, DT0, NH))
                last.then_inc(s_pf, 1)
                for u, m in enumerate((4, 0, 1, 2, 3), 1):
                    bank = free(u)
                    product(bank[:, :], lambda kt: ww(kt, X0 + m * P, P),
                            lambda kt: (x_hi[:, kt, :], x_lo[:, kt, :])).then_inc(s_pf, 1)
                bank = free(6)
                pe.wait_ge(s_dt, count(k, 1, 1))
                al = a[k.par][:, :, :].rearrange("p c h -> p (c h)")
                for i, m in enumerate((C_INCL, C_GTR, C_ONE)):
                    last = mm(bank[:, i * NC * NH:(i + 1) * NC * NH], cst[:, m:m + P], al, start=True, stop=True)
                last.then_inc(s_pf, 1)
                for c in range(NC):
                    bank = free(7 + c)
                    product(bank[:, :], lambda kt: xw_(kt, c), lambda kt: ww(kt, Z0, DI)).then_inc(s_pf, 1)

            def back(k):
                def scores(c):
                    if c == 0:
                        pe.wait_ge(s_sil, count(k, 6, 6))
                    cols = slice(c * Q, (c + 1) * Q)
                    pe.wait_ge(s_yT, count(k, NC, max(c - 1, 0)))
                    if c == 0:
                        pe.wait_ge(s_rT, count(k, 2, 0))
                    for m in range(MX):
                        last = nc.tensor.transpose(PX[:, m * P:(m + 1) * P], xch[k.par][:, m, cols], ident)
                    last.then_inc(s_XT, 1)
                    pe.wait_ge(s_Gm, count(k, NC, c))
                    pe.wait_ge(s_Bt, count(k, NC, c))
                    pe.wait_ge(s_r, count(k, NC, max(c - 1, 0)))
                    if c == 0:
                        pe.wait_ge(s_pos, count(k, 1, 0))
                    mm(PG[:, 0:Q], BT[k.par][:, cols], CT[k.par][:, cols], start=True, stop=True)
                    nc.tensor.transpose(PG[:, Q:Q + NST], BT[k.par][:, cols],
                                        cst[0:NST, C_ID:C_ID + NST]).then_inc(s_G, 1)
                    pe.wait_ge(s_am, count(k, NC, c + 1))
                    pe.wait_ge(s_E, count(k, NC, c))
                    mm(PD0[:, :], cst[:, C_GTR:C_GTR + Q], am[:, 0:4, :].rearrange("p h t -> p (h t)"),
                       start=True, stop=True)
                    mm(PD1[:, :], cst[:, C_GTR:C_GTR + Q], am[:, 4:8, :].rearrange("p h t -> p (h t)"),
                       start=True, stop=True).then_inc(s_D, 1)

                def project(c):
                    pe.wait_ge(s_xt, count(k, NC, min(c + 2, NC)))
                    pe.wait_ge(s_yz, count(k, NC, c + 1))
                    for m in range(MX):
                        last = nc.tensor.transpose(PX[:, m * P:(m + 1) * P], yz[c % 2][:, m * P:(m + 1) * P], ident)
                    last.then_inc(s_YT, 1)
                    pe.wait_ge(s_yT, count(k, NC, c + 1))
                    pe.wait_ge(s_Gm, count(k, NC, min(c + 2, NC)))
                    pe.wait_ge(s_Bt, count(k, NC, min(c + 2, NC)))
                    pe.wait_ge(s_r, count(k, NC, c))
                    for m in range(MX):
                        last = mm(PG[:, DM:2 * DM], yT[:, m, :], wo[:, m, :], start=(m == 0), stop=(m == MX - 1))
                    last.then_inc(s_O, 1)

                def mix(c):
                    cols = slice(c * Q, (c + 1) * Q)
                    pe.wait_ge(s_S, count(k, NC, c))
                    if c == 0 and k.par == 0:
                        pe.wait_ge(s_S0, k.b + (1 + BIAS))
                    mm(PI[:, :], CT[k.par][:, cols], S[:, :], start=True, stop=True).then_inc(s_yi, 1)
                    pe.wait_ge(s_M, count(k, NC, c + 1))
                    pe.wait_ge(s_yz, count(k, NC, c))
                    for h in range(NH):
                        last = mm(PY[:, h * HD:(h + 1) * HD], M[c % 2][:, h, :],
                                  xdt[c % 2][:, h * HD:(h + 1) * HD], start=True, stop=True)
                    last.then_inc(s_Y, 1)
                    pe.wait_ge(s_Bt, count(k, NC, c + 1))
                    pe.wait_ge(s_xw, count(k, NC, c + 1))
                    pe.wait_ge(s_t1, count(k, NC, c + 1))
                    mm(PI[0:NST, :], B_tok[c % 2][:, :], xw[c % 2][:, :], start=True, stop=True).then_inc(s_ds, 1)

                for c in range(NC):
                    scores(c)
                    if c:
                        project(c - 1)
                    mix(c)
                project(NC - 1)
                pe.wait_ge(s_x1, count(k, NC, NC))
                for half in range(2):
                    pe.wait_ge(s_yT, count(k, NC, NC))
                    pe.wait_ge(s_rT, count(k, 2, half))
                    for i in range(2):
                        for kt in range(KT):
                            at = (i * KT + kt) * P
                            last = nc.tensor.transpose(PX[:, at:at + P],
                                                       x1[k.par][:, 2 * half + i, kt * P:(kt + 1) * P], ident)
                    last.then_inc(s_RT, 1)
                pe.wait_ge(s_rT, count(k, 2, 2))
                pe.wait_ge(s_r, count(k, NC, NC))
                for c in range(NC):
                    for kt in range(KT):
                        last = mm(PG[:, c * NE:(c + 1) * NE], x1T[:, c, kt, :], wr_sb[:, kt, :],
                                  start=(kt == 0), stop=(kt == KT - 1))
                last.then_inc(s_lg, 1)
                pe.wait_ge(s_mask, count(k, 1, 1))
                mk = mask[:, :, :].rearrange("p c e -> p (c e)")
                mm(PG[:, 32:32 + NC * NE], cst[:, C_LESS:C_LESS + P], mk, start=True, stop=True)
                mm(PG[:, 64:64 + NC * NE], cst[:, C_ONE:C_ONE + P], mk, start=True, stop=True).then_inc(s_rk, 1)

            loop(pe, front, back)


def route(nc, xs, base, cst, table, pads, zero, pos_all, pos_y):
    with ExitStack() as ctx:
        def sb(name, shape, dt=F32):
            return ctx.enter_context(nc.sbuf_tensor(name, shape, dt))

        cnt = sb("cnt", [P, NE])
        more = sb("more", [P, NE, NTS])
        nt = sb("nt", [P, NE])
        first = sb("first", [P, NE])
        end = sb("end", [P, NE])
        past = sb("past", [P, NE, NTR])
        begun = sb("begun", [P, NE, NTR])
        row = sb("row", [P, NE, NTR])
        off = sb("off", [P, NE])
        by = sb("by", [P, 2 * T // P])
        inreg = sb("inreg", [P, 2 * T // P])
        step = sb("step", [P, 1])
        tf = sb("tf", [P, 2, NTR])
        s_v = ctx.enter_context(nc.semaphore("s_v"))
        s_table = ctx.enter_context(nc.semaphore("s_table"))
        s_pad = ctx.enter_context(nc.semaphore("s_pad"))
        s_zero = ctx.enter_context(nc.semaphore("s_zero"))
        block = ctx.enter_context(nc.Block())

        @block.gpsimd
        def _(pool):
            nc.gpsimd.memset(zero[:, :], 0.0).then_inc(s_zero, 1)

        @block.vector
        def _(dve):
            V = nc.vector
            steps = Steps()
            tiles = [P, NE, NTR]
            tj = cst[:, C_TJ:C_E].rearrange("p (e j) -> p e j", e=NE)
            reg = cst[:, C_REG:C_T16]
            V.tensor_tensor(cnt[:, :], base[:, :], reg, ALU.subtract).then_inc(s_v, 1)
            dve.wait_ge(s_v, steps.made(1))
            V.tensor_copy(pads[0:1, :], base[0:1, :]).then_inc(s_v, 1)
            dve.wait_ge(s_v, steps.made(1))
            V.tensor_tensor(more[:, :, :], cnt[:, :].unsqueeze(2).to_broadcast([P, NE, NTS]),
                                 cst[:, C_T16:C_TJ].rearrange("p (e j) -> p e j", e=NE), ALU.is_gt).then_inc(s_v, 1)
            dve.wait_ge(s_v, steps.made(1))
            V.tensor_reduce(nt[:, :], more[:, :, :], AX_X, ALU.add).then_inc(s_v, 1)
            dve.wait_ge(s_v, steps.made(1))
            V.tensor_copy(end[:, 0:1], nt[:, 0:1]).then_inc(s_v, 1)
            dve.wait_ge(s_v, steps.made(1))
            for e in range(1, NE):
                V.tensor_tensor(end[:, e:e + 1], end[:, e - 1:e], nt[:, e:e + 1], ALU.add).then_inc(s_v, 1)
                dve.wait_ge(s_v, steps.made(1))
            V.tensor_tensor(first[:, :], end[:, :], nt[:, :], ALU.subtract).then_inc(s_v, 1)
            dve.wait_ge(s_v, steps.made(1))
            V.tensor_tensor(past[:, :, :], tj, end[:, :].unsqueeze(2).to_broadcast(tiles), ALU.is_ge).then_inc(s_v, 1)
            dve.wait_ge(s_v, steps.made(1))
            V.tensor_tensor(begun[:, :, :], tj, first[:, :].unsqueeze(2).to_broadcast(tiles), ALU.is_ge).then_inc(s_v, 1)
            dve.wait_ge(s_v, steps.made(1))
            V.tensor_reduce(tf[:, 0, :], past[:, :, :].rearrange("p e j -> p j e"), AX_X, ALU.add).then_inc(s_v, 1)
            dve.wait_ge(s_v, steps.made(1))
            V.tensor_scalar(tf[:, 0, :], tf[:, 0, :], float(NE - 1), 1.0, ALU.min, ALU.add).then_inc(s_v, 1)
            dve.wait_ge(s_v, steps.made(1))
            V.scalar_tensor_tensor(out=off[:, :], in0=first[:, :], scalar=-float(TILE), in1=reg,
                                        op0=ALU.mult, op1=ALU.add).then_inc(s_v, 1)
            dve.wait_ge(s_v, steps.made(1))
            V.scalar_tensor_tensor(out=row[:, :, :], in0=tj, scalar=float(TILE),
                                        in1=off[:, :].unsqueeze(2).to_broadcast(tiles),
                                        op0=ALU.mult, op1=ALU.add).then_inc(s_v, 1)
            dve.wait_ge(s_v, steps.made(1))
            V.tensor_tensor(begun[:, :, :], begun[:, :, :], past[:, :, :], ALU.subtract).then_inc(s_v, 1)
            dve.wait_ge(s_v, steps.made(1))
            V.tensor_tensor(row[:, :, :], row[:, :, :], begun[:, :, :], ALU.mult).then_inc(s_v, 1)
            dve.wait_ge(s_v, steps.made(1))
            V.tensor_reduce(tf[:, 1, :], row[:, :, :].rearrange("p e j -> p j e"), AX_X, ALU.add).then_inc(s_v, 1)
            dve.wait_ge(s_v, steps.made(1))
            V.scalar_tensor_tensor(out=tf[:, 1, :], in0=past[:, NE - 1, :], scalar=float(DUMMY),
                                        in1=tf[:, 1, :], op0=ALU.mult, op1=ALU.add).then_inc(s_v, 1)
            dve.wait_ge(s_v, steps.made(1))
            V.tensor_copy(table[:, :, :], tf[0:1, :, :]).then_inc(s_table, 1)
            V.scalar_tensor_tensor(out=off[:, :], in0=first[:, :], scalar=float(TILE), in1=reg,
                                        op0=ALU.mult, op1=ALU.subtract).then_inc(s_v, 1)
            dve.wait_ge(s_v, steps.made(1))
            V.tensor_scalar(by[:, :], pos_all[:, :], off[:, 0:1], None, ALU.add).then_inc(s_v, 1)
            dve.wait_ge(s_v, steps.made(1))
            for e in range(1, NE):
                V.tensor_tensor(step[:, :], off[:, e:e + 1], off[:, e - 1:e], ALU.subtract).then_inc(s_v, 1)
                dve.wait_ge(s_v, steps.made(1))
                V.tensor_scalar(inreg[:, :], pos_all[:, :], float(R0 + e * CAP), step[:, :], ALU.is_ge, ALU.mult).then_inc(s_v, 1)
                dve.wait_ge(s_v, steps.made(1))
                V.tensor_tensor(by[:, :], by[:, :], inreg[:, :], ALU.add).then_inc(s_v, 1)
                dve.wait_ge(s_v, steps.made(1))
            V.tensor_copy(pos_y[:, :], by[:, :]).then_inc(s_v, 1)
            dve.wait_ge(s_v, steps.made(1))

        @block.sync
        def _(sp):
            sp.wait_ge(s_zero, 1)
            z = zero[:, :].rearrange("p (a d) -> p a d", d=DM)
            sp.dma_start(xs[DUMMY:DUMMY + TILE, :].rearrange("(p a) d -> p a d", p=P), z).then_inc(s_pad, 16)
            sp.wait_ge(s_table, 1)
            for e in range(NE):
                row0 = sp.value_load(pads[0:1, e:e + 1], min_val=R0 + e * CAP, max_val=R0 + e * CAP + T)
                sp.dma_start(xs[bass.ds(row0, TILE), :].rearrange("(p a) d -> p a d", p=P), z).then_inc(s_pad, 16)
            sp.wait_ge(s_pad, 16 * (NE + 1))


ROUTED, SHARED, NONE = "routed", "shared", None
PARTS = [(0, GU), (GU, 2 * GU), (2 * GU, WROW)]


def moe(nc, experts, xs, ys, out, pos_y, share_all, cst, table):
    with ExitStack() as ctx:
        def sb(name, shape, dt=F32):
            return ctx.enter_context(nc.sbuf_tensor(name, shape, dt))

        def bank(name):
            return ctx.enter_context(nc.psum_tensor(name, [P, 512], F32))

        def sem(name):
            return ctx.enter_context(nc.semaphore(name))

        def pair(name, shape, dt=F32):
            return [sb(f"{name}{i}", shape, dt) for i in range(2)]

        w_raw = sb("we_raw", [P, WROW])
        w_hi = pair("we_hi", [P, WROW], F32R)
        w_lo = pair("we_lo", [P, WROW], F32R)
        rows = pair("rows", [P, 2, DM])
        xt_hi = pair("xt_hi", [P, KT, TILE], F32R)
        xt_lo = pair("xt_lo", [P, KT, TILE], F32R)
        gate = pair("gate", [P, TILE])
        h = pair("h", [P, TILE])
        h_hi = pair("h_hi", [P, NCH, TILE], F32R)
        h_lo = pair("h_lo", [P, NCH, TILE], F32R)
        y_sb = pair("y_sb", [P, 2, DM])
        x1r = pair("x1r", [P, 2, DM])
        got = pair("got", [P, 2, 2, DM])
        idx = pair("idx", [P, 4], U32)
        share = pair("share", [P, 4])
        o = pair("o", [P, 2, DM])
        st6 = sb("mst6", [P, 2, 6])
        mv = sb("mmv", [P, 2, 2])
        rstd = sb("mrstd", [P, 2])
        mhalf = sb("mmhalf", [P, 2])

        H = [bank(f"H{i}") for i in range(NCH)]
        PT, PY = bank("PT"), bank("PYo")

        s_part = [sem(f"s_part{i}") for i in range(3)]
        s_rows = [sem("s_rows0"), sem("s_rows1")]
        s_x1r = [sem("s_x1r0"), sem("s_x1r1")]
        s_got = [sem("s_got0"), sem("s_got1")]
        s_ys = [sem("s_ys0"), sem("s_ys1")]
        s_out = [sem("s_out0"), sem("s_out1")]
        (s_wh, s_wl, s_wlp, s_xh, s_xl, s_T, s_gu, s_dn, s_sg, s_h, s_hh, s_hl, s_y, s_yr, s_idx, s_shr,
         s_o, s_mvr, s_rstd, s_mh, s_c, s_pc, s_hold) = [sem("m_" + n) for n in (
             "wh wl wlp xh xl T gu dn sg h hh hl y yr idx shr o mvr rstd mh c pc hold").split()]
        block = ctx.enter_context(nc.Block())

        def steps(eng, step, before=None):
            kind = lambda j: NONE if not 0 <= j < NTR + NTS else ROUTED if j < NTR else SHARED

            def one(j):
                step(Block(j // 2, j % 2), *[kind(j + i) for i in (-1, 0, 1, 2)])

            one(0)
            with eng.Fori(0, NTR // 2 - 2) as b:
                step(Block(b, 1), ROUTED, ROUTED, ROUTED, ROUTED)
                step(Block(b + 1, 0), ROUTED, ROUTED, ROUTED, ROUTED)
            for j in range(NTR - 3, NTR + 1):
                one(j)
            with eng.Fori(NTR // 2, (NTR + NTS) // 2 - 2) as b:
                step(Block(b, 1), SHARED, SHARED, SHARED, SHARED)
                step(Block(b + 1, 0), SHARED, SHARED, SHARED, SHARED)
            for j in range(NTR + NTS - 3, NTR + NTS + 1):
                one(j)

        def sharedno(k):
            return Block(k.b - NTR // 2, k.par)

        def is_(k, j):
            return isinstance(k.b, int) and 2 * k.b + k.par == j

        def rowsof(dram, row):
            return dram[bass.ds(row, TILE), :].rearrange("(a p) d -> p a d", p=P)

        @block.sync
        def _(sp):
            for s in s_out + s_ys:
                sp.sem_inc(s, 16)

            def tile_no(k):
                return k.b * 2 + k.par

            def entry(k, i, top):
                return sp.value_load(table[0:1, i, bass.ds(tile_no(k), 1)], min_val=0, max_val=top)

            def load(k, kind):
                sp.wait_ge(s_T, count(k, 1, -1))
                sp.sem_inc(s_hold, 1)
                if kind == ROUTED:
                    src = rowsof(xs, entry(k, 1, DUMMY))
                else:
                    src = rowsof(xs, tile_no(sharedno(k)) * TILE)
                sp.dma_start(rows[k.par][:, :, :], src).then_inc(s_rows[k.par], 16)
                if kind == ROUTED or is_(k, NTR):
                    expert = entry(k, 0, NE) if kind == ROUTED else 0
                    for i, (c0, c1) in enumerate(PARTS):
                        sp.wait_ge(s_wh, count(k, 3, i - 2))
                        sp.sem_inc(s_hold, 1)
                        if i < 2:
                            sp.wait_ge(s_wl, count(k, 2, i - 1))
                            sp.sem_inc(s_hold, 1)
                        else:
                            sp.wait_ge(s_wlp, count(k, 1, 0))
                            sp.sem_inc(s_hold, 1)
                        sp.dma_start(w_raw[:, c0:c1], experts[bass.ds(expert, 1), :, c0:c1].rearrange("e p n -> (e p) n")
                                     ).then_inc(s_part[i], 16)

            load(Block(0, 0), ROUTED)
            load(Block(0, 1), ROUTED)

            def step(k, prev, this, nxt, nxt2):
                if nxt2:
                    load(k.next().next(), nxt2)
                kp = k.prev() if prev else None
                if this == SHARED:
                    s = sharedno(k)
                    sp.wait_ge(s_o, count(s, 1, -1))
                    sp.sem_inc(s_hold, 1)
                    sp.dma_start(x1r[k.par][:, :, :], rowsof(xs, tile_no(s) * TILE)).then_inc(s_x1r[k.par], 16)
                if prev == ROUTED:
                    sp.wait_ge(s_y, count(kp, 1, 1))
                    sp.sem_inc(s_hold, 1)
                    sp.dma_start(rowsof(ys, tile_no(kp) * TILE), y_sb[kp.par][:, :, :]).then_inc(s_ys[kp.par], 16)
                if prev == SHARED:
                    s = sharedno(kp)
                    sp.wait_ge(s_o, count(s, 1, 1))
                    sp.sem_inc(s_hold, 1)
                    sp.dma_start(rowsof(out, tile_no(s) * TILE), o[kp.par][:, :, :]).then_inc(s_out[kp.par], 16)

            steps(sp, step)
            for i in range(2):
                sp.wait_ge(s_out[i], 16 * (NTS // 2) + 16)

        @block.gpsimd
        def _(pool):
            for s in (s_wlp, s_idx, s_shr, s_rstd, s_pc):
                pool.sem_inc(s, BIAS)
            nc.gpsimd.memset(mhalf[:, :], -0.5).then_inc(s_mh, 1)
            pool.wait_ge(s_mh, 1)

            def split(k):
                c0, c1 = PARTS[2]
                pool.wait_ge(s_part[2], k.count(16, 16))
                pool.wait_ge(s_wh, count(k, 3, 3))
                pool.wait_ge(s_dn, count(k, 1, -1))
                nc.gpsimd.tensor_tensor(w_lo[k.par][:, c0:c1], w_raw[:, c0:c1], w_hi[k.par][:, c0:c1].bitcast(F32),
                                        ALU.subtract).then_inc(s_wlp, 1)

            split(Block(0, 0))

            def step(k, prev, this, nxt, nxt2):
                if nxt == ROUTED or is_(k, NTR - 1):
                    split(k.next())
                if this == SHARED:
                    s = sharedno(k)
                    if is_(k, NTR):
                        for i in range(2):
                            pool.wait_ge(s_ys[i], 16 * (NTR // 2) + 16)
                    pool.wait_ge(s_o, count(s, 1, -1))
                    pool.sem_inc(s_hold, 1)
                    col = s.b * (4 * 2) + 2 * s.par
                    for i in range(2):
                        nc.gpsimd.tensor_copy(idx[k.par][:, 2 * i:2 * i + 2],
                                              pos_y[:, bass.ds(col + 4 * i, 2)]).then_inc(s_idx, 1)
                        nc.gpsimd.tensor_copy(share[k.par][:, 2 * i:2 * i + 2],
                                              share_all[:, bass.ds(col + 4 * i, 2)]).then_inc(s_shr, 1)
                    pool.wait_ge(s_idx, count(s, 2, 2))
                    pool.sem_inc(s_hold, 1)
                    for i in range(2):
                        for half in range(2):
                            pool.indirect_dma_start(
                                out=got[k.par][:, i, half, :], out_offset=None, in_=ys,
                                in_offset=bass.IndirectOffsetOnAxis(ap=idx[k.par][:, 2 * i + half:2 * i + half + 1],
                                                                    axis=0)).then_inc(s_got[k.par], 16)
                if prev == SHARED:
                    s = sharedno(k.prev())
                    pool.wait_ge(s_mvr, count(s, 1, 1))
                    pool.sem_inc(s_hold, 1)
                    nc.gpsimd.tensor_scalar(rstd[:, :], mv[:, :, 1], EPS, None, ALU.add).then_inc(s_pc, 1)
                    pool.wait_ge(s_pc, count(s, 1, 1))
                    nc.gpsimd.tensor_tensor(rstd[:, :], rstd[:, :], mhalf[:, :], ALU.pow).then_inc(s_rstd, 1)

            steps(pool, step)

        @block.scalar
        def _(act):
            for s in (s_wh, s_xh, s_sg, s_hh, s_y):
                act.sem_inc(s, BIAS)

            def split(k, i):
                c0, c1 = PARTS[i]
                act.wait_ge(s_part[i], k.count(16, 16))
                if i < 2:
                    act.wait_ge(s_gu, count(k, NCH, -NCH))
                else:
                    act.wait_ge(s_dn, count(k, 1, -1))
                nc.scalar.activation(w_hi[k.par][:, c0:c1], w_raw[:, c0:c1], ACT.Copy).then_inc(s_wh, 1)

            def split_x(k):
                act.wait_ge(s_T, count(k, 1, 1))
                act.wait_ge(s_gu, count(k, NCH, -NCH))
                nc.scalar.activation(xt_hi[k.par][:, :, :].rearrange("p a t -> p (a t)"), PT[:, :],
                                     ACT.Copy).then_inc(s_xh, 1)

            for i in range(3):
                split(Block(0, 0), i)
            split_x(Block(0, 0))

            def step(k, prev, this, nxt, nxt2):
                def silu(c):
                    act.wait_ge(s_gu, count(k, NCH, c + 1))
                    act.wait_ge(s_h, count(k, NCH, c - 1))
                    if c < NCH - 1:
                        nc.scalar.activation(gate[c % 2][:, :], H[c][:, 0:TILE], ACT.Silu).then_inc(s_sg, 1)
                    else:
                        nc.scalar.activation(gate[c % 2][64:P, :], H[c][0:64, 0:TILE], ACT.Silu).then_inc(s_sg, 1)

                def high(c):
                    lo = 0 if c < NCH - 1 else 64
                    act.wait_ge(s_h, count(k, NCH, c + 1))
                    act.wait_ge(s_dn, count(k, 1, -1))
                    nc.scalar.activation(h_hi[k.par][lo:P, c, :], h[c % 2][lo:P, :], ACT.Copy).then_inc(s_hh, 1)

                if this:
                    silu(0)
                    silu(1)
                    high(0)
                    high(1)
                if nxt == ROUTED or is_(k, NTR - 1):
                    for i in range(3):
                        split(k.next(), i)
                if prev == ROUTED:
                    kp = k.prev()
                    act.wait_ge(s_dn, count(kp, 1, 1))
                    act.wait_ge(s_ys[kp.par], sent(kp, 1))
                    nc.scalar.activation(y_sb[kp.par][:, :, :].rearrange("p a d -> p (a d)"), PY[:, :],
                                         ACT.Copy).then_inc(s_y, 1)
                if this:
                    silu(2)
                    silu(3)
                    high(2)
                if nxt:
                    split_x(k.next())
                if this:
                    silu(4)
                    high(3)
                    silu(5)
                    high(4)
                    high(5)

            steps(act, step)

        @block.vector
        def _(dve):
            V = nc.vector
            for s in (s_wl, s_xl, s_h, s_hl, s_yr, s_o, s_mvr, s_c):
                dve.sem_inc(s, BIAS)
            C = Steps(9)

            def split(k, i):
                c0, c1 = PARTS[i]
                dve.wait_ge(s_part[i], k.count(16, 16))
                dve.wait_ge(s_wh, count(k, 3, i + 1))
                V.tensor_tensor(w_lo[k.par][:, c0:c1], w_raw[:, c0:c1], w_hi[k.par][:, c0:c1].bitcast(F32),
                                ALU.subtract).then_inc(s_wl, 1)

            def split_x(k):
                dve.wait_ge(s_xh, count(k, 1, 1))
                V.tensor_tensor(xt_lo[k.par][:, :, :].rearrange("p a t -> p (a t)"), PT[:, :],
                                xt_hi[k.par][:, :, :].rearrange("p a t -> p (a t)").bitcast(F32),
                                ALU.subtract).then_inc(s_xl, 1)

            for i in range(2):
                split(Block(0, 0), i)
            split_x(Block(0, 0))

            def combine(k):
                s = sharedno(k)
                C.begin(s)
                dve.wait_ge(s_dn, count(k, 1, 1))
                dve.wait_ge(s_x1r[k.par], landed(s, 1))
                dve.wait_ge(s_out[k.par], sent(s, 1))
                V.tensor_tensor(o[k.par][:, :, :].rearrange("p a d -> p (a d)"), PY[:, :],
                                x1r[k.par][:, :, :].rearrange("p a d -> p (a d)"), ALU.add).then_inc(s_yr, 1)
                dve.wait_ge(s_yr, count(s, 1, 1))
                dve.wait_ge(s_got[k.par], landed(s, 4))
                dve.wait_ge(s_shr, count(s, 2, 2))
                for i in range(2):
                    for half in range(2):
                        ins = V.scalar_tensor_tensor(
                            out=o[k.par][:, half, :], in0=got[k.par][:, i, half, :],
                            scalar=share[k.par][:, 2 * i + half:2 * i + half + 1],
                            in1=o[k.par][:, half, :], op0=ALU.mult, op1=ALU.add)
                        ins.then_inc(s_c, 1)
                        C.made(1)
                    dve.wait_ge(s_c, C.made(0))
                for half in range(2):
                    V.bn_stats(st6[:, half, :], o[k.par][:, half, :]).then_inc(s_c, 1)
                    C.made(1)
                dve.wait_ge(s_c, C.made(0))
                dve.sem_inc(s_hold, 1)
                V.bn_aggr(mv[:, 0, :], st6[:, 0, :]).then_inc(s_c, 1)
                C.made(1)
                V.bn_aggr(mv[:, 1, :], st6[:, 1, :]).then_inc(s_mvr, 1)
                dve.wait_ge(s_mvr, count(s, 1, 1))
                dve.wait_ge(s_c, C.made(0))
                dve.wait_ge(s_rstd, count(s, 1, 1))
                V.tensor_scalar(o[k.par][:, 0, :], o[k.par][:, 0, :], mv[:, 0, 0:1], rstd[:, 0:1],
                                         ALU.subtract, ALU.mult).then_inc(s_c, 1)
                C.made(1)
                V.tensor_scalar(o[k.par][:, 1, :], o[k.par][:, 1, :], mv[:, 1, 0:1], rstd[:, 1:2],
                                ALU.subtract, ALU.mult).then_inc(s_o, 1)
                V.memset(st6[0:1, 0, 0:1], 0.0).then_inc(s_c, 1)
                C.made(1)
                C.end()

            def step(k, prev, this, nxt, nxt2):
                def product(c):
                    lo = 0 if c < NCH - 1 else 64
                    up = H[c][lo:P, 0:TILE] if lo else H[c][:, TILE:2 * TILE]
                    dve.wait_ge(s_sg, count(k, NCH, c + 1))
                    dve.wait_ge(s_hh, count(k, NCH, c - 1))
                    dve.wait_ge(s_hl, count(k, NCH, c - 1))
                    V.tensor_tensor(h[c % 2][lo:P, :], gate[c % 2][lo:P, :], up, ALU.mult).then_inc(s_h, 1)

                def low(c):
                    lo = 0 if c < NCH - 1 else 64
                    dve.wait_ge(s_hh, count(k, NCH, c + 1))
                    V.tensor_tensor(h_lo[k.par][lo:P, c, :], h[c % 2][lo:P, :],
                                    h_hi[k.par][lo:P, c, :].bitcast(F32), ALU.subtract).then_inc(s_hl, 1)

                if this:
                    product(0)
                    product(1)
                    low(0)
                    low(1)
                if nxt == ROUTED or is_(k, NTR - 1):
                    for i in range(2):
                        split(k.next(), i)
                if this:
                    product(2)
                    product(3)
                    low(2)
                if nxt:
                    split_x(k.next())
                if this:
                    product(4)
                    low(3)
                    product(5)
                    low(4)
                    low(5)
                if prev == SHARED:
                    combine(k.prev())

            steps(dve, step)

        @block.tensor
        def _(pe):
            mm = nc.tensor.matmul
            for s in (s_T, s_gu, s_dn):
                pe.sem_inc(s, BIAS)

            def turn(k):
                pe.wait_ge(s_rows[k.par], landed(k, 1))
                pe.wait_ge(s_xl, count(k, 1, 0))
                for kt in range(KT):
                    for half in range(2):
                        at = kt * TILE + half * P
                        last = nc.tensor.transpose(PT[:, at:at + P], rows[k.par][:, half, kt * P:(kt + 1) * P],
                                                   cst[:, C_ID:C_ID + P])
                last.then_inc(s_T, 1)

            turn(Block(0, 0))

            def down(k, kind):
                wp = k.par if kind == ROUTED else 0
                pe.wait_ge(s_hl, count(k, NCH, NCH))
                if kind == ROUTED:
                    pe.wait_ge(s_wlp, count(k, 1, 1))
                    pe.wait_ge(s_y, count(k, 1, 0))
                else:
                    pe.wait_ge(s_wlp, count(Block(NTR // 2, 0), 1, 1))
                    pe.wait_ge(s_y, count(Block(NTR // 2, 0), 1, 0))
                    pe.wait_ge(s_yr, count(sharedno(k), 1, 0))
                for half in range(2):
                    dst = PY[:, half * DM:(half + 1) * DM]
                    for c in range(NCH):
                        lo = 0 if c < NCH - 1 else 64
                        hs = slice(half * P, (half + 1) * P)
                        ws = slice(2 * GU + c * DM, 2 * GU + (c + 1) * DM)
                        hh, hl = h_hi[k.par][lo:P, c, hs], h_lo[k.par][lo:P, c, hs]
                        mm(dst, hh, w_hi[wp][lo:P, ws], start=(c == 0), stop=False)
                        mm(dst, hh, w_lo[wp][lo:P, ws], start=False, stop=False)
                        last = mm(dst, hl, w_hi[wp][lo:P, ws], start=False, stop=(c == NCH - 1))
                last.then_inc(s_dn, 1)

            def step(k, prev, this, nxt, nxt2):
                wp = k.par if this == ROUTED else 0

                def gate_up(c):
                    pe.wait_ge(s_h, count(k, NCH, c - NCH + 1))
                    for j in range(2 if c < NCH - 1 else 1):
                        dst = H[c][:, j * TILE:(j + 1) * TILE]
                        for kt in range(KT):
                            ws = slice(kt * GU + (2 * c + j) * P, kt * GU + (2 * c + j + 1) * P)
                            xh, xl = xt_hi[k.par][:, kt, :], xt_lo[k.par][:, kt, :]
                            mm(dst, w_hi[wp][:, ws], xh, start=(kt == 0), stop=False)
                            mm(dst, w_lo[wp][:, ws], xh, start=False, stop=False)
                            last = mm(dst, w_hi[wp][:, ws], xl, start=False, stop=(kt == KT - 1))
                    last.then_inc(s_gu, 1)

                if this:
                    pe.wait_ge(s_xl, count(k, 1, 1))
                    if this == ROUTED or is_(k, NTR):
                        pe.wait_ge(s_wl, count(k, 2, 2))
                for c in range(NCH):
                    if this:
                        gate_up(c)
                    if c == 1 and prev:
                        down(k.prev(), prev)
                    if c == 2 and nxt:
                        turn(k.next())

            steps(pe, step)


_OUT = ((BATCH, SEQ, DM), "float32")


def kernel(**inputs):
    import concourse.bacc as bacc
    from concourse.bass_utils import run_bass_kernel_spmd

    a = {n: np.asarray(v) for n, v in inputs.items()}

    def on_partitions(v):
        return np.ascontiguousarray(np.broadcast_to(v.reshape(1, -1), (P, v.size)))

    def in_tiles(v):
        return np.ascontiguousarray(np.moveaxis(v.reshape(-1, P, *v.shape[1:]), 0, 1))

    def expert_rows(g, u, d):
        n = g.shape[0]
        gt, ut = (np.swapaxes(w, 1, 2).reshape(n, KT, P, FF) for w in (g, u))
        full = (NCH - 1) * P
        pairs = np.stack([w[..., :full].reshape(n, KT, P, NCH - 1, P) for w in (gt, ut)], axis=4)
        gu = np.concatenate([pairs.reshape(n, KT, P, -1), gt[..., full:], ut[..., full:]], axis=3)
        dt = np.swapaxes(d, 1, 2)
        dn = np.zeros((n, NCH, P, DM), np.float32)
        dn[:, :NCH - 1] = dt[:, :full].reshape(n, NCH - 1, P, DM)
        dn[:, NCH - 1, P // 2:] = dt[:, full:]
        return np.ascontiguousarray(np.concatenate(
            [np.swapaxes(gu, 1, 2).reshape(n, P, -1), np.swapaxes(dn, 1, 2).reshape(n, P, -1)], axis=2))

    x = np.ascontiguousarray(a["L0_attn_x"].reshape(T, DM))
    experts = expert_rows(*(np.concatenate([a["L0_ffn_s" + w][None], a["L0_ffn_r" + w]]) for w in "gud"))
    arrays = {
        "x": x,
        "xT": in_tiles(np.ascontiguousarray(x.T)),
        "W_in": np.ascontiguousarray(a["L0_attn_W_in"]),
        "conv_w": np.ascontiguousarray(a["L0_attn_conv_w"]),
        "conv_b": in_tiles(a["L0_attn_conv_b"]),
        "dt_bias": on_partitions(a["L0_attn_dt_bias"]),
        "A_log": on_partitions(a["L0_attn_A_log"]),
        "Dh": on_partitions(a["L0_attn_D"]),
        "norm_w": in_tiles(a["L0_attn_norm_w"]),
        "W_out": np.ascontiguousarray(a["L0_attn_W_out"]),
        "experts": experts,
        "wr": in_tiles(np.ascontiguousarray(a["L0_ffn_wr"].T)),
        "rb": on_partitions(a["L0_ffn_rb"]),
        "consts": constants(),
    }
    nc = bacc.Bacc("TRN2", target_bir_lowering=False, num_devices=1)
    args = {n: nc.dram_tensor(n, v.shape, F32, kind="ExternalInput").ap() for n, v in arrays.items()}
    args["xs"] = nc.dram_tensor("xs", (NROWS, DM), F32).ap()
    args["ys"] = nc.dram_tensor("ys", (NTR * TILE, DM), F32).ap()
    args["out"] = nc.dram_tensor("out", (T, DM), F32, kind="ExternalOutput").ap()
    program(nc, **args)
    got = run_bass_kernel_spmd(nc, [arrays], core_ids=[0]).results[0]["out"]
    return got.reshape(_OUT[0])
```

```python
from contextlib import ExitStack

import numpy as np

import concourse.bass as bass
from concourse import mybir

F32 = mybir.dt.float32
F32R = mybir.dt.float32r
U32 = mybir.dt.uint32
I32 = mybir.dt.int32
ALU = mybir.AluOpType
ACT = mybir.ActivationFunctionType
AX_X = mybir.AxisListType.X

P = 128
BATCH, SEQ, DM = 4, 1024, 256
T = BATCH * SEQ
KT = DM // P
DI = 512
NST = 64
NH = 8
HD = DI // NH
NCONV = 4
NPROJ = 2 * DI + 2 * NST + NH
Z0, X0, BC0, DT0 = 0, DI, 2 * DI, 2 * DI + 2 * NST
Q = 128
NC = 4
BLK = NC * Q
NBLK = T // BLK
MX = DI // P
EPS = 1e-5

NE = 7
FF = 704
NCH = 6
TILE = 256
BIAS = 2
CAP = T + TILE
R0 = T
DUMMY = R0 + NE * CAP
NROWS = DUMMY + TILE
NTR = (2 * T + NE * (TILE - 1)) // TILE
NTR += NTR % 2
NTS = T // TILE
GU = 11 * P
DN = NCH * DM
WROW = KT * GU + DN


class Block:

    def __init__(self, b, par):
        self.b, self.par = b, par

    def next(self):
        return Block(self.b, 1) if self.par == 0 else Block(self.b + 1, 0)

    def prev(self):
        return Block(self.b, 0) if self.par else Block(self.b - 1, 1)

    def count(self, per, n):
        return self.b * (2 * per) + (self.par * per + n)


def count(k, per, n):
    v = k.count(per, n + BIAS)
    return max(v, BIAS) if isinstance(v, int) else v


def landed(k, loads):
    return (k.b + 1) * (16 * loads)


def sent(k, dmas):
    return k.b * (16 * dmas) + 16


class Steps:

    def __init__(self, per=0):
        self.per, self.n, self.k = per, 0, None

    def begin(self, k):
        self.k, self.n = k, 0

    def made(self, n):
        self.n += n
        return self.n if self.k is None else count(self.k, self.per, self.n)

    def end(self):
        assert self.n == self.per, (self.n, self.per)


def program(nc, x, xT, W_in, conv_w, conv_b, dt_bias, A_log, Dh, norm_w, W_out, experts, wr, rb, consts,
            xs, ys, out):
    with ExitStack() as ctx:
        keep = ctx.enter_context
        pos_all = keep(nc.sbuf_tensor("pos_all", [P, 2 * T // P], F32))
        pos_y = keep(nc.sbuf_tensor("pos_y", [P, 2 * T // P], U32))
        share_all = keep(nc.sbuf_tensor("share_all", [P, 2 * T // P], F32))
        base = keep(nc.sbuf_tensor("base", [P, NE], F32))
        cst = keep(nc.sbuf_tensor("cst", [P, NCONST], F32))
        table = keep(nc.sbuf_tensor("table", [1, 2, NTR], I32))
        pads = keep(nc.sbuf_tensor("pads", [1, NE], I32))
        zero = keep(nc.sbuf_tensor("zero", [P, 2 * DM], F32))
        mixer(nc, x, xT, W_in, conv_w, conv_b, dt_bias, A_log, Dh, norm_w, W_out, wr, rb, consts, xs,
              pos_all, share_all, base, cst)
        route(nc, xs, base, cst, table, pads, zero, pos_all, pos_y)
        moe(nc, experts, xs, ys, out, pos_y, share_all, cst, table)


C_ID = 0
C_INCL = C_ID + P
C_GTR = C_INCL + P
C_LESS = C_GTR + P
C_ONE = C_LESS + P
C_TIE = C_ONE + P
C_REG = C_TIE + NE * NE
C_T16 = C_REG + NE
C_TJ = C_T16 + NE * NTS
C_E = C_TJ + NE * NTR
NCONST = C_E + NE * NTR


def constants():
    c = np.zeros((P, NCONST), np.float32)
    k, t = np.arange(P)[:, None], np.arange(P)[None, :]
    for at, m in ((C_ID, k == t), (C_INCL, k <= t), (C_GTR, k > t), (C_LESS, k < t), (C_ONE, k >= 0)):
        c[:, at:at + P] = m
    i, j = np.arange(NE)[:, None], np.arange(NE)[None, :]
    c[:, C_TIE:C_REG] = (j < i).reshape(-1)
    c[:, C_REG:C_T16] = R0 + CAP * np.arange(NE)
    c[:, C_T16:C_TJ] = np.tile(TILE * np.arange(NTS), NE)
    c[:, C_TJ:C_E] = np.tile(np.arange(NTR), NE)
    c[:, C_E:] = np.repeat(np.arange(NE), NTR)
    return c


PF_USES, SOFT, ROUTE, TAPS = 11, 16, 27, 15
SERIES = [1.0 / (2 * i + 1) for i in range(9)]
CHANNELS = (4, 0, 1, 2, 3)


def following(k, c):
    return (k, c + 1) if c < NC - 1 else (k.next(), 0)


def before(k, c):
    return (k, c - 1) if c else (k.prev(), NC - 1)


def taps(u, n):
    if u == 2:
        return 2 * (NCONV - 1) + n
    first, second = (0, 1) if u < 2 else (3 * (NCONV - 1), 4)
    return first + 2 * n - (1 if n and u != second else 0)


def mixer(nc, x, xT, W_in, conv_w, conv_b, dt_bias, A_log, Dh, norm_w, W_out, wr, rb, consts, xs,
          pos_all, share_all, base, cst):
    with ExitStack() as ctx:
        def sb(name, shape, dt=F32):
            return ctx.enter_context(nc.sbuf_tensor(name, shape, dt))

        def bank(name):
            return ctx.enter_context(nc.psum_tensor(name, [P, 512], F32))

        def sem(name):
            return ctx.enter_context(nc.semaphore(name))

        def pair(name, shape, dt=F32):
            return [sb(f"{name}{i}", shape, dt) for i in range(2)]

        w_raw = sb("w_raw", [P, KT, NPROJ])
        w_hi = sb("w_hi", [P, KT, NPROJ], F32R)
        w_lo = sb("w_lo", [P, KT, NPROJ], F32R)
        cw = sb("cw", [P, 5, NCONV])
        cb = sb("cb", [P, 5])
        dtb = sb("dtb", [P, NH])
        alog = sb("alog", [P, NH])
        eA = sb("eA", [P, NH])
        Dp = sb("Dp", [P, NH])
        Dd = sb("Dd", [P, MX, P])
        nw = sb("nw", [P, MX])
        wo = sb("wo", [P, MX, DM])
        wr_sb = sb("wr_sb", [P, KT, NE])
        rb_sb = sb("rb_sb", [P, NE])
        x_raw = sb("x_raw", [P, KT, BLK])
        x_hi = sb("x_hi", [P, KT, BLK], F32R)
        x_lo = sb("x_lo", [P, KT, BLK], F32R)
        cin = pair("cin", [P, 5, BLK + NCONV - 1])
        conv = sb("conv", [P, 5, BLK])
        xch = pair("xch", [P, MX, BLK])
        BT = pair("BT", [NST, BLK])
        CT = pair("CT", [NST, BLK])
        zs = pair("zs", [P, NC, DI])
        xres = pair("xres", [P, NC, DM])
        dt_raw = sb("dt_raw", [P, NC * NH])
        dt_n = sb("dt_n", [P, NC * NH])
        dt_u = sb("dt_u", [P, NC * NH])
        dt_s = sb("dt_s", [P, NC * NH])
        dt_q = sb("dt_q", [P, NC * NH])
        dt_h = sb("dt_h", [P, NC * NH])
        dt_m = sb("dt_m", [P, NC * NH])
        dts = pair("dts", [P, NC, NH])
        a = pair("a", [P, NC, NH])
        ce = pair("ce", [P, 3, NC, NH])
        dw = pair("dw", [P, NC, NH])
        x_tok = pair("x_tok", [P, DI])
        B_tok = pair("B_tok", [P, NST])
        am = sb("am", [P, NH, Q])
        E = pair("E", [P, NH, Q])
        Gm = sb("Gm", [P, Q])
        M = pair("M", [P, NH, Q])
        xdt = pair("xdt", [P, DI])
        xw = pair("xw", [P, DI])
        t1 = sb("t1", [P, DI])
        yz = pair("yz", [P, DI])
        junk = sb("junk", [P, DI])
        ss = pair("ss", [P, 1])
        rs = pair("rs", [P, 1])
        yT = sb("yT", [P, MX, Q])
        S = sb("S", [NST, DI])
        S2 = sb("S2", [NST, DI])
        r = sb("r", [P, DM])
        st6 = sb("st6", [P, 6])
        mv = sb("mv", [P, 2])
        rln = sb("rln", [P, 1])
        mhalf = sb("mhalf", [P, 1])
        x1 = pair("x1", [P, NC, DM])
        x1T = sb("x1T", [P, NC, KT, Q])
        lg = sb("lg", [P, NC, NE])
        mx = sb("mx", [P, NC])
        ex = sb("ex", [P, NC, NE])
        pr = sb("pr", [P, NC, NE])
        sm = sb("sm", [P, NC])
        gt = sb("gt", [P, NC, NE, NE])
        eq = sb("eq", [P, NC, NE, NE])
        rank = sb("rank", [P, NC, NE])
        oh = sb("oh", [P, 2, NC, NE])
        mask = sb("mask", [P, NC, NE])
        rk = sb("rk", [P, 2, NC, NE])
        cbase = sb("cbase", [P, NC, NE])
        slot = sb("slot", [P, NC, NE])
        tmp = sb("tmp", [P, 2, NC, NE])
        posf = sb("posf", [P, 2, NC])
        top = sb("top", [P, 2, NC])
        posu = [sb(f"posu{i}", [P, 2, NC], U32) for i in range(2)]

        PF = [bank("PF0"), bank("PF1")]
        PX, PG, PD0, PD1, PY, PI = [bank(n) for n in ("PX", "PG", "PD0", "PD1", "PY", "PI")]

        s_w, s_wo_in = sem("s_w"), sem("s_wo_in")
        s_small = sem("s_small")
        s_xT = sem("s_xT")
        s_xres = [sem("s_xres0"), sem("s_xres1")]
        s_whi, s_wlo, s_eA, s_wo, s_Dd, s_base, s_mh = [sem(n) for n in
                                                       ("s_whi", "s_wlo", "s_eA", "s_wo", "s_Dd", "s_base", "s_mh")]
        s_xhi, s_xlo, s_halo, s_dtn, s_dtu, s_dt, s_soft, s_dw = [sem(n) for n in (
            "s_xhi", "s_xlo", "s_halo", "s_dtn", "s_dtu", "s_dt", "s_soft", "s_dw")]
        s_pf, s_pff = sem("s_pf"), sem("s_pff")
        s_tap, s_sil, s_zs = sem("s_tap"), sem("s_sil"), sem("s_zs")
        s_S0 = sem("s_S0")
        s_hold = sem("s_hold")
        (s_XT, s_xt, s_Bt, s_G, s_D, s_am, s_E, s_Gm, s_xd, s_xw, s_M, s_Y, s_yi, s_t1, s_ya, s_S2, s_ds, s_S,
         s_yz, s_ss, s_ms, s_rs, s_YT, s_yT, s_O, s_r, s_bs, s_mv, s_ve, s_r1, s_x1) = [sem("s_" + n) for n in (
             "XT xt Bt G D am E Gm xd xw M Y yi t1 ya S2 ds S yz ss ms rs YT yT O r bs mv ve r1 x1").split()]
        s_RT, s_rT, s_lg, s_lr, s_lm, s_ex, s_mask, s_rk, s_rr, s_pos, s_dvr = [sem(n) for n in (
            "s_RT s_rT s_lg s_lr s_lm s_ex s_mask s_rk s_rr s_pos s_dvr").split()]
        s_sc, s_scd = sem("s_sc"), sem("s_scd")
        s_xo = [sem("s_xo0"), sem("s_xo1")]

        block = ctx.enter_context(nc.Block())

        def loop(eng, body):
            body(Block(0, 0), True, False)
            with eng.Fori(0, NBLK // 2 - 1) as b:
                body(Block(b, 1), False, False)
                body(Block(b + 1, 0), False, False)
            body(Block(NBLK // 2 - 1, 1), False, True)

        def start(eng, *sems):
            for s in sems:
                eng.sem_inc(s, BIAS)

        FIRST, LAST, END = Block(0, 0), Block(NBLK // 2 - 1, 1), Block(NBLK // 2, 0)
        x_v = x.rearrange("(g p) d -> p g d", p=P)
        xs_v = xs[0:T, :].rearrange("(g p) d -> p g d", p=P)

        @block.sync
        def _(sp):
            for s in s_xo:
                sp.sem_inc(s, 16)
            sp.dma_start(w_raw[:, :, :], W_in.rearrange("(a p) n -> p a n", p=P)).then_inc(s_w, 16)

            def load_x(f):
                sp.wait_ge(s_xhi, count(f, 1, 0))
                sp.sem_inc(s_hold, 1)
                sp.wait_ge(s_xlo, count(f, 1, 0))
                sp.sem_inc(s_hold, 1)
                t0 = f.b * (2 * BLK) + f.par * BLK
                sp.dma_start(x_raw[:, :, :], xT[:, :, bass.ds(t0, BLK)]).then_inc(s_xT, 16)

            def load_residual(f):
                sp.wait_ge(s_r, count(f, NC, -NC))
                sp.sem_inc(s_hold, 1)
                g0 = f.b * (2 * NC) + f.par * NC
                sp.dma_start(xres[f.par][:, :, :], x_v[:, bass.ds(g0, NC), :]).then_inc(s_xres[f.par], 16)

            def store(k):
                sp.wait_ge(s_x1, count(k, NC, NC))
                sp.sem_inc(s_hold, 1)
                g0 = k.b * (2 * NC) + k.par * NC
                sp.dma_start(xs_v[:, bass.ds(g0, NC), :], x1[k.par][:, :, :]).then_inc(s_xo[k.par], 16)

            load_x(FIRST)
            for dst, src in ((cst[:, :], consts), (cw[:, :, :], conv_w.rearrange("(m p) k -> p m k", p=P)),
                             (cb[:, :], conv_b), (dtb[:, :], dt_bias), (alog[:, :], A_log), (Dp[:, :], Dh),
                             (nw[:, :], norm_w), (wr_sb[:, :, :], wr), (rb_sb[:, :], rb)):
                sp.dma_start(dst, src).then_inc(s_small, 16)
            sp.dma_start(wo[:, :, :], W_out.rearrange("(m p) n -> p m n", p=P)).then_inc(s_wo_in, 16)
            load_residual(FIRST)

            def body(k, first, last):
                if not last:
                    load_x(k.next())
                    load_residual(k.next())
                if not first:
                    store(k.prev())

            loop(sp, body)
            store(LAST)
            for i in range(2):
                sp.wait_ge(s_xo[i], 16 * (NBLK // 2) + 16)

        @block.gpsimd
        def _(pool):
            start(pool, s_scd, s_am, s_xw, s_S2, s_dw, s_ms, s_rs, s_ve, s_r1)
            nc.gpsimd.memset(mhalf[:, :], -0.5).then_inc(s_mh, 1)
            pool.wait_ge(s_small, 144)
            pool.wait_ge(s_mh, 1)

            def decays(q, c):
                pool.wait_ge(s_dt, count(q, 1, 1))
                pool.wait_ge(s_D, count(q, NC, c))
                nc.gpsimd.tensor_tensor(
                    am[:, :, :], a[q.par][:, c, :].unsqueeze(2).to_broadcast([P, NH, Q]),
                    cst[:, C_INCL:C_INCL + Q].unsqueeze(1).to_broadcast([P, NH, Q]),
                    ALU.mult).then_inc(s_am, 1)

            def weighted(q, c):
                if c == 0:
                    pool.wait_ge(s_dt, count(q, 1, 1))
                    pool.wait_ge(s_pff, count(q, PF_USES, 7))
                    pool.wait_ge(s_xw, count(q, NC, -NC))
                    nc.gpsimd.tensor_tensor(dw[q.par][:, :, :], dts[q.par][:, :, :], ce[q.par][:, 1, :, :],
                                            ALU.mult).then_inc(s_dw, 1)
                    pool.wait_ge(s_dw, count(q, 1, 1))
                pool.wait_ge(s_xt, count(q, NC, c + 1))
                pool.wait_ge(s_ds, count(q, NC, c - 1))
                nc.gpsimd.tensor_tensor(
                    xw[c % 2][:, :].rearrange("p (h d) -> p h d", h=NH),
                    x_tok[c % 2][:, :].rearrange("p (h d) -> p h d", h=NH),
                    dw[q.par][:, c, :].unsqueeze(2).to_broadcast([P, NH, HD]), ALU.mult).then_inc(s_xw, 1)

            def state(k, c):
                pool.wait_ge(s_pff, count(k, PF_USES, 7))
                pool.wait_ge(s_S, count(k, NC, c))
                if c == 0 and k.par == 0:
                    pool.wait_ge(s_S0, k.b + (1 + BIAS))
                nc.gpsimd.tensor_tensor(
                    S2[:, :].rearrange("p (h d) -> p h d", h=NH), S[:, :].rearrange("p (h d) -> p h d", h=NH),
                    ce[k.par][0:NST, 2, c, :].unsqueeze(2).to_broadcast([NST, NH, HD]), ALU.mult).then_inc(s_S2, 1)

            def rms(k, c):
                pool.wait_ge(s_ss, count(k, NC, c + 1))
                pool.wait_ge(s_r, count(k, NC, c - 1))
                pool.sem_inc(s_hold, 1)
                nc.gpsimd.tensor_scalar(rs[c % 2][:, :], ss[c % 2][:, :], 1.0 / DI, EPS,
                                        ALU.mult, ALU.add).then_inc(s_ms, 1)
                pool.wait_ge(s_ms, count(k, NC, c + 1))
                nc.gpsimd.tensor_tensor(rs[c % 2][:, :], rs[c % 2][:, :], mhalf[:, :],
                                        ALU.pow).then_inc(s_rs, 1)

            def deviation(k, c):
                pool.wait_ge(s_mv, count(k, NC, c + 1))
                pool.wait_ge(s_x1, count(k, NC, c))
                pool.sem_inc(s_hold, 1)
                nc.gpsimd.tensor_scalar(rln[:, :], mv[:, 1:2], EPS, None, ALU.add).then_inc(s_ve, 1)
                pool.wait_ge(s_ve, count(k, NC, c + 1))
                nc.gpsimd.tensor_tensor(rln[:, :], rln[:, :], mhalf[:, :], ALU.pow).then_inc(s_r1, 1)

            def scatter(k, i, c0):
                for c in (c0, c0 + 1):
                    pool.indirect_dma_start(
                        out=xs, out_offset=bass.IndirectOffsetOnAxis(ap=posu[k.par][:, i, c:c + 1], axis=0),
                        in_=x1[k.par][:, c, :], in_offset=None).then_inc(s_sc, 16)

            def slot_of(k, c, more, rows_of=None):
                state(k, c)
                if c or k is not FIRST:
                    deviation(*before(k, c))
                q, n = following(k, c)
                if c == NC - 1:
                    rms(k, c)
                if more:
                    weighted(q, n)
                if rows_of:
                    if c == NC - 1:
                        pool.wait_ge(s_pos, count(rows_of, 1, 1))
                        pool.sem_inc(s_hold, 1)
                    scatter(rows_of, (c + 1) % NC, 0)
                if more == 2:
                    decays(*following(q, n))
                if rows_of:
                    scatter(rows_of, (c + 1) % NC, 2)
                if c < NC - 1:
                    rms(k, c)

            decays(FIRST, 0)
            weighted(FIRST, 0)
            decays(FIRST, 1)
            slot_of(FIRST, 0, 2)

            def body(k, first, last):
                slot_of(k, 1, 2)
                slot_of(k, 2, 1 if last else 2)
                slot_of(k, 3, 0 if last else 2, None if first else k.prev())
                if not last:
                    slot_of(k.next(), 0, 2, None if first else k.prev())
                    if not first:
                        pool.wait_ge(s_sc, k.count(16 * 2 * NC, 0))
                        pool.sem_inc(s_scd, 1)

            loop(pool, body)
            scatter(LAST.prev(), 1, 0)
            scatter(LAST.prev(), 1, 2)
            deviation(LAST, NC - 1)
            pool.wait_ge(s_pos, count(LAST, 1, 1))
            pool.sem_inc(s_hold, 1)
            for i in range(2):
                scatter(LAST, i, 0)
                scatter(LAST, i, 2)
            pool.wait_ge(s_sc, END.count(16 * 2 * NC, 0))

        @block.scalar
        def _(act):
            start(act, s_xhi, s_dtu, s_pff, s_sil, s_zs, s_xt, s_Bt, s_E, s_ss, s_yT, s_rT, s_ex)
            act.wait_ge(s_w, 16)
            nc.scalar.activation(w_hi[:, :, :], w_raw[:, :, :], ACT.Copy).then_inc(s_whi, 1)

            def split_x(f):
                act.wait_ge(s_xT, f.count(16, 16))
                act.wait_ge(s_pf, count(f, PF_USES, 0))
                nc.scalar.activation(x_hi[:, :, :], x_raw[:, :, :], ACT.Copy).then_inc(s_xhi, 1)

            def dt_of(f):
                act.wait_ge(s_dt, count(f, 1, 0))
                act.wait_ge(s_pf, count(f, PF_USES, 1))
                nc.scalar.activation(dt_raw[:, :], PF[f.par][:, 0:NC * NH], ACT.Copy).then_inc(s_pff, 1)

            def channels(f, u):
                m = CHANNELS[u]
                src = PF[(u + 1 + f.par) % 2][:, :]
                act.wait_ge(s_pf, count(f, PF_USES, u + 2))
                act.wait_ge(s_tap, count(f, TAPS, 0))
                act.wait_ge(s_sil, count(f, 3, 0))
                nc.scalar.activation(cin[f.par][:, m, NCONV - 1:], src, ACT.Copy)
                nc.scalar.activation(conv[:, m, :], src, ACT.Identity, bias=cb[:, m:m + 1],
                                     scale=cw[:, m, NCONV - 1:NCONV]).then_inc(s_pff, 1)

            def exp_dt(f):
                act.wait_ge(s_dtn, count(f, 1, 1))
                nc.scalar.activation(dt_u[:, :], dt_n[:, :], ACT.Exp).then_inc(s_dtu, 1)

            def exp_decays(f):
                act.wait_ge(s_t1, count(f, NC, -NC))
                act.wait_ge(s_S2, count(f, NC, -NC))
                act.wait_ge(s_dw, count(f, 1, -1))
                act.wait_ge(s_pf, count(f, PF_USES, 7))
                nc.scalar.activation(ce[f.par][:, :, :, :].rearrange("p i c h -> p (i c h)"),
                                     PF[(6 + f.par) % 2][:, 0:3 * NC * NH], ACT.Exp).then_inc(s_pff, 1)

            def gates(f, c):
                act.wait_ge(s_yz, count(f, NC, -NC))
                act.wait_ge(s_pf, count(f, PF_USES, 8 + c))
                nc.scalar.activation(zs[f.par][:, c, :], PF[(7 + c + f.par) % 2][:, :],
                                     ACT.Copy).then_inc(s_pff, 1)

            def silus(f):
                act.wait_ge(s_Y, count(f, NC, -NC))
                act.wait_ge(s_tap, count(f, TAPS, TAPS))
                nc.scalar.activation(BT[f.par][:, :], conv[0:NST, 4, :], ACT.Silu).then_inc(s_sil, 1)
                nc.scalar.activation(CT[f.par][:, :], conv[NST:P, 4, :], ACT.Silu).then_inc(s_sil, 1)
                nc.scalar.activation(xch[f.par][:, :, :], conv[:, 0:MX, :], ACT.Silu).then_inc(s_sil, 1)
                act.wait_ge(s_pff, count(f, PF_USES, PF_USES))
                nc.scalar.activation(zs[f.par][:, :, :], zs[f.par][:, :, :], ACT.Silu).then_inc(s_zs, 1)

            def tokens(q, c):
                act.wait_ge(s_XT, count(q, NC, c + 1))
                act.wait_ge(s_xd, count(q, NC, c - 1))
                act.wait_ge(s_xw, count(q, NC, c - 1))
                nc.scalar.activation(x_tok[c % 2][:, :], PX[:, :], ACT.Copy).then_inc(s_xt, 1)
                act.wait_ge(s_G, count(q, NC, c + 1))
                act.wait_ge(s_ds, count(q, NC, c - 1))
                nc.scalar.activation(B_tok[c % 2][:, :], PG[:, Q:Q + NST], ACT.Copy).then_inc(s_Bt, 1)
                act.wait_ge(s_D, count(q, NC, c + 1))
                act.wait_ge(s_M, count(q, NC, c - 1))
                nc.scalar.activation(E[c % 2][:, 0:4, :].rearrange("p h t -> p (h t)"), PD0[:, :], ACT.Exp)
                nc.scalar.activation(E[c % 2][:, 4:8, :].rearrange("p h t -> p (h t)"), PD1[:, :],
                                     ACT.Exp).then_inc(s_E, 1)

            def squares(k, c):
                act.wait_ge(s_yz, count(k, NC, c + 1))
                act.wait_ge(s_rs, count(k, NC, c - 1))
                nc.scalar.activation(junk[:, :], yz[c % 2][:, :], ACT.Square,
                                     accum_out=ss[c % 2][:, :]).then_inc(s_ss, 1)

            def transposed(k, c):
                act.wait_ge(s_YT, count(k, NC, c + 1))
                act.wait_ge(s_O, count(k, NC, c))
                nc.scalar.activation(yT[:, :, :].rearrange("p m t -> p (m t)"), PX[:, :],
                                     ACT.Copy).then_inc(s_yT, 1)

            def router_rows(k, half):
                act.wait_ge(s_RT, count(k, 2, half + 1))
                act.wait_ge(s_lg, count(k, 1, 0))
                nc.scalar.activation(x1T[:, 2 * half:2 * half + 2, :, :].rearrange("p c a t -> p (c a t)"),
                                     PY[:, :], ACT.Copy).then_inc(s_rT, 1)

            def router_exp(k):
                act.wait_ge(s_lm, count(k, 1, 1))
                act.wait_ge(s_mask, count(k, 1, 0))
                nc.scalar.activation(ex[:, :, :], lg[:, :, :], ACT.Exp).then_inc(s_ex, 1)

            split_x(FIRST)
            act.wait_ge(s_small, 144)
            nc.scalar.activation(eA[:, :], alog[:, :], ACT.Exp).then_inc(s_eA, 1)
            dt_of(FIRST)
            channels(FIRST, 0)
            channels(FIRST, 1)
            exp_dt(FIRST)
            for u in (2, 3, 4):
                channels(FIRST, u)
            exp_decays(FIRST)
            for c in range(NC):
                gates(FIRST, c)
            silus(FIRST)
            tokens(FIRST, 0)

            def body(k, first, last):
                f = k.next()
                for c in range(NC):
                    q, n = following(k, c)
                    if c == 0 and not last:
                        split_x(f)
                    if c == 2 and not first:
                        router_exp(k.prev())
                    if c == 3:
                        if not last:
                            silus(f)
                        transposed(k, c)
                        squares(k, c)
                    if n or not last:
                        tokens(q, n)
                    if c == 1 and not first:
                        router_rows(k.prev(), 0)
                    if c == 0 and not last:
                        dt_of(f)
                        channels(f, 0)
                    if c == 1 and not last:
                        exp_dt(f)
                        channels(f, 3)
                    if c == 2 and not last:
                        exp_decays(f)
                        gates(f, 0)
                    if c == 1 and not first:
                        router_rows(k.prev(), 1)
                    if c < NC - 1:
                        transposed(k, c)
                    if c == 0 and not last:
                        channels(f, 1)
                        channels(f, 2)
                    if c == 1 and not last:
                        channels(f, 4)
                    if c == 2 and not last:
                        gates(f, 1)
                        gates(f, 2)
                    if c < NC - 1:
                        squares(k, c)
                    if c == 2 and not last:
                        gates(f, 3)

            loop(act, body)
            router_rows(LAST, 0)
            router_rows(LAST, 1)
            router_exp(LAST)

        @block.vector
        def _(dve):
            start(dve, s_xlo, s_halo, s_dtn, s_dt, s_soft, s_tap, s_S0, s_Gm, s_xd, s_M, s_t1, s_ya, s_S, s_yz, s_r, s_bs,
                  s_mv, s_x1, s_lr, s_lm, s_mask, s_rr, s_pos, s_dvr)
            V = nc.vector
            dve.wait_ge(s_whi, 1)
            V.tensor_tensor(w_lo[:, :, :], w_raw[:, :, :], w_hi[:, :, :].bitcast(F32),
                            ALU.subtract).then_inc(s_wlo, 1)
            dve.wait_ge(s_xhi, count(FIRST, 1, 1))
            V.tensor_tensor(x_lo[:, :, :], x_raw[:, :, :], x_hi[:, :, :].bitcast(F32),
                            ALU.subtract).then_inc(s_xlo, 1)
            dve.wait_ge(s_small, 144)
            for m in range(MX):
                V.tensor_tensor(Dd[:, m, :].rearrange("p (h d) -> p h d", h=2),
                                cst[:, C_ID:C_ID + P].rearrange("p (h d) -> p h d", h=2),
                                Dp[:, 2 * m:2 * m + 2].unsqueeze(2).to_broadcast([P, 2, HD]),
                                ALU.mult).then_inc(s_Dd, 1)
            dve.wait_ge(s_wo_in, 16)
            for m in range(MX):
                V.tensor_scalar(wo[:, m, :], wo[:, m, :], nw[:, m:m + 1], None, ALU.mult).then_inc(s_wo, 1)
            V.tensor_copy(base[:, :], cst[:, C_REG:C_REG + NE]).then_inc(s_base, 1)
            dve.wait_ge(s_eA, 1)
            dve.wait_ge(s_base, 1)
            F = Steps(SOFT)
            R = Steps(ROUTE)
            heads = [P, NC, NH]

            def by_chunk(t):
                return t[:, :].rearrange("p (c h) -> p c h", c=NC)

            def h64(ap):
                return ap.rearrange("p (h d) -> p h d", h=NH)

            def split_x(f):
                dve.wait_ge(s_xhi, count(f, 1, 1))
                V.tensor_tensor(x_lo[:, :, :], x_raw[:, :, :], x_hi[:, :, :].bitcast(F32),
                                ALU.subtract).then_inc(s_xlo, 1)

            def halo(f):
                dve.wait_ge(s_tap, count(f, TAPS, 0))
                if f.par == 0:
                    V.memset(cin[0][:, :, 0:NCONV - 1], 0.0).then_inc(s_halo, 1)
                else:
                    V.tensor_copy(cin[1][:, :, 0:NCONV - 1], cin[0][:, :, BLK:]).then_inc(s_halo, 1)

            def tap(f, u, n):
                m = CHANNELS[u]
                if n == 0:
                    dve.wait_ge(s_halo, count(f, 1, 1))
                    dve.wait_ge(s_pff, count(f, PF_USES, u + 2))
                else:
                    dve.wait_ge(s_tap, count(f, TAPS, taps(u, n)))
                V.scalar_tensor_tensor(out=conv[:, m, :], in0=cin[f.par][:, m, n:n + BLK],
                                       scalar=cw[:, m, n:n + 1], in1=conv[:, m, :],
                                       op0=ALU.mult, op1=ALU.add).then_inc(s_tap, 1)

            def soft_first(f):
                F.begin(f)
                dve.wait_ge(s_pff, count(f, PF_USES, 1))
                V.tensor_tensor(by_chunk(dt_s), by_chunk(dt_raw), dtb[:, :].unsqueeze(1).to_broadcast(heads),
                                ALU.add).then_inc(s_soft, 1)
                dve.wait_ge(s_soft, F.made(1))
                V.tensor_scalar(dt_m[:, :], dt_s[:, :], 0.0, None, ALU.max).then_inc(s_soft, 1)
                F.made(1)
                V.scalar_tensor_tensor(out=dt_n[:, :], in0=dt_s[:, :], scalar=-1.0, in1=dt_s[:, :],
                                       op0=ALU.mult, op1=ALU.min).then_inc(s_dtn, 1)

            def soft_ratio(f):
                dve.wait_ge(s_dtu, count(f, 1, 1))
                V.tensor_scalar(dt_q[:, :], dt_u[:, :], 2.0, None, ALU.add).then_inc(s_soft, 1)
                dve.wait_ge(s_soft, F.made(1))
                V.reciprocal(dt_q[:, :], dt_q[:, :]).then_inc(s_soft, 1)
                dve.wait_ge(s_soft, F.made(1))
                V.tensor_tensor(dt_s[:, :], dt_u[:, :], dt_q[:, :], ALU.mult).then_inc(s_soft, 1)
                F.made(1)

            def soft_square(f):
                dve.wait_ge(s_soft, F.made(0))
                V.tensor_tensor(dt_q[:, :], dt_s[:, :], dt_s[:, :], ALU.mult).then_inc(s_soft, 1)
                dve.wait_ge(s_soft, F.made(1))
                V.tensor_scalar(dt_h[:, :], dt_q[:, :], SERIES[8], None, ALU.mult).then_inc(s_soft, 1)
                F.made(1)

            def soft_term(f, i):
                dve.wait_ge(s_soft, F.made(0))
                V.scalar_tensor_tensor(out=dt_h[:, :], in0=dt_h[:, :], scalar=SERIES[i], in1=dt_q[:, :],
                                       op0=ALU.add, op1=ALU.mult).then_inc(s_soft, 1)
                F.made(1)

            def soft_last(f):
                dve.wait_ge(s_soft, F.made(0))
                V.scalar_tensor_tensor(out=dt_h[:, :], in0=dt_h[:, :], scalar=1.0, in1=dt_s[:, :],
                                       op0=ALU.add, op1=ALU.mult).then_inc(s_soft, 1)
                dve.wait_ge(s_soft, F.made(1))
                dve.wait_ge(s_am, count(f, NC, -NC))
                V.scalar_tensor_tensor(out=dts[f.par][:, :, :].rearrange("p c h -> p (c h)"),
                                       in0=dt_h[:, :], scalar=2.0, in1=dt_m[:, :],
                                       op0=ALU.mult, op1=ALU.add).then_inc(s_soft, 1)
                dve.wait_ge(s_soft, F.made(1))
                V.scalar_tensor_tensor(out=a[f.par][:, :, :], in0=dts[f.par][:, :, :], scalar=-1.0,
                                       in1=eA[:, :].unsqueeze(1).to_broadcast(heads),
                                       op0=ALU.mult, op1=ALU.mult).then_inc(s_dt, 1)
                F.end()

            def tap_pair(f, u, n):
                tap(f, u, n)
                tap(f, u + 1, n)

            def soft_and_taps(f):
                soft_ratio(f)
                tap(f, 2, 0)
                soft_square(f)
                soft_term(f, 7)
                soft_term(f, 6)
                tap(f, 2, 1)
                soft_term(f, 5)
                soft_term(f, 4)
                soft_term(f, 3)
                tap(f, 2, 2)
                soft_term(f, 2)
                soft_term(f, 1)
                soft_last(f)

            def prepare(q, c):
                dve.wait_ge(s_xt, count(q, NC, c + 1))
                dve.wait_ge(s_dt, count(q, 1, 1))
                dve.wait_ge(s_Y, count(q, NC, c - 1))
                V.tensor_tensor(h64(xdt[c % 2][:, :]), h64(x_tok[c % 2][:, :]),
                                dts[q.par][:, c, :].unsqueeze(2).to_broadcast([P, NH, HD]),
                                ALU.mult).then_inc(s_xd, 1)
                dve.wait_ge(s_Bt, count(q, NC, c + 1))
                dve.wait_ge(s_M, count(q, NC, c))
                V.tensor_tensor(Gm[:, :], PG[:, 0:Q], cst[:, C_INCL:C_INCL + Q], ALU.mult).then_inc(s_Gm, 1)

            def decayed(q, c):
                dve.wait_ge(s_Gm, count(q, NC, c + 1))
                dve.wait_ge(s_E, count(q, NC, c + 1))
                dve.wait_ge(s_Y, count(q, NC, c - 1))
                V.tensor_tensor(M[c % 2][:, :, :], E[c % 2][:, :, :],
                                Gm[:, :].unsqueeze(1).to_broadcast([P, NH, Q]), ALU.mult).then_inc(s_M, 1)

            def inherited(k, c):
                if c == 0:
                    dve.wait_ge(s_zs, count(k, 1, 1))
                dve.wait_ge(s_yz, count(k, NC, c))
                dve.wait_ge(s_yi, count(k, NC, c + 1))
                V.tensor_tensor(h64(t1[:, :]), h64(PI[:, :]),
                                ce[k.par][:, 0, c, :].unsqueeze(2).to_broadcast([P, NH, HD]),
                                ALU.mult).then_inc(s_t1, 1)

            def outputs(k, c):
                dve.wait_ge(s_t1, count(k, NC, c + 1))
                dve.wait_ge(s_Y, count(k, NC, c + 1))
                V.tensor_tensor(t1[:, :], t1[:, :], PY[:, :], ALU.add).then_inc(s_ya, 1)
                dve.wait_ge(s_ds, count(k, NC, c + 1))
                dve.wait_ge(s_S2, count(k, NC, c + 1))
                V.tensor_tensor(S[:, :], S2[:, :], PI[0:NST, :], ALU.add).then_inc(s_S, 1)
                dve.wait_ge(s_ya, count(k, NC, c + 1))
                dve.wait_ge(s_ss, count(k, NC, c - 1))
                dve.wait_ge(s_YT, count(k, NC, c - 1))
                V.tensor_tensor(yz[c % 2][:, :], t1[:, :], zs[k.par][:, c, :], ALU.mult).then_inc(s_yz, 1)

            def residual(k, c):
                if c == 0:
                    dve.wait_ge(s_xres[k.par], landed(k, 1))
                dve.wait_ge(s_x1, count(k, NC, c))
                dve.wait_ge(s_O, count(k, NC, c + 1))
                dve.wait_ge(s_rs, count(k, NC, c + 1))
                V.scalar_tensor_tensor(out=r[:, :], in0=PG[:, DM:2 * DM], scalar=rs[c % 2][:, :],
                                       in1=xres[k.par][:, c, :], op0=ALU.mult, op1=ALU.add).then_inc(s_r, 1)
                dve.wait_ge(s_r, count(k, NC, c + 1))
                V.bn_stats(st6[:, :], r[:, :]).then_inc(s_bs, 1)
                dve.wait_ge(s_bs, count(k, NC, c + 1))
                dve.sem_inc(s_hold, 1)
                V.bn_aggr(mv[:, :], st6[:, :]).then_inc(s_mv, 1)

            def finish(k, c):
                if c == 0:
                    dve.wait_ge(s_scd, count(k, 1, -1))
                    dve.wait_ge(s_xo[k.par], sent(k, 1))
                dve.wait_ge(s_r1, count(k, NC, c + 1))
                V.tensor_scalar(x1[k.par][:, c, :], r[:, :], mv[:, 0:1], rln[:, :], ALU.subtract,
                                ALU.mult).then_inc(s_x1, 1)

            ce4 = [P, NC, NE]

            def logits(k):
                R.begin(k)
                dve.wait_ge(s_lg, count(k, 1, 1))
                V.tensor_tensor(lg[:, :, :], PY[:, 0:NC * NE].rearrange("p (c e) -> p c e", c=NC),
                                rb_sb[:, :].unsqueeze(1).to_broadcast(ce4), ALU.add).then_inc(s_lr, 1)
                dve.wait_ge(s_lr, count(k, 1, 1))
                V.tensor_reduce(mx[:, :], lg[:, :, :], AX_X, ALU.max).then_inc(s_dvr, 1)
                dve.wait_ge(s_dvr, R.made(1))
                V.tensor_tensor(lg[:, :, :], lg[:, :, :], mx[:, :].unsqueeze(2).to_broadcast(ce4),
                                ALU.subtract).then_inc(s_lm, 1)

            def choices(k):
                dve.wait_ge(s_ex, count(k, 1, 1))
                V.tensor_reduce(sm[:, :], ex[:, :, :], AX_X, ALU.add).then_inc(s_dvr, 1)
                dve.wait_ge(s_dvr, R.made(1))
                V.reciprocal(sm[:, :], sm[:, :]).then_inc(s_dvr, 1)
                dve.wait_ge(s_dvr, R.made(1))
                V.tensor_tensor(pr[:, :, :], ex[:, :, :], sm[:, :].unsqueeze(2).to_broadcast(ce4),
                                ALU.mult).then_inc(s_dvr, 1)
                dve.wait_ge(s_dvr, R.made(1))
                c44 = [P, NC, NE, NE]
                pj, pi = pr[:, :, :].unsqueeze(2).to_broadcast(c44), pr[:, :, :].unsqueeze(3).to_broadcast(c44)
                V.tensor_tensor(eq[:, :, :, :], pj, pi, ALU.is_equal).then_inc(s_dvr, 1)
                R.made(1)
                V.tensor_tensor(gt[:, :, :, :], pj, pi, ALU.is_gt).then_inc(s_dvr, 1)
                dve.wait_ge(s_dvr, R.made(0))
                V.tensor_tensor(eq[:, :, :, :].rearrange("p c i j -> p c (i j)"),
                                eq[:, :, :, :].rearrange("p c i j -> p c (i j)"),
                                cst[:, C_TIE:C_REG].unsqueeze(1).to_broadcast([P, NC, NE * NE]),
                                ALU.mult).then_inc(s_dvr, 1)
                dve.wait_ge(s_dvr, R.made(2))
                V.tensor_tensor(gt[:, :, :, :], gt[:, :, :, :], eq[:, :, :, :], ALU.add).then_inc(s_dvr, 1)
                dve.wait_ge(s_dvr, R.made(1))
                V.tensor_reduce(rank[:, :, :].rearrange("p c e -> p (c e)"),
                                gt[:, :, :, :].rearrange("p c i j -> p (c i) j"), AX_X, ALU.add).then_inc(s_dvr, 1)
                dve.wait_ge(s_dvr, R.made(1))
                for i in range(2):
                    V.tensor_scalar(oh[:, i, :, :], rank[:, :, :], float(i), None, ALU.is_equal).then_inc(s_dvr, 1)
                    R.made(1)
                dve.wait_ge(s_dvr, R.made(0))
                V.tensor_tensor(mask[:, :, :], oh[:, 0, :, :], oh[:, 1, :, :], ALU.add).then_inc(s_mask, 1)

            def shares(k):
                for i in range(2):
                    V.tensor_tensor(tmp[:, i, :, :], oh[:, i, :, :], pr[:, :, :], ALU.mult).then_inc(s_dvr, 1)
                    R.made(1)
                dve.wait_ge(s_dvr, R.made(0))
                V.tensor_reduce(top[:, :, :].rearrange("p i c -> p (i c)"),
                                tmp[:, :, :, :].rearrange("p i c e -> p (i c) e"), AX_X, ALU.add).then_inc(s_dvr, 1)
                dve.wait_ge(s_dvr, R.made(1))
                V.tensor_tensor(sm[:, :], top[:, 0, :], top[:, 1, :], ALU.add).then_inc(s_dvr, 1)
                dve.wait_ge(s_dvr, R.made(1))
                V.reciprocal(sm[:, :], sm[:, :]).then_inc(s_dvr, 1)
                dve.wait_ge(s_dvr, R.made(1))
                g0 = k.b * (4 * NC) + k.par * 2 * NC
                V.tensor_tensor(
                    share_all[:, bass.ds(g0, 2 * NC)].rearrange("p (i c) -> p i c", i=2), top[:, :, :],
                    sm[:, :].unsqueeze(1).to_broadcast([P, 2, NC]), ALU.mult).then_inc(s_dvr, 1)
                R.made(1)

            def ranks(k):
                dve.wait_ge(s_rk, count(k, 1, 1))
                V.tensor_copy(rk[:, :, :, :].rearrange("p i c e -> p (i c e)"),
                              PY[:, 0:2 * NC * NE]).then_inc(s_rr, 1)

            def slots(k):
                dve.wait_ge(s_rr, count(k, 1, 1))
                for c in range(NC):
                    if c == 0:
                        V.tensor_copy(cbase[:, 0, :], base[:, :]).then_inc(s_dvr, 1)
                    else:
                        V.tensor_tensor(cbase[:, c, :], cbase[:, c - 1, :], rk[:, 1, c - 1, :],
                                        ALU.add).then_inc(s_dvr, 1)
                    dve.wait_ge(s_dvr, R.made(1))
                V.tensor_tensor(base[:, :], cbase[:, NC - 1, :], rk[:, 1, NC - 1, :], ALU.add).then_inc(s_dvr, 1)
                R.made(1)
                V.tensor_tensor(slot[:, :, :], cbase[:, :, :], rk[:, 0, :, :], ALU.add).then_inc(s_dvr, 1)
                dve.wait_ge(s_dvr, R.made(1))
                for i in range(2):
                    V.tensor_tensor(tmp[:, i, :, :], oh[:, i, :, :], slot[:, :, :], ALU.mult).then_inc(s_dvr, 1)
                    R.made(1)
                dve.wait_ge(s_dvr, R.made(0))
                V.tensor_reduce(posf[:, :, :].rearrange("p i c -> p (i c)"),
                                tmp[:, :, :, :].rearrange("p i c e -> p (i c) e"), AX_X, ALU.add).then_inc(s_dvr, 1)
                dve.wait_ge(s_dvr, R.made(1))
                g0 = k.b * (4 * NC) + k.par * 2 * NC
                V.tensor_copy(pos_all[:, bass.ds(g0, 2 * NC)],
                              posf[:, :, :].rearrange("p i c -> p (i c)")).then_inc(s_dvr, 1)
                R.made(1)
                V.tensor_copy(posu[k.par][:, :, :], posf[:, :, :]).then_inc(s_pos, 1)
                R.end()

            halo(FIRST)
            soft_first(FIRST)
            for n in range(NCONV - 1):
                tap_pair(FIRST, 0, n)
            soft_and_taps(FIRST)
            for n in range(NCONV - 1):
                tap_pair(FIRST, 3, n)
            prepare(FIRST, 0)
            decayed(FIRST, 0)

            def body(k, first, last):
                f = k.next()
                for c in range(NC):
                    q, n = following(k, c)
                    if c == 0 and k.par == 0:
                        dve.wait_ge(s_S, count(k, NC, 0))
                        V.memset(S[:, :], 0.0).then_inc(s_S0, 1)
                    inherited(k, c)
                    if c or not first:
                        residual(*before(k, c))
                    outputs(k, c)
                    if c or not first:
                        finish(*before(k, c))
                    if c == 3 and not first:
                        shares(k.prev())
                        slots(k.prev())
                    if c == 0 and not last:
                        halo(f)
                        split_x(f)
                    if n or not last:
                        prepare(q, n)
                        if c == 0 and not last:
                            soft_first(f)
                            tap_pair(f, 0, 0)
                        decayed(q, n)
                    if c == 0 and not last:
                        tap_pair(f, 0, 1)
                    if c == 1:
                        if not last:
                            tap_pair(f, 0, 2)
                            soft_and_taps(f)
                        if not first:
                            logits(k.prev())
                    if c == 2:
                        if not first:
                            choices(k.prev())
                        if not last:
                            for i in range(NCONV - 1):
                                tap_pair(f, 3, i)
                        if not first:
                            ranks(k.prev())

            loop(dve, body)
            residual(LAST, NC - 1)
            finish(LAST, NC - 1)
            logits(LAST)
            choices(LAST)
            ranks(LAST)
            shares(LAST)
            slots(LAST)

        @block.tensor
        def _(pe):
            start(pe, s_pf, s_XT, s_G, s_D, s_Y, s_yi, s_ds, s_YT, s_O, s_RT, s_lg, s_rk)
            pe.wait_ge(s_wlo, 1)
            mm = nc.tensor.matmul
            ident = cst[:, C_ID:C_ID + P]

            def product(dst, lhs, rhs):
                for kt in range(KT):
                    (lh, ll), (rh, rl) = lhs(kt), rhs(kt)
                    mm(dst, lh, rh, start=(kt == 0), stop=False)
                    mm(dst, lh, rl, start=False, stop=False)
                    last = mm(dst, ll, rh, start=False, stop=(kt == KT - 1))
                return last

            def x_of(kt, c):
                return x_hi[:, kt, c * Q:(c + 1) * Q], x_lo[:, kt, c * Q:(c + 1) * Q]

            def w_of(kt, lo, n):
                return w_hi[:, kt, lo:lo + n], w_lo[:, kt, lo:lo + n]

            def dt_of(f):
                pe.wait_ge(s_xhi, count(f, 1, 1))
                pe.wait_ge(s_xlo, count(f, 1, 1))
                pe.wait_ge(s_pff, count(f, PF_USES, -1))
                for c in range(NC):
                    last = product(PF[f.par][:, c * NH:(c + 1) * NH],
                                   lambda kt: x_of(kt, c), lambda kt: w_of(kt, DT0, NH))
                last.then_inc(s_pf, 1)

            def channels(f, u):
                pe.wait_ge(s_pff, count(f, PF_USES, u))
                product(PF[(u + 1 + f.par) % 2][:, :], lambda kt: w_of(kt, X0 + CHANNELS[u] * P, P),
                        lambda kt: (x_hi[:, kt, :], x_lo[:, kt, :])).then_inc(s_pf, 1)

            def sums(f):
                pe.wait_ge(s_pff, count(f, PF_USES, 5))
                pe.wait_ge(s_dt, count(f, 1, 1))
                al = a[f.par][:, :, :].rearrange("p c h -> p (c h)")
                for i, m in enumerate((C_INCL, C_GTR, C_ONE)):
                    last = mm(PF[(6 + f.par) % 2][:, i * NC * NH:(i + 1) * NC * NH], cst[:, m:m + P], al,
                              start=True, stop=True)
                last.then_inc(s_pf, 1)

            def gates(f, c):
                pe.wait_ge(s_pff, count(f, PF_USES, 6 + c))
                product(PF[(7 + c + f.par) % 2][:, :], lambda kt: x_of(kt, c),
                        lambda kt: w_of(kt, Z0, DI)).then_inc(s_pf, 1)

            def tokens(q, c):
                cols = slice(c * Q, (c + 1) * Q)
                if c == 0:
                    pe.wait_ge(s_sil, count(q, 3, 3))
                pe.wait_ge(s_yT, count(q, NC, max(c - 1, 0)))
                for m in range(MX):
                    last = nc.tensor.transpose(PX[:, m * P:(m + 1) * P], xch[q.par][:, m, cols], ident)
                last.then_inc(s_XT, 1)
                pe.wait_ge(s_Gm, count(q, NC, c))
                pe.wait_ge(s_Bt, count(q, NC, c))
                pe.wait_ge(s_r, count(q, NC, c - 1))
                mm(PG[:, 0:Q], BT[q.par][:, cols], CT[q.par][:, cols], start=True, stop=True)
                nc.tensor.transpose(PG[:, Q:Q + NST], BT[q.par][:, cols],
                                    cst[0:NST, C_ID:C_ID + NST]).then_inc(s_G, 1)

            def decays(q, c):
                pe.wait_ge(s_am, count(q, NC, c + 1))
                pe.wait_ge(s_E, count(q, NC, c))
                mm(PD0[:, :], cst[:, C_GTR:C_GTR + Q], am[:, 0:4, :].rearrange("p h t -> p (h t)"),
                   start=True, stop=True)
                mm(PD1[:, :], cst[:, C_GTR:C_GTR + Q], am[:, 4:8, :].rearrange("p h t -> p (h t)"),
                   start=True, stop=True).then_inc(s_D, 1)

            def mix(k, c, first):
                cols = slice(c * Q, (c + 1) * Q)
                pe.wait_ge(s_S, count(k, NC, c))
                if c == 0 and k.par == 0:
                    pe.wait_ge(s_S0, k.b + (1 + BIAS))
                mm(PI[:, :], CT[k.par][:, cols], S[:, :], start=True, stop=True).then_inc(s_yi, 1)
                pe.wait_ge(s_ya, count(k, NC, c))
                if c == 2 and not first:
                    pe.wait_ge(s_lr, count(k, 1, 0))
                if c == 3 and not first:
                    pe.wait_ge(s_rr, count(k, 1, 0))
                pe.wait_ge(s_xd, count(k, NC, c + 1))
                pe.wait_ge(s_M, count(k, NC, c + 1))
                for m in range(MX):
                    mm(PY[:, m * P:(m + 1) * P], xch[k.par][:, m, cols], Dd[:, m, :], start=True, stop=False)
                    for h in (2 * m, 2 * m + 1):
                        last = mm(PY[:, h * HD:(h + 1) * HD], M[c % 2][:, h, :],
                                  xdt[c % 2][:, h * HD:(h + 1) * HD], start=False, stop=(h % 2 == 1))
                last.then_inc(s_Y, 1)
                pe.wait_ge(s_Bt, count(k, NC, c + 1))
                pe.wait_ge(s_xw, count(k, NC, c + 1))
                pe.wait_ge(s_t1, count(k, NC, c + 1))
                mm(PI[0:NST, :], B_tok[c % 2][:, :], xw[c % 2][:, :], start=True, stop=True).then_inc(s_ds, 1)

            def turned(k, c):
                pe.wait_ge(s_xt, count(k, NC, min(c + 2, NC)))
                pe.wait_ge(s_yz, count(k, NC, c + 1))
                for m in range(MX):
                    last = nc.tensor.transpose(PX[:, m * P:(m + 1) * P], yz[c % 2][:, m * P:(m + 1) * P], ident)
                last.then_inc(s_YT, 1)

            def project(k, c, more):
                pe.wait_ge(s_yT, count(k, NC, c + 1))
                pe.wait_ge(s_Gm, count(k, NC, c + 1 + more))
                pe.wait_ge(s_Bt, count(k, NC, c + 1 + more))
                pe.wait_ge(s_r, count(k, NC, c))
                for m in range(MX):
                    last = mm(PG[:, DM:2 * DM], yT[:, m, :], wo[:, m, :], start=(m == 0), stop=(m == MX - 1))
                last.then_inc(s_O, 1)

            def router_rows(k, half):
                pe.wait_ge(s_x1, count(k, NC, NC))
                pe.wait_ge(s_rT, count(k, 2, half))
                for i in range(2):
                    for kt in range(KT):
                        at = (i * KT + kt) * P
                        last = nc.tensor.transpose(PY[:, at:at + P],
                                                   x1[k.par][:, 2 * half + i, kt * P:(kt + 1) * P], ident)
                last.then_inc(s_RT, 1)

            def logits(k):
                pe.wait_ge(s_rT, count(k, 2, 2))
                for c in range(NC):
                    for kt in range(KT):
                        last = mm(PY[:, c * NE:(c + 1) * NE], x1T[:, c, kt, :], wr_sb[:, kt, :],
                                  start=(kt == 0), stop=(kt == KT - 1))
                last.then_inc(s_lg, 1)

            def ranks(k):
                pe.wait_ge(s_mask, count(k, 1, 1))
                mk = mask[:, :, :].rearrange("p c e -> p (c e)")
                mm(PY[:, 0:NC * NE], cst[:, C_LESS:C_LESS + P], mk, start=True, stop=True)
                mm(PY[:, NC * NE:2 * NC * NE], cst[:, C_ONE:C_ONE + P], mk, start=True, stop=True).then_inc(s_rk, 1)

            dt_of(FIRST)
            for u in range(5):
                channels(FIRST, u)
            pe.wait_ge(s_small, 144)
            sums(FIRST)
            for c in range(NC):
                gates(FIRST, c)
            tokens(FIRST, 0)
            decays(FIRST, 0)
            pe.wait_ge(s_Dd, MX)
            pe.wait_ge(s_wo, MX)

            def body(k, first, last):
                f = k.next()
                for c in range(NC):
                    q, n = following(k, c)
                    more = 0 if last and n == 0 else 1
                    mix(k, c, first)
                    if c == 3:
                        turned(k, c)
                        if more:
                            decays(q, n)
                            tokens(q, n)
                        project(k, c, more)
                        continue
                    tokens(q, n)
                    decays(q, n)
                    if c == 0:
                        if not last:
                            dt_of(f)
                            channels(f, 0)
                        turned(k, c)
                        if not last:
                            channels(f, 1)
                            channels(f, 2)
                    if c == 1:
                        if not first:
                            pe.wait_ge(s_ya, count(k, NC, 2))
                            router_rows(k.prev(), 0)
                        if not last:
                            channels(f, 3)
                        if not first:
                            router_rows(k.prev(), 1)
                        turned(k, c)
                        if not first:
                            logits(k.prev())
                        if not last:
                            channels(f, 4)
                    if c == 2:
                        if not last:
                            sums(f)
                            gates(f, 0)
                        turned(k, c)
                        if not last:
                            gates(f, 1)
                            gates(f, 2)
                        if not first:
                            pe.wait_ge(s_ya, count(k, NC, 3))
                            ranks(k.prev())
                    project(k, c, more)
                    if c == 2 and not last:
                        gates(f, 3)

            loop(pe, body)
            pe.wait_ge(s_ya, count(LAST, NC, NC))
            router_rows(LAST, 0)
            router_rows(LAST, 1)
            logits(LAST)
            ranks(LAST)


def route(nc, xs, base, cst, table, pads, zero, pos_all, pos_y):
    with ExitStack() as ctx:
        def sb(name, shape, dt=F32):
            return ctx.enter_context(nc.sbuf_tensor(name, shape, dt))

        cnt = sb("cnt", [P, NE])
        more = sb("more", [P, NE, NTS])
        nt = sb("nt", [P, NE])
        first = sb("first", [P, NE])
        end = sb("end", [P, NE])
        past = sb("past", [P, NE, NTR])
        begun = sb("begun", [P, NE, NTR])
        row = sb("row", [P, NE, NTR])
        off = sb("off", [P, NE])
        by = sb("by", [P, 2 * T // P])
        inreg = sb("inreg", [P, 2 * T // P])
        step = sb("step", [P, 1])
        tf = sb("tf", [P, 2, NTR])
        s_v = ctx.enter_context(nc.semaphore("s_v"))
        s_table = ctx.enter_context(nc.semaphore("s_table"))
        s_pad = ctx.enter_context(nc.semaphore("s_pad"))
        s_zero = ctx.enter_context(nc.semaphore("s_zero"))
        block = ctx.enter_context(nc.Block())

        @block.gpsimd
        def _(pool):
            nc.gpsimd.memset(zero[:, :], 0.0).then_inc(s_zero, 1)

        @block.vector
        def _(dve):
            V = nc.vector
            steps = Steps()
            tiles = [P, NE, NTR]
            tj = cst[:, C_TJ:C_E].rearrange("p (e j) -> p e j", e=NE)
            reg = cst[:, C_REG:C_T16]
            V.tensor_tensor(cnt[:, :], base[:, :], reg, ALU.subtract).then_inc(s_v, 1)
            dve.wait_ge(s_v, steps.made(1))
            V.tensor_copy(pads[0:1, :], base[0:1, :]).then_inc(s_v, 1)
            dve.wait_ge(s_v, steps.made(1))
            V.tensor_tensor(more[:, :, :], cnt[:, :].unsqueeze(2).to_broadcast([P, NE, NTS]),
                                 cst[:, C_T16:C_TJ].rearrange("p (e j) -> p e j", e=NE), ALU.is_gt).then_inc(s_v, 1)
            dve.wait_ge(s_v, steps.made(1))
            V.tensor_reduce(nt[:, :], more[:, :, :], AX_X, ALU.add).then_inc(s_v, 1)
            dve.wait_ge(s_v, steps.made(1))
            V.tensor_copy(end[:, 0:1], nt[:, 0:1]).then_inc(s_v, 1)
            dve.wait_ge(s_v, steps.made(1))
            for e in range(1, NE):
                V.tensor_tensor(end[:, e:e + 1], end[:, e - 1:e], nt[:, e:e + 1], ALU.add).then_inc(s_v, 1)
                dve.wait_ge(s_v, steps.made(1))
            V.tensor_tensor(first[:, :], end[:, :], nt[:, :], ALU.subtract).then_inc(s_v, 1)
            dve.wait_ge(s_v, steps.made(1))
            V.tensor_tensor(past[:, :, :], tj, end[:, :].unsqueeze(2).to_broadcast(tiles), ALU.is_ge).then_inc(s_v, 1)
            dve.wait_ge(s_v, steps.made(1))
            V.tensor_tensor(begun[:, :, :], tj, first[:, :].unsqueeze(2).to_broadcast(tiles), ALU.is_ge).then_inc(s_v, 1)
            dve.wait_ge(s_v, steps.made(1))
            V.tensor_reduce(tf[:, 0, :], past[:, :, :].rearrange("p e j -> p j e"), AX_X, ALU.add).then_inc(s_v, 1)
            dve.wait_ge(s_v, steps.made(1))
            V.tensor_scalar(tf[:, 0, :], tf[:, 0, :], float(NE - 1), 1.0, ALU.min, ALU.add).then_inc(s_v, 1)
            dve.wait_ge(s_v, steps.made(1))
            V.scalar_tensor_tensor(out=off[:, :], in0=first[:, :], scalar=-float(TILE), in1=reg,
                                        op0=ALU.mult, op1=ALU.add).then_inc(s_v, 1)
            dve.wait_ge(s_v, steps.made(1))
            V.scalar_tensor_tensor(out=row[:, :, :], in0=tj, scalar=float(TILE),
                                        in1=off[:, :].unsqueeze(2).to_broadcast(tiles),
                                        op0=ALU.mult, op1=ALU.add).then_inc(s_v, 1)
            dve.wait_ge(s_v, steps.made(1))
            V.tensor_tensor(begun[:, :, :], begun[:, :, :], past[:, :, :], ALU.subtract).then_inc(s_v, 1)
            dve.wait_ge(s_v, steps.made(1))
            V.tensor_tensor(row[:, :, :], row[:, :, :], begun[:, :, :], ALU.mult).then_inc(s_v, 1)
            dve.wait_ge(s_v, steps.made(1))
            V.tensor_reduce(tf[:, 1, :], row[:, :, :].rearrange("p e j -> p j e"), AX_X, ALU.add).then_inc(s_v, 1)
            dve.wait_ge(s_v, steps.made(1))
            V.scalar_tensor_tensor(out=tf[:, 1, :], in0=past[:, NE - 1, :], scalar=float(DUMMY),
                                        in1=tf[:, 1, :], op0=ALU.mult, op1=ALU.add).then_inc(s_v, 1)
            dve.wait_ge(s_v, steps.made(1))
            V.tensor_copy(table[:, :, :], tf[0:1, :, :]).then_inc(s_table, 1)
            V.scalar_tensor_tensor(out=off[:, :], in0=first[:, :], scalar=float(TILE), in1=reg,
                                        op0=ALU.mult, op1=ALU.subtract).then_inc(s_v, 1)
            dve.wait_ge(s_v, steps.made(1))
            V.tensor_scalar(by[:, :], pos_all[:, :], off[:, 0:1], None, ALU.add).then_inc(s_v, 1)
            dve.wait_ge(s_v, steps.made(1))
            for e in range(1, NE):
                V.tensor_tensor(step[:, :], off[:, e:e + 1], off[:, e - 1:e], ALU.subtract).then_inc(s_v, 1)
                dve.wait_ge(s_v, steps.made(1))
                V.tensor_scalar(inreg[:, :], pos_all[:, :], float(R0 + e * CAP), step[:, :], ALU.is_ge, ALU.mult).then_inc(s_v, 1)
                dve.wait_ge(s_v, steps.made(1))
                V.tensor_tensor(by[:, :], by[:, :], inreg[:, :], ALU.add).then_inc(s_v, 1)
                dve.wait_ge(s_v, steps.made(1))
            V.tensor_copy(pos_y[:, :], by[:, :]).then_inc(s_v, 1)
            dve.wait_ge(s_v, steps.made(1))

        @block.sync
        def _(sp):
            sp.wait_ge(s_zero, 1)
            z = zero[:, :].rearrange("p (a d) -> p a d", d=DM)
            sp.dma_start(xs[DUMMY:DUMMY + TILE, :].rearrange("(p a) d -> p a d", p=P), z).then_inc(s_pad, 16)
            sp.wait_ge(s_table, 1)
            for e in range(NE):
                row0 = sp.value_load(pads[0:1, e:e + 1], min_val=R0 + e * CAP, max_val=R0 + e * CAP + T)
                sp.dma_start(xs[bass.ds(row0, TILE), :].rearrange("(p a) d -> p a d", p=P), z).then_inc(s_pad, 16)
            sp.wait_ge(s_pad, 16 * (NE + 1))


ROUTED, SHARED, NONE = "routed", "shared", None
PARTS = [(0, GU), (GU, 2 * GU), (2 * GU, WROW)]


def moe(nc, experts, xs, ys, out, pos_y, share_all, cst, table):
    with ExitStack() as ctx:
        def sb(name, shape, dt=F32):
            return ctx.enter_context(nc.sbuf_tensor(name, shape, dt))

        def bank(name):
            return ctx.enter_context(nc.psum_tensor(name, [P, 512], F32))

        def sem(name):
            return ctx.enter_context(nc.semaphore(name))

        def pair(name, shape, dt=F32):
            return [sb(f"{name}{i}", shape, dt) for i in range(2)]

        w_raw = sb("we_raw", [P, WROW])
        w_hi = pair("we_hi", [P, WROW], F32R)
        w_lo = pair("we_lo", [P, WROW], F32R)
        rows = pair("rows", [P, 2, DM])
        xt_hi = pair("xt_hi", [P, KT, TILE], F32R)
        xt_lo = pair("xt_lo", [P, KT, TILE], F32R)
        gate = pair("gate", [P, TILE])
        h = pair("h", [P, TILE])
        h_hi = pair("h_hi", [P, NCH, TILE], F32R)
        h_lo = pair("h_lo", [P, NCH, TILE], F32R)
        y_sb = pair("y_sb", [P, 2, DM])
        x1r = pair("x1r", [P, 2, DM])
        got = pair("got", [P, 2, 2, DM])
        idx = pair("idx", [P, 4], U32)
        share = pair("share", [P, 4])
        o = pair("o", [P, 2, DM])
        st6 = sb("mst6", [P, 2, 6])
        mv = sb("mmv", [P, 2, 2])
        rstd = sb("mrstd", [P, 2])
        mhalf = sb("mmhalf", [P, 2])

        H = [bank(f"H{i}") for i in range(NCH)]
        PT, PY = bank("PT"), bank("PYo")

        s_part = [sem(f"s_part{i}") for i in range(3)]
        s_rows = [sem("s_rows0"), sem("s_rows1")]
        s_x1r = [sem("s_x1r0"), sem("s_x1r1")]
        s_got = [sem("s_got0"), sem("s_got1")]
        s_ys = [sem("s_ys0"), sem("s_ys1")]
        s_out = [sem("s_out0"), sem("s_out1")]
        (s_wh, s_wl, s_wlp, s_xh, s_xl, s_T, s_gu, s_dn, s_sg, s_h, s_hh, s_hl, s_y, s_yr, s_idx, s_shr,
         s_o, s_mvr, s_rstd, s_mh, s_c, s_pc, s_hold) = [sem("m_" + n) for n in (
             "wh wl wlp xh xl T gu dn sg h hh hl y yr idx shr o mvr rstd mh c pc hold").split()]
        block = ctx.enter_context(nc.Block())

        def steps(eng, step, before=None):
            kind = lambda j: NONE if not 0 <= j < NTR + NTS else ROUTED if j < NTR else SHARED

            def one(j):
                step(Block(j // 2, j % 2), *[kind(j + i) for i in (-1, 0, 1, 2)])

            one(0)
            with eng.Fori(0, NTR // 2 - 2) as b:
                step(Block(b, 1), ROUTED, ROUTED, ROUTED, ROUTED)
                step(Block(b + 1, 0), ROUTED, ROUTED, ROUTED, ROUTED)
            for j in range(NTR - 3, NTR + 1):
                one(j)
            with eng.Fori(NTR // 2, (NTR + NTS) // 2 - 2) as b:
                step(Block(b, 1), SHARED, SHARED, SHARED, SHARED)
                step(Block(b + 1, 0), SHARED, SHARED, SHARED, SHARED)
            for j in range(NTR + NTS - 3, NTR + NTS + 1):
                one(j)

        def sharedno(k):
            return Block(k.b - NTR // 2, k.par)

        def is_(k, j):
            return isinstance(k.b, int) and 2 * k.b + k.par == j

        def rowsof(dram, row):
            return dram[bass.ds(row, TILE), :].rearrange("(a p) d -> p a d", p=P)

        @block.sync
        def _(sp):
            for s in s_out + s_ys:
                sp.sem_inc(s, 16)

            def tile_no(k):
                return k.b * 2 + k.par

            def entry(k, i, top):
                return sp.value_load(table[0:1, i, bass.ds(tile_no(k), 1)], min_val=0, max_val=top)

            def load(k, kind):
                sp.wait_ge(s_T, count(k, 1, -1))
                sp.sem_inc(s_hold, 1)
                if kind == ROUTED:
                    src = rowsof(xs, entry(k, 1, DUMMY))
                else:
                    src = rowsof(xs, tile_no(sharedno(k)) * TILE)
                sp.dma_start(rows[k.par][:, :, :], src).then_inc(s_rows[k.par], 16)
                if kind == ROUTED or is_(k, NTR):
                    expert = entry(k, 0, NE) if kind == ROUTED else 0
                    for i, (c0, c1) in enumerate(PARTS):
                        sp.wait_ge(s_wh, count(k, 3, i - 2))
                        sp.sem_inc(s_hold, 1)
                        if i < 2:
                            sp.wait_ge(s_wl, count(k, 2, i - 1))
                            sp.sem_inc(s_hold, 1)
                        else:
                            sp.wait_ge(s_wlp, count(k, 1, 0))
                            sp.sem_inc(s_hold, 1)
                        sp.dma_start(w_raw[:, c0:c1], experts[bass.ds(expert, 1), :, c0:c1].rearrange("e p n -> (e p) n")
                                     ).then_inc(s_part[i], 16)

            load(Block(0, 0), ROUTED)
            load(Block(0, 1), ROUTED)

            def step(k, prev, this, nxt, nxt2):
                if nxt2:
                    load(k.next().next(), nxt2)
                kp = k.prev() if prev else None
                if this == SHARED:
                    s = sharedno(k)
                    sp.wait_ge(s_o, count(s, 1, -1))
                    sp.sem_inc(s_hold, 1)
                    sp.dma_start(x1r[k.par][:, :, :], rowsof(xs, tile_no(s) * TILE)).then_inc(s_x1r[k.par], 16)
                if prev == ROUTED:
                    sp.wait_ge(s_y, count(kp, 1, 1))
                    sp.sem_inc(s_hold, 1)
                    sp.dma_start(rowsof(ys, tile_no(kp) * TILE), y_sb[kp.par][:, :, :]).then_inc(s_ys[kp.par], 16)
                if prev == SHARED:
                    s = sharedno(kp)
                    sp.wait_ge(s_o, count(s, 1, 1))
                    sp.sem_inc(s_hold, 1)
                    sp.dma_start(rowsof(out, tile_no(s) * TILE), o[kp.par][:, :, :]).then_inc(s_out[kp.par], 16)

            steps(sp, step)
            for i in range(2):
                sp.wait_ge(s_out[i], 16 * (NTS // 2) + 16)

        @block.gpsimd
        def _(pool):
            for s in (s_wlp, s_idx, s_shr, s_rstd, s_pc):
                pool.sem_inc(s, BIAS)
            nc.gpsimd.memset(mhalf[:, :], -0.5).then_inc(s_mh, 1)
            pool.wait_ge(s_mh, 1)

            def split(k):
                c0, c1 = PARTS[2]
                pool.wait_ge(s_part[2], k.count(16, 16))
                pool.wait_ge(s_wh, count(k, 3, 3))
                pool.wait_ge(s_dn, count(k, 1, -1))
                nc.gpsimd.tensor_tensor(w_lo[k.par][:, c0:c1], w_raw[:, c0:c1], w_hi[k.par][:, c0:c1].bitcast(F32),
                                        ALU.subtract).then_inc(s_wlp, 1)

            split(Block(0, 0))

            def step(k, prev, this, nxt, nxt2):
                if nxt == ROUTED or is_(k, NTR - 1):
                    split(k.next())
                if this == SHARED:
                    s = sharedno(k)
                    if is_(k, NTR):
                        for i in range(2):
                            pool.wait_ge(s_ys[i], 16 * (NTR // 2) + 16)
                    pool.wait_ge(s_o, count(s, 1, -1))
                    pool.sem_inc(s_hold, 1)
                    col = s.b * (4 * 2) + 2 * s.par
                    for i in range(2):
                        nc.gpsimd.tensor_copy(idx[k.par][:, 2 * i:2 * i + 2],
                                              pos_y[:, bass.ds(col + 4 * i, 2)]).then_inc(s_idx, 1)
                        nc.gpsimd.tensor_copy(share[k.par][:, 2 * i:2 * i + 2],
                                              share_all[:, bass.ds(col + 4 * i, 2)]).then_inc(s_shr, 1)
                    pool.wait_ge(s_idx, count(s, 2, 2))
                    pool.sem_inc(s_hold, 1)
                    for i in range(2):
                        for half in range(2):
                            pool.indirect_dma_start(
                                out=got[k.par][:, i, half, :], out_offset=None, in_=ys,
                                in_offset=bass.IndirectOffsetOnAxis(ap=idx[k.par][:, 2 * i + half:2 * i + half + 1],
                                                                    axis=0)).then_inc(s_got[k.par], 16)
                if prev == SHARED:
                    s = sharedno(k.prev())
                    pool.wait_ge(s_mvr, count(s, 1, 1))
                    pool.sem_inc(s_hold, 1)
                    nc.gpsimd.tensor_scalar(rstd[:, :], mv[:, :, 1], EPS, None, ALU.add).then_inc(s_pc, 1)
                    pool.wait_ge(s_pc, count(s, 1, 1))
                    nc.gpsimd.tensor_tensor(rstd[:, :], rstd[:, :], mhalf[:, :], ALU.pow).then_inc(s_rstd, 1)

            steps(pool, step)

        @block.scalar
        def _(act):
            for s in (s_wh, s_xh, s_sg, s_hh, s_y):
                act.sem_inc(s, BIAS)

            def split(k, i):
                c0, c1 = PARTS[i]
                act.wait_ge(s_part[i], k.count(16, 16))
                if i < 2:
                    act.wait_ge(s_gu, count(k, NCH, -NCH))
                else:
                    act.wait_ge(s_dn, count(k, 1, -1))
                nc.scalar.activation(w_hi[k.par][:, c0:c1], w_raw[:, c0:c1], ACT.Copy).then_inc(s_wh, 1)

            def split_x(k):
                act.wait_ge(s_T, count(k, 1, 1))
                act.wait_ge(s_gu, count(k, NCH, -NCH))
                nc.scalar.activation(xt_hi[k.par][:, :, :].rearrange("p a t -> p (a t)"), PT[:, :],
                                     ACT.Copy).then_inc(s_xh, 1)

            for i in range(3):
                split(Block(0, 0), i)
            split_x(Block(0, 0))

            def step(k, prev, this, nxt, nxt2):
                def silu(c):
                    act.wait_ge(s_gu, count(k, NCH, c + 1))
                    act.wait_ge(s_h, count(k, NCH, c - 1))
                    if c < NCH - 1:
                        nc.scalar.activation(gate[c % 2][:, :], H[c][:, 0:TILE], ACT.Silu).then_inc(s_sg, 1)
                    else:
                        nc.scalar.activation(gate[c % 2][64:P, :], H[c][0:64, 0:TILE], ACT.Silu).then_inc(s_sg, 1)

                def high(c):
                    lo = 0 if c < NCH - 1 else 64
                    act.wait_ge(s_h, count(k, NCH, c + 1))
                    act.wait_ge(s_dn, count(k, 1, -1))
                    nc.scalar.activation(h_hi[k.par][lo:P, c, :], h[c % 2][lo:P, :], ACT.Copy).then_inc(s_hh, 1)

                if this:
                    silu(0)
                    silu(1)
                    high(0)
                    high(1)
                if nxt == ROUTED or is_(k, NTR - 1):
                    for i in range(3):
                        split(k.next(), i)
                if prev == ROUTED:
                    kp = k.prev()
                    act.wait_ge(s_dn, count(kp, 1, 1))
                    act.wait_ge(s_ys[kp.par], sent(kp, 1))
                    nc.scalar.activation(y_sb[kp.par][:, :, :].rearrange("p a d -> p (a d)"), PY[:, :],
                                         ACT.Copy).then_inc(s_y, 1)
                if this:
                    silu(2)
                    silu(3)
                    high(2)
                if nxt:
                    split_x(k.next())
                if this:
                    silu(4)
                    high(3)
                    silu(5)
                    high(4)
                    high(5)

            steps(act, step)

        @block.vector
        def _(dve):
            V = nc.vector
            for s in (s_wl, s_xl, s_h, s_hl, s_yr, s_o, s_mvr, s_c):
                dve.sem_inc(s, BIAS)
            C = Steps(9)

            def split(k, i):
                c0, c1 = PARTS[i]
                dve.wait_ge(s_part[i], k.count(16, 16))
                dve.wait_ge(s_wh, count(k, 3, i + 1))
                V.tensor_tensor(w_lo[k.par][:, c0:c1], w_raw[:, c0:c1], w_hi[k.par][:, c0:c1].bitcast(F32),
                                ALU.subtract).then_inc(s_wl, 1)

            def split_x(k):
                dve.wait_ge(s_xh, count(k, 1, 1))
                V.tensor_tensor(xt_lo[k.par][:, :, :].rearrange("p a t -> p (a t)"), PT[:, :],
                                xt_hi[k.par][:, :, :].rearrange("p a t -> p (a t)").bitcast(F32),
                                ALU.subtract).then_inc(s_xl, 1)

            for i in range(2):
                split(Block(0, 0), i)
            split_x(Block(0, 0))

            def combine(k):
                s = sharedno(k)
                C.begin(s)
                dve.wait_ge(s_dn, count(k, 1, 1))
                dve.wait_ge(s_x1r[k.par], landed(s, 1))
                dve.wait_ge(s_out[k.par], sent(s, 1))
                V.tensor_tensor(o[k.par][:, :, :].rearrange("p a d -> p (a d)"), PY[:, :],
                                x1r[k.par][:, :, :].rearrange("p a d -> p (a d)"), ALU.add).then_inc(s_yr, 1)
                dve.wait_ge(s_yr, count(s, 1, 1))
                dve.wait_ge(s_got[k.par], landed(s, 4))
                dve.wait_ge(s_shr, count(s, 2, 2))
                for i in range(2):
                    for half in range(2):
                        ins = V.scalar_tensor_tensor(
                            out=o[k.par][:, half, :], in0=got[k.par][:, i, half, :],
                            scalar=share[k.par][:, 2 * i + half:2 * i + half + 1],
                            in1=o[k.par][:, half, :], op0=ALU.mult, op1=ALU.add)
                        ins.then_inc(s_c, 1)
                        C.made(1)
                    dve.wait_ge(s_c, C.made(0))
                for half in range(2):
                    V.bn_stats(st6[:, half, :], o[k.par][:, half, :]).then_inc(s_c, 1)
                    C.made(1)
                dve.wait_ge(s_c, C.made(0))
                dve.sem_inc(s_hold, 1)
                V.bn_aggr(mv[:, 0, :], st6[:, 0, :]).then_inc(s_c, 1)
                C.made(1)
                V.bn_aggr(mv[:, 1, :], st6[:, 1, :]).then_inc(s_mvr, 1)
                dve.wait_ge(s_mvr, count(s, 1, 1))
                dve.wait_ge(s_c, C.made(0))
                dve.wait_ge(s_rstd, count(s, 1, 1))
                V.tensor_scalar(o[k.par][:, 0, :], o[k.par][:, 0, :], mv[:, 0, 0:1], rstd[:, 0:1],
                                         ALU.subtract, ALU.mult).then_inc(s_c, 1)
                C.made(1)
                V.tensor_scalar(o[k.par][:, 1, :], o[k.par][:, 1, :], mv[:, 1, 0:1], rstd[:, 1:2],
                                ALU.subtract, ALU.mult).then_inc(s_o, 1)
                V.memset(st6[0:1, 0, 0:1], 0.0).then_inc(s_c, 1)
                C.made(1)
                C.end()

            def step(k, prev, this, nxt, nxt2):
                def product(c):
                    lo = 0 if c < NCH - 1 else 64
                    up = H[c][lo:P, 0:TILE] if lo else H[c][:, TILE:2 * TILE]
                    dve.wait_ge(s_sg, count(k, NCH, c + 1))
                    dve.wait_ge(s_hh, count(k, NCH, c - 1))
                    dve.wait_ge(s_hl, count(k, NCH, c - 1))
                    V.tensor_tensor(h[c % 2][lo:P, :], gate[c % 2][lo:P, :], up, ALU.mult).then_inc(s_h, 1)

                def low(c):
                    lo = 0 if c < NCH - 1 else 64
                    dve.wait_ge(s_hh, count(k, NCH, c + 1))
                    V.tensor_tensor(h_lo[k.par][lo:P, c, :], h[c % 2][lo:P, :],
                                    h_hi[k.par][lo:P, c, :].bitcast(F32), ALU.subtract).then_inc(s_hl, 1)

                if this:
                    product(0)
                    product(1)
                    low(0)
                    low(1)
                if nxt == ROUTED or is_(k, NTR - 1):
                    for i in range(2):
                        split(k.next(), i)
                if this:
                    product(2)
                    product(3)
                    low(2)
                if nxt:
                    split_x(k.next())
                if this:
                    product(4)
                    low(3)
                    product(5)
                    low(4)
                    low(5)
                if prev == SHARED:
                    combine(k.prev())

            steps(dve, step)

        @block.tensor
        def _(pe):
            mm = nc.tensor.matmul
            for s in (s_T, s_gu, s_dn):
                pe.sem_inc(s, BIAS)

            def turn(k):
                pe.wait_ge(s_rows[k.par], landed(k, 1))
                pe.wait_ge(s_xl, count(k, 1, 0))
                for kt in range(KT):
                    for half in range(2):
                        at = kt * TILE + half * P
                        last = nc.tensor.transpose(PT[:, at:at + P], rows[k.par][:, half, kt * P:(kt + 1) * P],
                                                   cst[:, C_ID:C_ID + P])
                last.then_inc(s_T, 1)

            turn(Block(0, 0))

            def down(k, kind):
                wp = k.par if kind == ROUTED else 0
                pe.wait_ge(s_hl, count(k, NCH, NCH))
                if kind == ROUTED:
                    pe.wait_ge(s_wlp, count(k, 1, 1))
                    pe.wait_ge(s_y, count(k, 1, 0))
                else:
                    pe.wait_ge(s_wlp, count(Block(NTR // 2, 0), 1, 1))
                    pe.wait_ge(s_y, count(Block(NTR // 2, 0), 1, 0))
                    pe.wait_ge(s_yr, count(sharedno(k), 1, 0))
                for half in range(2):
                    dst = PY[:, half * DM:(half + 1) * DM]
                    for c in range(NCH):
                        lo = 0 if c < NCH - 1 else 64
                        hs = slice(half * P, (half + 1) * P)
                        ws = slice(2 * GU + c * DM, 2 * GU + (c + 1) * DM)
                        hh, hl = h_hi[k.par][lo:P, c, hs], h_lo[k.par][lo:P, c, hs]
                        mm(dst, hh, w_hi[wp][lo:P, ws], start=(c == 0), stop=False)
                        mm(dst, hh, w_lo[wp][lo:P, ws], start=False, stop=False)
                        last = mm(dst, hl, w_hi[wp][lo:P, ws], start=False, stop=(c == NCH - 1))
                last.then_inc(s_dn, 1)

            def step(k, prev, this, nxt, nxt2):
                wp = k.par if this == ROUTED else 0

                def gate_up(c):
                    pe.wait_ge(s_h, count(k, NCH, c - NCH + 1))
                    for j in range(2 if c < NCH - 1 else 1):
                        dst = H[c][:, j * TILE:(j + 1) * TILE]
                        for kt in range(KT):
                            ws = slice(kt * GU + (2 * c + j) * P, kt * GU + (2 * c + j + 1) * P)
                            xh, xl = xt_hi[k.par][:, kt, :], xt_lo[k.par][:, kt, :]
                            mm(dst, w_hi[wp][:, ws], xh, start=(kt == 0), stop=False)
                            mm(dst, w_lo[wp][:, ws], xh, start=False, stop=False)
                            last = mm(dst, w_hi[wp][:, ws], xl, start=False, stop=(kt == KT - 1))
                    last.then_inc(s_gu, 1)

                if this:
                    pe.wait_ge(s_xl, count(k, 1, 1))
                    if this == ROUTED or is_(k, NTR):
                        pe.wait_ge(s_wl, count(k, 2, 2))
                for c in range(NCH):
                    if this:
                        gate_up(c)
                    if c == 1 and prev:
                        down(k.prev(), prev)
                    if c == 2 and nxt:
                        turn(k.next())

            steps(pe, step)


_OUT = ((BATCH, SEQ, DM), "float32")


def kernel(**inputs):
    import concourse.bacc as bacc
    from concourse.bass_utils import run_bass_kernel_spmd

    a = {n: np.asarray(v) for n, v in inputs.items()}

    def on_partitions(v):
        return np.ascontiguousarray(np.broadcast_to(v.reshape(1, -1), (P, v.size)))

    def in_tiles(v):
        return np.ascontiguousarray(np.moveaxis(v.reshape(-1, P, *v.shape[1:]), 0, 1))

    def expert_rows(g, u, d):
        n = g.shape[0]
        gt, ut = (np.swapaxes(w, 1, 2).reshape(n, KT, P, FF) for w in (g, u))
        full = (NCH - 1) * P
        pairs = np.stack([w[..., :full].reshape(n, KT, P, NCH - 1, P) for w in (gt, ut)], axis=4)
        gu = np.concatenate([pairs.reshape(n, KT, P, -1), gt[..., full:], ut[..., full:]], axis=3)
        dt = np.swapaxes(d, 1, 2)
        dn = np.zeros((n, NCH, P, DM), np.float32)
        dn[:, :NCH - 1] = dt[:, :full].reshape(n, NCH - 1, P, DM)
        dn[:, NCH - 1, P // 2:] = dt[:, full:]
        return np.ascontiguousarray(np.concatenate(
            [np.swapaxes(gu, 1, 2).reshape(n, P, -1), np.swapaxes(dn, 1, 2).reshape(n, P, -1)], axis=2))

    x = np.ascontiguousarray(a["L0_attn_x"].reshape(T, DM))
    experts = expert_rows(*(np.concatenate([a["L0_ffn_s" + w][None], a["L0_ffn_r" + w]]) for w in "gud"))
    arrays = {
        "x": x,
        "xT": in_tiles(np.ascontiguousarray(x.T)),
        "W_in": np.ascontiguousarray(a["L0_attn_W_in"]),
        "conv_w": np.ascontiguousarray(a["L0_attn_conv_w"]),
        "conv_b": in_tiles(a["L0_attn_conv_b"]),
        "dt_bias": on_partitions(a["L0_attn_dt_bias"]),
        "A_log": on_partitions(a["L0_attn_A_log"]),
        "Dh": on_partitions(a["L0_attn_D"]),
        "norm_w": in_tiles(a["L0_attn_norm_w"]),
        "W_out": np.ascontiguousarray(a["L0_attn_W_out"]),
        "experts": experts,
        "wr": in_tiles(np.ascontiguousarray(a["L0_ffn_wr"].T)),
        "rb": on_partitions(a["L0_ffn_rb"]),
        "consts": constants(),
    }
    nc = bacc.Bacc("TRN2", target_bir_lowering=False, num_devices=1)
    args = {n: nc.dram_tensor(n, v.shape, F32, kind="ExternalInput").ap() for n, v in arrays.items()}
    args["xs"] = nc.dram_tensor("xs", (NROWS, DM), F32).ap()
    args["ys"] = nc.dram_tensor("ys", (NTR * TILE, DM), F32).ap()
    args["out"] = nc.dram_tensor("out", (T, DM), F32, kind="ExternalOutput").ap()
    program(nc, **args)
    got = run_bass_kernel_spmd(nc, [arrays], core_ids=[0]).results[0]["out"]
    return got.reshape(_OUT[0])
```

```python
from contextlib import ExitStack

import numpy as np

import concourse.bass as bass
from concourse import mybir

F32 = mybir.dt.float32
F32R = mybir.dt.float32r
U32 = mybir.dt.uint32
I32 = mybir.dt.int32
ALU = mybir.AluOpType
ACT = mybir.ActivationFunctionType
AX_X = mybir.AxisListType.X

P = 128
BATCH, SEQ, DM = 4, 1024, 256
T = BATCH * SEQ
KT = DM // P
DI = 512
NST = 64
NH = 8
HD = DI // NH
NCONV = 4
NPROJ = 2 * DI + 2 * NST + NH
Z0, X0, BC0, DT0 = 0, DI, 2 * DI, 2 * DI + 2 * NST
Q = 128
NC = 4
BLK = NC * Q
NBLK = T // BLK
MX = DI // P
EPS = 1e-5

NE = 7
FF = 704
NCH = 6
TILE = 256
BIAS = 2
CAP = T + TILE
R0 = T
DUMMY = R0 + NE * CAP
NROWS = DUMMY + TILE
NTR = (2 * T + NE * (TILE - 1)) // TILE
NTR += NTR % 2
NTS = T // TILE
GU = 11 * P
DN = NCH * DM
WROW = KT * GU + DN


class Block:

    def __init__(self, b, par):
        self.b, self.par = b, par

    def next(self):
        return Block(self.b, 1) if self.par == 0 else Block(self.b + 1, 0)

    def prev(self):
        return Block(self.b, 0) if self.par else Block(self.b - 1, 1)

    def count(self, per, n):
        return self.b * (2 * per) + (self.par * per + n)


def count(k, per, n):
    v = k.count(per, n + BIAS)
    return max(v, BIAS) if isinstance(v, int) else v


def landed(k, loads):
    return (k.b + 1) * (16 * loads)


def sent(k, dmas):
    return k.b * (16 * dmas) + 16


class Steps:

    def __init__(self, per=0):
        self.per, self.n, self.k = per, 0, None

    def begin(self, k):
        self.k, self.n = k, 0

    def made(self, n):
        self.n += n
        return self.n if self.k is None else count(self.k, self.per, self.n)

    def end(self):
        assert self.n == self.per, (self.n, self.per)


def program(nc, x, xT, W_in, conv_w, conv_b, dt_bias, A_log, Dh, norm_w, W_out, experts, wr, rb, consts,
            xs, ys, out):
    with ExitStack() as ctx:
        keep = ctx.enter_context
        pos_all = keep(nc.sbuf_tensor("pos_all", [P, 2 * T // P], F32))
        off_y = keep(nc.sbuf_tensor("off_y", [P, NE], F32))
        share_all = keep(nc.sbuf_tensor("share_all", [P, 2 * T // P], F32))
        base = keep(nc.sbuf_tensor("base", [P, NE], F32))
        cst = keep(nc.sbuf_tensor("cst", [P, NCONST], F32))
        table = keep(nc.sbuf_tensor("table", [1, 2, NTR], I32))
        pads = keep(nc.sbuf_tensor("pads", [1, NE], I32))
        mixer(nc, x, xT, W_in, conv_w, conv_b, dt_bias, A_log, Dh, norm_w, W_out, wr, rb, consts, xs,
              pos_all, off_y, share_all, base, cst, table, pads)
        moe(nc, experts, xs, ys, out, pos_all, off_y, share_all, cst, table)


C_ID = 0
C_INCL = C_ID + P
C_GTR = C_INCL + P
C_LESS = C_GTR + P
C_ONE = C_LESS + P
C_TIE = C_ONE + P
C_REG = C_TIE + NE * NE
C_T16 = C_REG + NE
C_TJ = C_T16 + NE * NTS
C_E = C_TJ + NE * NTR
NCONST = C_E + NE * NTR


def constants():
    c = np.zeros((P, NCONST), np.float32)
    k, t = np.arange(P)[:, None], np.arange(P)[None, :]
    for at, m in ((C_ID, k == t), (C_INCL, k <= t), (C_GTR, k > t), (C_LESS, k < t), (C_ONE, k >= 0)):
        c[:, at:at + P] = m
    i, j = np.arange(NE)[:, None], np.arange(NE)[None, :]
    c[:, C_TIE:C_REG] = (j < i).reshape(-1)
    c[:, C_REG:C_T16] = R0 + CAP * np.arange(NE)
    c[:, C_T16:C_TJ] = np.tile(TILE * np.arange(NTS), NE)
    c[:, C_TJ:C_E] = np.tile(np.arange(NTR), NE)
    c[:, C_E:] = np.repeat(np.arange(NE), NTR)
    return c


PF_USES, SOFT, ROUTE, TAPS = 12, 16, 25, 15
DT_ROWS, DT_TOKENS, CHANNEL_USE, SUMS, GATES = 0, 2, (1, 3, 4, 5, 6), 7, 8
SERIES = [1.0 / (2 * i + 1) for i in range(9)]
CHANNELS = (4, 0, 1, 2, 3)


def following(k, c):
    return (k, c + 1) if c < NC - 1 else (k.next(), 0)


def before(k, c):
    return (k, c - 1) if c else (k.prev(), NC - 1)


def taps(u, n):
    if u == 2:
        return 2 * (NCONV - 1) + n
    first, second = (0, 1) if u < 2 else (3 * (NCONV - 1), 4)
    return first + 2 * n - (1 if n and u != second else 0)


def mixer(nc, x, xT, W_in, conv_w, conv_b, dt_bias, A_log, Dh, norm_w, W_out, wr, rb, consts, xs,
          pos_all, off_y, share_all, base, cst, table, pads):
    with ExitStack() as ctx:
        def sb(name, shape, dt=F32):
            return ctx.enter_context(nc.sbuf_tensor(name, shape, dt))

        def bank(name):
            return ctx.enter_context(nc.psum_tensor(name, [P, 512], F32))

        def sem(name):
            return ctx.enter_context(nc.semaphore(name))

        def pair(name, shape, dt=F32):
            return [sb(f"{name}{i}", shape, dt) for i in range(2)]

        w_raw = sb("w_raw", [P, KT, NPROJ])
        w_hi = sb("w_hi", [P, KT, NPROJ], F32R)
        w_lo = sb("w_lo", [P, KT, NPROJ], F32R)
        cw = sb("cw", [P, 5, NCONV])
        cb = sb("cb", [P, 5])
        dtb = sb("dtb", [P, NH])
        alog = sb("alog", [P, NH])
        eA = sb("eA", [P, NH])
        Dp = sb("Dp", [P, NH])
        Dd = sb("Dd", [P, MX, P])
        nw = sb("nw", [P, MX])
        wo = sb("wo", [P, MX, DM])
        wr_sb = sb("wr_sb", [P, KT, NE])
        rb_sb = sb("rb_sb", [P, NE])
        x_raw = sb("x_raw", [P, KT, BLK])
        x_hi = sb("x_hi", [P, KT, BLK], F32R)
        x_lo = sb("x_lo", [P, KT, BLK], F32R)
        cin = pair("cin", [P, 5, BLK + NCONV - 1])
        conv = sb("conv", [P, 5, BLK])
        xch = pair("xch", [P, MX, BLK])
        BT = pair("BT", [NST, BLK])
        CT = pair("CT", [NST, BLK])
        zs = pair("zs", [P, NC, DI])
        xres = pair("xres", [P, NC, DM])
        dtT = sb("dtT", [NH, BLK])
        dt_raw = sb("dt_raw", [P, NC * NH])
        dt_n = sb("dt_n", [P, NC * NH])
        dt_u = sb("dt_u", [P, NC * NH])
        dt_s = sb("dt_s", [P, NC * NH])
        dt_q = sb("dt_q", [P, NC * NH])
        dt_h = sb("dt_h", [P, NC * NH])
        dt_m = sb("dt_m", [P, NC * NH])
        dts = pair("dts", [P, NC, NH])
        a = pair("a", [P, NC, NH])
        ce = pair("ce", [P, 3, NC, NH])
        dw = pair("dw", [P, NC, NH])
        x_tok = pair("x_tok", [P, DI])
        B_tok = pair("B_tok", [P, NST])
        a_hi = pair("a_hi", [P, NC, NH], F32R)
        a_lo = pair("a_lo", [P, NC, NH], F32R)
        am_hi = sb("am_hi", [P, NH, Q], F32R)
        am_lo = sb("am_lo", [P, NH, Q], F32R)
        after = sb("after", [P, Q], F32R)
        E = pair("E", [P, NH, Q])
        Gm = sb("Gm", [P, Q])
        M = pair("M", [P, NH, Q])
        xdt = pair("xdt", [P, DI])
        xw = pair("xw", [P, DI])
        t1 = sb("t1", [P, DI])
        yz = pair("yz", [P, DI])
        junk = sb("junk", [P, DI])
        ss = pair("ss", [P, 1])
        rs = pair("rs", [P, 1])
        yT = sb("yT", [P, MX, Q])
        S = sb("S", [NST, DI])
        S2 = sb("S2", [NST, DI])
        r = sb("r", [P, DM])
        st6 = sb("st6", [P, 6])
        mv = sb("mv", [P, 2])
        rln = sb("rln", [P, 1])
        mhalf = sb("mhalf", [P, 1])
        x1 = pair("x1", [P, NC, DM])
        x1T = sb("x1T", [P, NC, KT, Q])
        lg = sb("lg", [P, NC, NE])
        mx = sb("mx", [P, NC])
        ex = sb("ex", [P, NC, NE])
        pr = sb("pr", [P, NC, NE])
        sm = sb("sm", [P, NC])
        gt = sb("gt", [P, NC, NE, NE])
        eq = sb("eq", [P, NC, NE, NE])
        rank = sb("rank", [P, NC, NE])
        oh = sb("oh", [P, 2, NC, NE])
        mask = sb("mask", [P, NC, NE])
        rk = sb("rk", [P, 2, NC, NE])
        cbase = sb("cbase", [P, NC, NE])
        slot = sb("slot", [P, NC, NE])
        tmp = sb("tmp", [P, 2, NC, NE])
        posf = sb("posf", [P, 2, NC])
        top = sb("top", [P, 2, NC])
        posu = [sb(f"posu{i}", [P, 2, NC], U32) for i in range(2)]

        cnt = sb("cnt", [P, NE])
        more = sb("more", [P, NE, NTS])
        nt = sb("nt", [P, NE])
        first = sb("first", [P, NE])
        end = sb("end", [P, NE])
        past = sb("past", [P, NE, NTR])
        begun = sb("begun", [P, NE, NTR])
        row = sb("row", [P, NE, NTR])
        off = sb("off", [P, NE])
        tf = sb("tf", [P, 2, NTR])
        zero = w_raw[:, 0, 0:2 * DM]

        PF = [bank("PF0"), bank("PF1")]
        PX, PG, PD0, PD1, PY, PI = [bank(n) for n in ("PX", "PG", "PD0", "PD1", "PY", "PI")]

        s_w, s_wz, s_wo_in = sem("s_w"), sem("s_wz"), sem("s_wo_in")
        s_small = sem("s_small")
        s_xT = sem("s_xT")
        s_xres = [sem("s_xres0"), sem("s_xres1")]
        s_whi, s_wlo, s_eA, s_wo, s_Dd, s_base, s_mh = [sem(n) for n in
                                                       ("s_whi", "s_wlo", "s_eA", "s_wo", "s_Dd", "s_base", "s_mh")]
        s_xhi, s_xlo, s_halo, s_dtn, s_dtu, s_dt, s_soft, s_dw, s_ahi, s_alo = [sem(n) for n in (
            "s_xhi", "s_xlo", "s_halo", "s_dtn", "s_dtu", "s_dt", "s_soft", "s_dw", "s_ahi", "s_alo")]
        s_pf, s_pff = sem("s_pf"), sem("s_pff")
        s_tap, s_sil, s_zs = sem("s_tap"), sem("s_sil"), sem("s_zs")
        s_S0 = sem("s_S0")
        s_hold = sem("s_hold")
        (s_XT, s_xt, s_Bt, s_G, s_D, s_am, s_E, s_Gm, s_xd, s_xw, s_M, s_Y, s_yi, s_t1, s_ya, s_S2, s_ds, s_S,
         s_yz, s_ss, s_ms, s_rs, s_YT, s_yT, s_O, s_r, s_bs, s_mv, s_ve, s_r1, s_x1) = [sem("s_" + n) for n in (
             "XT xt Bt G D am E Gm xd xw M Y yi t1 ya S2 ds S yz ss ms rs YT yT O r bs mv ve r1 x1").split()]
        s_RT, s_rT, s_lg, s_lr, s_lm, s_ex, s_mask, s_rk, s_rr, s_pos, s_dvr = [sem(n) for n in (
            "s_RT s_rT s_lg s_lr s_lm s_ex s_mask s_rk s_rr s_pos s_dvr").split()]
        s_sc, s_scd = sem("s_sc"), sem("s_scd")
        s_xo = [sem("s_xo0"), sem("s_xo1")]

        block = ctx.enter_context(nc.Block())

        def loop(eng, body):
            body(Block(0, 0), True, False)
            with eng.Fori(0, NBLK // 2 - 1) as b:
                body(Block(b, 1), False, False)
                body(Block(b + 1, 0), False, False)
            body(Block(NBLK // 2 - 1, 1), False, True)

        def start(eng, *sems):
            for s in sems:
                eng.sem_inc(s, BIAS)

        s_v = sem("s_v")
        s_pads, s_pad, s_zero = sem("s_pads"), sem("s_pad"), sem("s_zero")

        FIRST, LAST, END = Block(0, 0), Block(NBLK // 2 - 1, 1), Block(NBLK // 2, 0)
        x_v = x.rearrange("(g p) d -> p g d", p=P)
        xs_v = xs[0:T, :].rearrange("(g p) d -> p g d", p=P)

        @block.sync
        def _(sp):
            for s in s_xo:
                sp.sem_inc(s, 16)
            w_v = W_in.rearrange("(a p) n -> p a n", p=P)
            sp.dma_start(w_raw[:, :, X0:], w_v[:, :, X0:]).then_inc(s_w, 16)

            def load_x(f):
                sp.wait_ge(s_xhi, count(f, 1, 0))
                sp.sem_inc(s_hold, 1)
                sp.wait_ge(s_xlo, count(f, 1, 0))
                sp.sem_inc(s_hold, 1)
                t0 = f.b * (2 * BLK) + f.par * BLK
                sp.dma_start(x_raw[:, :, :], xT[:, :, bass.ds(t0, BLK)]).then_inc(s_xT, 16)

            def load_residual(f):
                sp.wait_ge(s_r, count(f, NC, -NC))
                sp.sem_inc(s_hold, 1)
                g0 = f.b * (2 * NC) + f.par * NC
                sp.dma_start(xres[f.par][:, :, :], x_v[:, bass.ds(g0, NC), :]).then_inc(s_xres[f.par], 16)

            def store(k):
                sp.wait_ge(s_x1, count(k, NC, NC))
                sp.sem_inc(s_hold, 1)
                g0 = k.b * (2 * NC) + k.par * NC
                sp.dma_start(xs_v[:, bass.ds(g0, NC), :], x1[k.par][:, :, :]).then_inc(s_xo[k.par], 16)

            load_x(FIRST)
            sp.dma_start(w_raw[:, :, 0:X0], w_v[:, :, 0:X0]).then_inc(s_wz, 16)
            for dst, src in ((cst[:, :], consts), (cw[:, :, :], conv_w.rearrange("(m p) k -> p m k", p=P)),
                             (cb[:, :], conv_b), (dtb[:, :], dt_bias), (alog[:, :], A_log), (Dp[:, :], Dh),
                             (nw[:, :], norm_w), (wr_sb[:, :, :], wr), (rb_sb[:, :], rb)):
                sp.dma_start(dst, src).then_inc(s_small, 16)
            sp.dma_start(wo[:, :, :], W_out.rearrange("(m p) n -> p m n", p=P)).then_inc(s_wo_in, 16)
            load_residual(FIRST)

            def body(k, first, last):
                if not last:
                    load_x(k.next())
                    load_residual(k.next())
                if not first:
                    store(k.prev())

            loop(sp, body)
            store(LAST)
            sp.wait_ge(s_zero, 1)
            z = zero.rearrange("p (a d) -> p a d", d=DM)
            sp.dma_start(xs[DUMMY:DUMMY + TILE, :].rearrange("(p a) d -> p a d", p=P), z).then_inc(s_pad, 16)
            sp.wait_ge(s_pads, 1)
            for e in range(NE):
                row0 = sp.value_load(pads[0:1, e:e + 1], min_val=R0 + e * CAP, max_val=R0 + e * CAP + T)
                sp.dma_start(xs[bass.ds(row0, TILE), :].rearrange("(p a) d -> p a d", p=P), z).then_inc(s_pad, 16)
            sp.wait_ge(s_pad, 16 * (NE + 1))
            for i in range(2):
                sp.wait_ge(s_xo[i], 16 * (NBLK // 2) + 16)

        @block.gpsimd
        def _(pool):
            start(pool, s_ahi, s_alo, s_scd, s_am, s_xw, s_S2, s_dw, s_ms, s_rs, s_ve, s_r1)
            nc.gpsimd.memset(mhalf[:, :], -0.5).then_inc(s_mh, 1)
            pool.wait_ge(s_wlo, 2)
            nc.gpsimd.memset(zero, 0.0).then_inc(s_zero, 1)
            pool.wait_ge(s_small, 144)
            pool.wait_ge(s_mh, 1)

            def decays(q, c):
                if c == 0:
                    pool.wait_ge(s_dt, count(q, 1, 1))
                    pool.wait_ge(s_am, count(q, NC, -NC))
                    nc.gpsimd.tensor_tensor(a_hi[q.par][:, :, :].rearrange("p c h -> p (c h)"),
                                            a[q.par][:, :, :].rearrange("p c h -> p (c h)"),
                                            cst[:, C_ONE:C_ONE + NC * NH], ALU.mult).then_inc(s_ahi, 1)
                    pool.wait_ge(s_ahi, count(q, 1, 1))
                    nc.gpsimd.tensor_tensor(a_lo[q.par][:, :, :], a[q.par][:, :, :],
                                            a_hi[q.par][:, :, :].bitcast(F32), ALU.subtract).then_inc(s_alo, 1)
                    pool.wait_ge(s_alo, count(q, 1, 1))
                pool.wait_ge(s_D, count(q, NC, c))
                for am, half in ((am_hi, a_hi), (am_lo, a_lo)):
                    last = nc.gpsimd.tensor_tensor(
                        am[:, :, :], half[q.par][:, c, :].bitcast(F32).unsqueeze(2).to_broadcast([P, NH, Q]),
                        cst[:, C_INCL:C_INCL + Q].unsqueeze(1).to_broadcast([P, NH, Q]), ALU.mult)
                last.then_inc(s_am, 1)

            def weighted(q, c):
                if c == 0:
                    pool.wait_ge(s_dt, count(q, 1, 1))
                    pool.wait_ge(s_pff, count(q, PF_USES, SUMS + 1))
                    pool.wait_ge(s_xw, count(q, NC, -NC))
                    nc.gpsimd.tensor_tensor(dw[q.par][:, :, :], dts[q.par][:, :, :], ce[q.par][:, 1, :, :],
                                            ALU.mult).then_inc(s_dw, 1)
                    pool.wait_ge(s_dw, count(q, 1, 1))
                pool.wait_ge(s_xt, count(q, NC, c + 1))
                pool.wait_ge(s_ds, count(q, NC, c - 1))
                nc.gpsimd.tensor_tensor(
                    xw[c % 2][:, :].rearrange("p (h d) -> p h d", h=NH),
                    x_tok[c % 2][:, :].rearrange("p (h d) -> p h d", h=NH),
                    dw[q.par][:, c, :].unsqueeze(2).to_broadcast([P, NH, HD]), ALU.mult).then_inc(s_xw, 1)

            def state(k, c):
                pool.wait_ge(s_pff, count(k, PF_USES, SUMS + 1))
                pool.wait_ge(s_S, count(k, NC, c))
                if k is FIRST and c == 0:
                    pool.wait_ge(s_S0, 1)
                nc.gpsimd.tensor_tensor(
                    S2[:, :].rearrange("p (h d) -> p h d", h=NH), S[:, :].rearrange("p (h d) -> p h d", h=NH),
                    ce[k.par][0:NST, 2, c, :].unsqueeze(2).to_broadcast([NST, NH, HD]), ALU.mult).then_inc(s_S2, 1)

            def rms(k, c):
                pool.wait_ge(s_ss, count(k, NC, c + 1))
                pool.wait_ge(s_r, count(k, NC, c - 1))
                pool.sem_inc(s_hold, 1)
                nc.gpsimd.tensor_scalar(rs[c % 2][:, :], ss[c % 2][:, :], 1.0 / DI, EPS,
                                        ALU.mult, ALU.add).then_inc(s_ms, 1)
                pool.wait_ge(s_ms, count(k, NC, c + 1))
                nc.gpsimd.tensor_tensor(rs[c % 2][:, :], rs[c % 2][:, :], mhalf[:, :],
                                        ALU.pow).then_inc(s_rs, 1)

            def deviation(k, c):
                pool.wait_ge(s_mv, count(k, NC, c + 1))
                pool.wait_ge(s_x1, count(k, NC, c))
                pool.sem_inc(s_hold, 1)
                nc.gpsimd.tensor_scalar(rln[:, :], mv[:, 1:2], EPS, None, ALU.add).then_inc(s_ve, 1)
                pool.wait_ge(s_ve, count(k, NC, c + 1))
                nc.gpsimd.tensor_tensor(rln[:, :], rln[:, :], mhalf[:, :], ALU.pow).then_inc(s_r1, 1)

            def scatter(k, i, c0):
                for c in (c0, c0 + 1):
                    pool.indirect_dma_start(
                        out=xs, out_offset=bass.IndirectOffsetOnAxis(ap=posu[k.par][:, i, c:c + 1], axis=0),
                        in_=x1[k.par][:, c, :], in_offset=None).then_inc(s_sc, 16)

            def slot_of(k, c, more, rows_of=None):
                state(k, c)
                if c or k is not FIRST:
                    deviation(*before(k, c))
                if rows_of and c == 0:
                    scatter(rows_of, 0, 2)
                q, n = following(k, c)
                if c == NC - 1:
                    if more == 2:
                        decays(*following(q, n))
                    rms(k, c)
                if more:
                    weighted(q, n)
                if rows_of:
                    if c == NC - 1:
                        pool.wait_ge(s_pos, count(rows_of, 1, 1))
                        pool.sem_inc(s_hold, 1)
                    scatter(rows_of, (c + 1) % NC, 0)
                if more == 2 and c < NC - 1:
                    decays(*following(q, n))
                if rows_of and c == 0:
                    scatter(rows_of, 1, 2)
                if c < NC - 1:
                    rms(k, c)

            decays(FIRST, 0)
            weighted(FIRST, 0)
            decays(FIRST, 1)
            slot_of(FIRST, 0, 2)

            def body(k, first, last):
                slot_of(k, 1, 2)
                slot_of(k, 2, 1 if last else 2)
                slot_of(k, 3, 0 if last else 2, None if first else k.prev())
                if not last:
                    slot_of(k.next(), 0, 2, None if first else k.prev())
                    if not first:
                        pool.wait_ge(s_sc, k.count(16 * 2 * NC, 0))
                        pool.sem_inc(s_scd, 1)

            loop(pool, body)
            deviation(LAST, NC - 1)
            scatter(LAST.prev(), 0, 2)
            scatter(LAST.prev(), 1, 0)
            scatter(LAST.prev(), 1, 2)
            pool.wait_ge(s_pos, count(LAST, 1, 1))
            pool.sem_inc(s_hold, 1)
            for i in range(2):
                scatter(LAST, i, 0)
                scatter(LAST, i, 2)
            pool.wait_ge(s_sc, END.count(16 * 2 * NC, 0))

        @block.scalar
        def _(act):
            start(act, s_xhi, s_dtu, s_pff, s_sil, s_zs, s_xt, s_Bt, s_E, s_ss, s_yT, s_rT, s_ex)
            act.wait_ge(s_w, 16)
            nc.scalar.activation(w_hi[:, :, X0:], w_raw[:, :, X0:], ACT.Copy).then_inc(s_whi, 1)

            def split_x(f):
                act.wait_ge(s_xT, f.count(16, 16))
                act.wait_ge(s_pf, count(f, PF_USES, 0))
                nc.scalar.activation(x_hi[:, :, :], x_raw[:, :, :], ACT.Copy).then_inc(s_xhi, 1)

            def dt_rows(f):
                act.wait_ge(s_pf, count(f, PF_USES, DT_ROWS + 1))
                nc.scalar.activation(dtT[:, :], PF[DT_ROWS % 2][0:NH, :], ACT.Copy).then_inc(s_pff, 1)

            def dt_tokens(f):
                act.wait_ge(s_dt, count(f, 1, 0))
                act.wait_ge(s_pf, count(f, PF_USES, DT_TOKENS + 1))
                nc.scalar.activation(dt_raw[:, :], PF[DT_TOKENS % 2][:, 0:NC * NH], ACT.Copy).then_inc(s_pff, 1)

            def channels(f, u):
                m = CHANNELS[u]
                src = PF[CHANNEL_USE[u] % 2][:, :]
                act.wait_ge(s_pf, count(f, PF_USES, CHANNEL_USE[u] + 1))
                act.wait_ge(s_tap, count(f, TAPS, 0))
                act.wait_ge(s_sil, count(f, 3, 0))
                nc.scalar.activation(cin[f.par][:, m, NCONV - 1:], src, ACT.Copy)
                nc.scalar.activation(conv[:, m, :], src, ACT.Identity, bias=cb[:, m:m + 1],
                                     scale=cw[:, m, NCONV - 1:NCONV]).then_inc(s_pff, 1)

            def exp_dt(f):
                act.wait_ge(s_dtn, count(f, 1, 1))
                nc.scalar.activation(dt_u[:, :], dt_n[:, :], ACT.Exp).then_inc(s_dtu, 1)

            def exp_decays(f):
                act.wait_ge(s_t1, count(f, NC, -NC))
                act.wait_ge(s_S2, count(f, NC, -NC))
                act.wait_ge(s_dw, count(f, 1, -1))
                act.wait_ge(s_pf, count(f, PF_USES, SUMS + 1))
                nc.scalar.activation(ce[f.par][:, :, :, :].rearrange("p i c h -> p (i c h)"),
                                     PF[SUMS % 2][:, 0:3 * NC * NH], ACT.Exp).then_inc(s_pff, 1)

            def gates(f, c):
                act.wait_ge(s_yz, count(f, NC, -NC))
                act.wait_ge(s_pf, count(f, PF_USES, GATES + c + 1))
                nc.scalar.activation(zs[f.par][:, c, :], PF[(GATES + c) % 2][:, :],
                                     ACT.Copy).then_inc(s_pff, 1)

            def silus(f):
                act.wait_ge(s_Y, count(f, NC, -NC))
                act.wait_ge(s_tap, count(f, TAPS, TAPS))
                nc.scalar.activation(BT[f.par][:, :], conv[0:NST, 4, :], ACT.Silu).then_inc(s_sil, 1)
                nc.scalar.activation(CT[f.par][:, :], conv[NST:P, 4, :], ACT.Silu).then_inc(s_sil, 1)
                nc.scalar.activation(xch[f.par][:, :, :], conv[:, 0:MX, :], ACT.Silu).then_inc(s_sil, 1)

            def gate_silus(f):
                act.wait_ge(s_pff, count(f, PF_USES, PF_USES))
                nc.scalar.activation(zs[f.par][:, :, :], zs[f.par][:, :, :], ACT.Silu).then_inc(s_zs, 1)

            def x_tokens(q, c):
                act.wait_ge(s_XT, count(q, NC, c + 1))
                act.wait_ge(s_xd, count(q, NC, c - 1))
                act.wait_ge(s_xw, count(q, NC, c - 1))
                nc.scalar.activation(x_tok[c % 2][:, :], PX[:, :], ACT.Copy).then_inc(s_xt, 1)

            def B_tokens(q, c):
                act.wait_ge(s_G, count(q, NC, c + 1))
                act.wait_ge(s_ds, count(q, NC, c - 1))
                nc.scalar.activation(B_tok[c % 2][:, :], PG[:, Q:Q + NST], ACT.Copy).then_inc(s_Bt, 1)

            def decays(q, c):
                act.wait_ge(s_D, count(q, NC, c + 1))
                act.wait_ge(s_M, count(q, NC, c - 1))
                nc.scalar.activation(E[c % 2][:, 0:4, :].rearrange("p h t -> p (h t)"), PD0[:, :], ACT.Exp)
                nc.scalar.activation(E[c % 2][:, 4:8, :].rearrange("p h t -> p (h t)"), PD1[:, :],
                                     ACT.Exp).then_inc(s_E, 1)

            def squares(k, c):
                act.wait_ge(s_yz, count(k, NC, c + 1))
                act.wait_ge(s_rs, count(k, NC, c - 1))
                nc.scalar.activation(junk[:, :], yz[c % 2][:, :], ACT.Square,
                                     accum_out=ss[c % 2][:, :]).then_inc(s_ss, 1)

            def transposed(k, c):
                act.wait_ge(s_YT, count(k, NC, c + 1))
                act.wait_ge(s_O, count(k, NC, c))
                nc.scalar.activation(yT[:, :, :].rearrange("p m t -> p (m t)"), PX[:, :],
                                     ACT.Copy).then_inc(s_yT, 1)

            def router_rows(k, half):
                act.wait_ge(s_RT, count(k, 2, half + 1))
                act.wait_ge(s_lg, count(k, 1, 0))
                nc.scalar.activation(x1T[:, 2 * half:2 * half + 2, :, :].rearrange("p c a t -> p (c a t)"),
                                     PY[:, :], ACT.Copy).then_inc(s_rT, 1)

            def router_exp(k):
                act.wait_ge(s_lm, count(k, 1, 1))
                act.wait_ge(s_mask, count(k, 1, 0))
                nc.scalar.activation(ex[:, :, :], lg[:, :, :], ACT.Exp).then_inc(s_ex, 1)

            split_x(FIRST)
            act.wait_ge(s_wz, 16)
            nc.scalar.activation(w_hi[:, :, 0:X0], w_raw[:, :, 0:X0], ACT.Copy).then_inc(s_whi, 1)
            act.wait_ge(s_small, 144)
            nc.scalar.activation(eA[:, :], alog[:, :], ACT.Exp).then_inc(s_eA, 1)
            dt_rows(FIRST)
            channels(FIRST, 0)
            dt_tokens(FIRST)
            channels(FIRST, 1)
            exp_dt(FIRST)
            for u in (2, 3, 4):
                channels(FIRST, u)
            exp_decays(FIRST)
            gates(FIRST, 0)
            gates(FIRST, 1)
            decays(FIRST, 0)
            silus(FIRST)
            B_tokens(FIRST, 0)
            x_tokens(FIRST, 0)
            gates(FIRST, 2)
            gates(FIRST, 3)
            gate_silus(FIRST)

            def body(k, first, last):
                f = k.next()
                for c in range(NC):
                    q, n = following(k, c)
                    if c == 0 and not last:
                        split_x(f)
                    if c == 2 and not first:
                        router_exp(k.prev())
                    if c == 3:
                        if not last:
                            decays(q, n)
                            silus(f)
                            B_tokens(q, n)
                        transposed(k, c)
                        if not last:
                            x_tokens(q, n)
                        squares(k, c)
                        if not last:
                            gates(f, 3)
                            gate_silus(f)
                        continue
                    x_tokens(q, n)
                    B_tokens(q, n)
                    decays(q, n)
                    if c == 1 and not first:
                        router_rows(k.prev(), 0)
                    if c == 0 and not last:
                        dt_rows(f)
                        channels(f, 0)
                        dt_tokens(f)
                    if c == 1 and not last:
                        exp_dt(f)
                        channels(f, 3)
                    if c == 2 and not last:
                        exp_decays(f)
                        gates(f, 0)
                    if c == 1 and not first:
                        router_rows(k.prev(), 1)
                    transposed(k, c)
                    if c == 0 and not last:
                        channels(f, 1)
                        channels(f, 2)
                    if c == 1 and not last:
                        channels(f, 4)
                    if c == 2 and not last:
                        gates(f, 1)
                        gates(f, 2)
                    squares(k, c)

            loop(act, body)
            router_rows(LAST, 0)
            router_rows(LAST, 1)
            router_exp(LAST)

        @block.vector
        def _(dve):
            start(dve, s_xlo, s_halo, s_dtn, s_dt, s_soft, s_tap, s_Gm, s_xd, s_M, s_t1, s_ya, s_S, s_yz, s_r, s_bs,
                  s_mv, s_x1, s_lr, s_lm, s_mask, s_rr, s_pos, s_dvr)
            V = nc.vector
            dve.wait_ge(s_whi, 1)
            V.tensor_tensor(w_lo[:, :, X0:], w_raw[:, :, X0:], w_hi[:, :, X0:].bitcast(F32),
                            ALU.subtract).then_inc(s_wlo, 1)
            dve.wait_ge(s_xhi, count(FIRST, 1, 1))
            V.tensor_tensor(x_lo[:, :, :], x_raw[:, :, :], x_hi[:, :, :].bitcast(F32),
                            ALU.subtract).then_inc(s_xlo, 1)
            dve.wait_ge(s_whi, 2)
            V.tensor_tensor(w_lo[:, :, 0:X0], w_raw[:, :, 0:X0], w_hi[:, :, 0:X0].bitcast(F32),
                            ALU.subtract).then_inc(s_wlo, 1)
            dve.wait_ge(s_small, 144)
            for m in range(MX):
                V.tensor_tensor(Dd[:, m, :].rearrange("p (h d) -> p h d", h=2),
                                cst[:, C_ID:C_ID + P].rearrange("p (h d) -> p h d", h=2),
                                Dp[:, 2 * m:2 * m + 2].unsqueeze(2).to_broadcast([P, 2, HD]),
                                ALU.mult).then_inc(s_Dd, 1)
            V.tensor_copy(after[:, :], cst[:, C_GTR:C_GTR + Q]).then_inc(s_Dd, 1)
            dve.wait_ge(s_wo_in, 16)
            for m in range(MX):
                V.tensor_scalar(wo[:, m, :], wo[:, m, :], nw[:, m:m + 1], None, ALU.mult).then_inc(s_wo, 1)
            V.memset(S[:, :], 0.0).then_inc(s_S0, 1)
            V.tensor_copy(base[:, :], cst[:, C_REG:C_REG + NE]).then_inc(s_base, 1)
            dve.wait_ge(s_eA, 1)
            dve.wait_ge(s_base, 1)
            F = Steps(SOFT)
            R = Steps(ROUTE)
            heads = [P, NC, NH]

            def by_chunk(t):
                return t[:, :].rearrange("p (c h) -> p c h", c=NC)

            def h64(ap):
                return ap.rearrange("p (h d) -> p h d", h=NH)

            def split_x(f):
                dve.wait_ge(s_xhi, count(f, 1, 1))
                V.tensor_tensor(x_lo[:, :, :], x_raw[:, :, :], x_hi[:, :, :].bitcast(F32),
                                ALU.subtract).then_inc(s_xlo, 1)

            def halo(f):
                dve.wait_ge(s_tap, count(f, TAPS, 0))
                if f.par == 0:
                    V.memset(cin[0][:, :, 0:NCONV - 1], 0.0).then_inc(s_halo, 1)
                else:
                    V.tensor_copy(cin[1][:, :, 0:NCONV - 1], cin[0][:, :, BLK:]).then_inc(s_halo, 1)

            def tap(f, u, n):
                m = CHANNELS[u]
                if n == 0:
                    dve.wait_ge(s_halo, count(f, 1, 1))
                    dve.wait_ge(s_pff, count(f, PF_USES, CHANNEL_USE[u] + 1))
                else:
                    dve.wait_ge(s_tap, count(f, TAPS, taps(u, n)))
                V.scalar_tensor_tensor(out=conv[:, m, :], in0=cin[f.par][:, m, n:n + BLK],
                                       scalar=cw[:, m, n:n + 1], in1=conv[:, m, :],
                                       op0=ALU.mult, op1=ALU.add).then_inc(s_tap, 1)

            def soft_first(f):
                F.begin(f)
                dve.wait_ge(s_pff, count(f, PF_USES, DT_TOKENS + 1))
                V.tensor_tensor(by_chunk(dt_s), by_chunk(dt_raw), dtb[:, :].unsqueeze(1).to_broadcast(heads),
                                ALU.add).then_inc(s_soft, 1)
                dve.wait_ge(s_soft, F.made(1))
                V.tensor_scalar(dt_m[:, :], dt_s[:, :], 0.0, None, ALU.max).then_inc(s_soft, 1)
                F.made(1)
                V.scalar_tensor_tensor(out=dt_n[:, :], in0=dt_s[:, :], scalar=-1.0, in1=dt_s[:, :],
                                       op0=ALU.mult, op1=ALU.min).then_inc(s_dtn, 1)

            def soft_ratio(f):
                dve.wait_ge(s_dtu, count(f, 1, 1))
                V.tensor_scalar(dt_q[:, :], dt_u[:, :], 2.0, None, ALU.add).then_inc(s_soft, 1)
                dve.wait_ge(s_soft, F.made(1))
                V.reciprocal(dt_q[:, :], dt_q[:, :]).then_inc(s_soft, 1)
                dve.wait_ge(s_soft, F.made(1))
                V.tensor_tensor(dt_s[:, :], dt_u[:, :], dt_q[:, :], ALU.mult).then_inc(s_soft, 1)
                F.made(1)

            def soft_square(f):
                dve.wait_ge(s_soft, F.made(0))
                V.tensor_tensor(dt_q[:, :], dt_s[:, :], dt_s[:, :], ALU.mult).then_inc(s_soft, 1)
                dve.wait_ge(s_soft, F.made(1))
                V.tensor_scalar(dt_h[:, :], dt_q[:, :], SERIES[8], None, ALU.mult).then_inc(s_soft, 1)
                F.made(1)

            def soft_term(f, i):
                dve.wait_ge(s_soft, F.made(0))
                V.scalar_tensor_tensor(out=dt_h[:, :], in0=dt_h[:, :], scalar=SERIES[i], in1=dt_q[:, :],
                                       op0=ALU.add, op1=ALU.mult).then_inc(s_soft, 1)
                F.made(1)

            def soft_last(f):
                dve.wait_ge(s_soft, F.made(0))
                V.scalar_tensor_tensor(out=dt_h[:, :], in0=dt_h[:, :], scalar=1.0, in1=dt_s[:, :],
                                       op0=ALU.add, op1=ALU.mult).then_inc(s_soft, 1)
                dve.wait_ge(s_soft, F.made(1))
                dve.wait_ge(s_am, count(f, NC, -NC))
                V.scalar_tensor_tensor(out=dts[f.par][:, :, :].rearrange("p c h -> p (c h)"),
                                       in0=dt_h[:, :], scalar=2.0, in1=dt_m[:, :],
                                       op0=ALU.mult, op1=ALU.add).then_inc(s_soft, 1)
                dve.wait_ge(s_soft, F.made(1))
                V.scalar_tensor_tensor(out=a[f.par][:, :, :], in0=dts[f.par][:, :, :], scalar=-1.0,
                                       in1=eA[:, :].unsqueeze(1).to_broadcast(heads),
                                       op0=ALU.mult, op1=ALU.mult).then_inc(s_dt, 1)
                F.end()

            def tap_pair(f, u, n):
                tap(f, u, n)
                tap(f, u + 1, n)

            def soft_and_taps(f):
                soft_ratio(f)
                tap(f, 2, 0)
                soft_square(f)
                soft_term(f, 7)
                soft_term(f, 6)
                tap(f, 2, 1)
                soft_term(f, 5)
                soft_term(f, 4)

            def soft_end(f):
                soft_term(f, 3)
                tap(f, 2, 2)
                soft_term(f, 2)
                soft_term(f, 1)
                soft_last(f)

            def scores(q, c):
                dve.wait_ge(s_Bt, count(q, NC, c + 1))
                dve.wait_ge(s_M, count(q, NC, c))
                V.tensor_tensor(Gm[:, :], PG[:, 0:Q], cst[:, C_INCL:C_INCL + Q], ALU.mult).then_inc(s_Gm, 1)

            def by_dt(q, c):
                dve.wait_ge(s_xt, count(q, NC, c + 1))
                dve.wait_ge(s_dt, count(q, 1, 1))
                dve.wait_ge(s_Y, count(q, NC, c - 1))
                V.tensor_tensor(h64(xdt[c % 2][:, :]), h64(x_tok[c % 2][:, :]),
                                dts[q.par][:, c, :].unsqueeze(2).to_broadcast([P, NH, HD]),
                                ALU.mult).then_inc(s_xd, 1)

            def decayed(q, c):
                dve.wait_ge(s_Gm, count(q, NC, c + 1))
                dve.wait_ge(s_E, count(q, NC, c + 1))
                dve.wait_ge(s_Y, count(q, NC, c - 1))
                V.tensor_tensor(M[c % 2][:, :, :], E[c % 2][:, :, :],
                                Gm[:, :].unsqueeze(1).to_broadcast([P, NH, Q]), ALU.mult).then_inc(s_M, 1)

            def inherited(k, c):
                if c == 0:
                    dve.wait_ge(s_zs, count(k, 1, 1))
                dve.wait_ge(s_yz, count(k, NC, c))
                dve.wait_ge(s_yi, count(k, NC, c + 1))
                V.tensor_tensor(h64(t1[:, :]), h64(PI[:, :]),
                                ce[k.par][:, 0, c, :].unsqueeze(2).to_broadcast([P, NH, HD]),
                                ALU.mult).then_inc(s_t1, 1)

            def outputs(k, c):
                dve.wait_ge(s_t1, count(k, NC, c + 1))
                dve.wait_ge(s_Y, count(k, NC, c + 1))
                V.tensor_tensor(t1[:, :], t1[:, :], PY[:, :], ALU.add).then_inc(s_ya, 1)

            def gated(k, c):
                dve.wait_ge(s_ya, count(k, NC, c + 1))
                dve.wait_ge(s_ss, count(k, NC, c - 1))
                dve.wait_ge(s_YT, count(k, NC, c - 1))
                V.tensor_tensor(yz[c % 2][:, :], t1[:, :], zs[k.par][:, c, :], ALU.mult).then_inc(s_yz, 1)

            def state(k, c):
                dve.wait_ge(s_ds, count(k, NC, c + 1))
                dve.wait_ge(s_S2, count(k, NC, c + 1))
                if k.par == 1 and c == NC - 1:
                    V.memset(S[:, :], 0.0).then_inc(s_S, 1)
                else:
                    V.tensor_tensor(S[:, :], S2[:, :], PI[0:NST, :], ALU.add).then_inc(s_S, 1)

            def residual(k, c):
                if c == 0:
                    dve.wait_ge(s_xres[k.par], landed(k, 1))
                dve.wait_ge(s_x1, count(k, NC, c))
                dve.wait_ge(s_O, count(k, NC, c + 1))
                dve.wait_ge(s_rs, count(k, NC, c + 1))
                V.scalar_tensor_tensor(out=r[:, :], in0=PG[:, DM:2 * DM], scalar=rs[c % 2][:, :],
                                       in1=xres[k.par][:, c, :], op0=ALU.mult, op1=ALU.add).then_inc(s_r, 1)
                dve.wait_ge(s_r, count(k, NC, c + 1))
                V.bn_stats(st6[:, :], r[:, :]).then_inc(s_bs, 1)
                dve.wait_ge(s_bs, count(k, NC, c + 1))
                dve.sem_inc(s_hold, 1)
                V.bn_aggr(mv[:, :], st6[:, :]).then_inc(s_mv, 1)

            def finish(k, c):
                if c == 0:
                    dve.wait_ge(s_scd, count(k, 1, -1))
                    dve.wait_ge(s_xo[k.par], sent(k, 1))
                dve.wait_ge(s_r1, count(k, NC, c + 1))
                V.tensor_scalar(x1[k.par][:, c, :], r[:, :], mv[:, 0:1], rln[:, :], ALU.subtract,
                                ALU.mult).then_inc(s_x1, 1)

            ce4 = [P, NC, NE]

            def logits(k):
                R.begin(k)
                dve.wait_ge(s_lg, count(k, 1, 1))
                V.tensor_tensor(lg[:, :, :], PY[:, 0:NC * NE].rearrange("p (c e) -> p c e", c=NC),
                                rb_sb[:, :].unsqueeze(1).to_broadcast(ce4), ALU.add).then_inc(s_lr, 1)
                dve.wait_ge(s_lr, count(k, 1, 1))
                V.tensor_reduce(mx[:, :], lg[:, :, :], AX_X, ALU.max).then_inc(s_dvr, 1)
                dve.wait_ge(s_dvr, R.made(1))
                V.tensor_tensor(lg[:, :, :], lg[:, :, :], mx[:, :].unsqueeze(2).to_broadcast(ce4),
                                ALU.subtract).then_inc(s_lm, 1)

            def choices(k):
                dve.wait_ge(s_ex, count(k, 1, 1))
                V.tensor_reduce(sm[:, :], ex[:, :, :], AX_X, ALU.add).then_inc(s_dvr, 1)
                dve.wait_ge(s_dvr, R.made(1))
                V.reciprocal(sm[:, :], sm[:, :]).then_inc(s_dvr, 1)
                dve.wait_ge(s_dvr, R.made(1))
                V.tensor_tensor(pr[:, :, :], ex[:, :, :], sm[:, :].unsqueeze(2).to_broadcast(ce4),
                                ALU.mult).then_inc(s_dvr, 1)
                dve.wait_ge(s_dvr, R.made(1))
                c44 = [P, NC, NE, NE]
                pj, pi = pr[:, :, :].unsqueeze(2).to_broadcast(c44), pr[:, :, :].unsqueeze(3).to_broadcast(c44)
                V.tensor_tensor(eq[:, :, :, :], pj, pi, ALU.is_equal).then_inc(s_dvr, 1)
                R.made(1)
                V.tensor_tensor(gt[:, :, :, :], pj, pi, ALU.is_gt).then_inc(s_dvr, 1)
                dve.wait_ge(s_dvr, R.made(0))
                V.tensor_tensor(eq[:, :, :, :].rearrange("p c i j -> p c (i j)"),
                                eq[:, :, :, :].rearrange("p c i j -> p c (i j)"),
                                cst[:, C_TIE:C_REG].unsqueeze(1).to_broadcast([P, NC, NE * NE]),
                                ALU.mult).then_inc(s_dvr, 1)
                dve.wait_ge(s_dvr, R.made(2))
                V.tensor_tensor(gt[:, :, :, :], gt[:, :, :, :], eq[:, :, :, :], ALU.add).then_inc(s_dvr, 1)
                dve.wait_ge(s_dvr, R.made(1))
                V.tensor_reduce(rank[:, :, :].rearrange("p c e -> p (c e)"),
                                gt[:, :, :, :].rearrange("p c i j -> p (c i) j"), AX_X, ALU.add).then_inc(s_dvr, 1)
                dve.wait_ge(s_dvr, R.made(1))
                for i in range(2):
                    V.tensor_scalar(oh[:, i, :, :], rank[:, :, :], float(i), None, ALU.is_equal).then_inc(s_dvr, 1)
                    R.made(1)
                dve.wait_ge(s_dvr, R.made(0))
                V.tensor_tensor(mask[:, :, :], oh[:, 0, :, :], oh[:, 1, :, :], ALU.add).then_inc(s_mask, 1)

            def shares(k):
                V.tensor_tensor(tmp[:, :, :, :], oh[:, :, :, :], pr[:, :, :].unsqueeze(1).to_broadcast(
                    [P, 2, NC, NE]), ALU.mult).then_inc(s_dvr, 1)
                dve.wait_ge(s_dvr, R.made(1))
                V.tensor_reduce(top[:, :, :].rearrange("p i c -> p (i c)"),
                                tmp[:, :, :, :].rearrange("p i c e -> p (i c) e"), AX_X, ALU.add).then_inc(s_dvr, 1)
                dve.wait_ge(s_dvr, R.made(1))
                V.tensor_tensor(sm[:, :], top[:, 0, :], top[:, 1, :], ALU.add).then_inc(s_dvr, 1)
                dve.wait_ge(s_dvr, R.made(1))
                V.reciprocal(sm[:, :], sm[:, :]).then_inc(s_dvr, 1)
                dve.wait_ge(s_dvr, R.made(1))
                g0 = k.b * (4 * NC) + k.par * 2 * NC
                V.tensor_tensor(
                    share_all[:, bass.ds(g0, 2 * NC)].rearrange("p (i c) -> p i c", i=2), top[:, :, :],
                    sm[:, :].unsqueeze(1).to_broadcast([P, 2, NC]), ALU.mult).then_inc(s_dvr, 1)
                R.made(1)
                R.end()

            def ranks(k):
                dve.wait_ge(s_rk, count(k, 1, 1))
                V.tensor_copy(rk[:, :, :, :].rearrange("p i c e -> p (i c e)"),
                              PY[:, 0:2 * NC * NE]).then_inc(s_rr, 1)

            def slots(k):
                dve.wait_ge(s_rr, count(k, 1, 1))
                for c in range(NC):
                    if c == 0:
                        V.tensor_copy(cbase[:, 0, :], base[:, :]).then_inc(s_dvr, 1)
                    else:
                        V.tensor_tensor(cbase[:, c, :], cbase[:, c - 1, :], rk[:, 1, c - 1, :],
                                        ALU.add).then_inc(s_dvr, 1)
                    dve.wait_ge(s_dvr, R.made(1))
                V.tensor_tensor(base[:, :], cbase[:, NC - 1, :], rk[:, 1, NC - 1, :], ALU.add).then_inc(s_dvr, 1)
                R.made(1)
                V.tensor_tensor(slot[:, :, :], cbase[:, :, :], rk[:, 0, :, :], ALU.add).then_inc(s_dvr, 1)
                dve.wait_ge(s_dvr, R.made(1))
                V.tensor_tensor(tmp[:, :, :, :], oh[:, :, :, :], slot[:, :, :].unsqueeze(1).to_broadcast(
                    [P, 2, NC, NE]), ALU.mult).then_inc(s_dvr, 1)
                dve.wait_ge(s_dvr, R.made(1))
                V.tensor_reduce(posf[:, :, :].rearrange("p i c -> p (i c)"),
                                tmp[:, :, :, :].rearrange("p i c e -> p (i c) e"), AX_X, ALU.add).then_inc(s_dvr, 1)
                dve.wait_ge(s_dvr, R.made(1))
                g0 = k.b * (4 * NC) + k.par * 2 * NC
                V.tensor_copy(pos_all[:, bass.ds(g0, 2 * NC)],
                              posf[:, :, :].rearrange("p i c -> p (i c)")).then_inc(s_dvr, 1)
                R.made(1)
                V.tensor_copy(posu[k.par][:, :, :], posf[:, :, :]).then_inc(s_pos, 1)

            def tile_table():
                steps = Steps()
                dve.wait_ge(s_pos, count(LAST, 1, 1))
                tiles = [P, NE, NTR]
                tj = cst[:, C_TJ:C_E].rearrange("p (e j) -> p e j", e=NE)
                reg = cst[:, C_REG:C_T16]
                V.tensor_copy(pads[0:1, :], base[0:1, :]).then_inc(s_pads, 1)
                V.tensor_tensor(cnt[:, :], base[:, :], reg, ALU.subtract).then_inc(s_v, 1)
                dve.wait_ge(s_v, steps.made(1))
                V.tensor_tensor(more[:, :, :], cnt[:, :].unsqueeze(2).to_broadcast([P, NE, NTS]),
                                     cst[:, C_T16:C_TJ].rearrange("p (e j) -> p e j", e=NE), ALU.is_gt).then_inc(s_v, 1)
                dve.wait_ge(s_v, steps.made(1))
                V.tensor_reduce(nt[:, :], more[:, :, :], AX_X, ALU.add).then_inc(s_v, 1)
                dve.wait_ge(s_v, steps.made(1))
                V.tensor_copy(end[:, 0:1], nt[:, 0:1]).then_inc(s_v, 1)
                dve.wait_ge(s_v, steps.made(1))
                for e in range(1, NE):
                    V.tensor_tensor(end[:, e:e + 1], end[:, e - 1:e], nt[:, e:e + 1], ALU.add).then_inc(s_v, 1)
                    dve.wait_ge(s_v, steps.made(1))
                V.tensor_tensor(first[:, :], end[:, :], nt[:, :], ALU.subtract).then_inc(s_v, 1)
                dve.wait_ge(s_v, steps.made(1))
                V.tensor_tensor(past[:, :, :], tj, end[:, :].unsqueeze(2).to_broadcast(tiles),
                                ALU.is_ge).then_inc(s_v, 1)
                dve.wait_ge(s_v, steps.made(1))
                V.tensor_tensor(begun[:, :, :], tj, first[:, :].unsqueeze(2).to_broadcast(tiles),
                                ALU.is_ge).then_inc(s_v, 1)
                dve.wait_ge(s_v, steps.made(1))
                V.tensor_reduce(tf[:, 0, :], past[:, :, :].rearrange("p e j -> p j e"), AX_X, ALU.add).then_inc(s_v, 1)
                dve.wait_ge(s_v, steps.made(1))
                V.tensor_scalar(tf[:, 0, :], tf[:, 0, :], float(NE - 1), 1.0, ALU.min, ALU.add).then_inc(s_v, 1)
                dve.wait_ge(s_v, steps.made(1))
                V.scalar_tensor_tensor(out=off[:, :], in0=first[:, :], scalar=-float(TILE), in1=reg,
                                            op0=ALU.mult, op1=ALU.add).then_inc(s_v, 1)
                dve.wait_ge(s_v, steps.made(1))
                V.scalar_tensor_tensor(out=row[:, :, :], in0=tj, scalar=float(TILE),
                                            in1=off[:, :].unsqueeze(2).to_broadcast(tiles),
                                            op0=ALU.mult, op1=ALU.add).then_inc(s_v, 1)
                dve.wait_ge(s_v, steps.made(1))
                V.tensor_tensor(begun[:, :, :], begun[:, :, :], past[:, :, :], ALU.subtract).then_inc(s_v, 1)
                dve.wait_ge(s_v, steps.made(1))
                V.tensor_tensor(row[:, :, :], row[:, :, :], begun[:, :, :], ALU.mult).then_inc(s_v, 1)
                dve.wait_ge(s_v, steps.made(1))
                V.tensor_reduce(tf[:, 1, :], row[:, :, :].rearrange("p e j -> p j e"), AX_X, ALU.add).then_inc(s_v, 1)
                dve.wait_ge(s_v, steps.made(1))
                V.scalar_tensor_tensor(out=tf[:, 1, :], in0=past[:, NE - 1, :], scalar=float(DUMMY),
                                            in1=tf[:, 1, :], op0=ALU.mult, op1=ALU.add).then_inc(s_v, 1)
                dve.wait_ge(s_v, steps.made(1))
                V.tensor_copy(table[:, :, :], tf[0:1, :, :]).then_inc(s_v, 1)
                V.scalar_tensor_tensor(out=off_y[:, :], in0=first[:, :], scalar=float(TILE), in1=reg,
                                       op0=ALU.mult, op1=ALU.subtract).then_inc(s_v, 1)
                dve.wait_ge(s_v, steps.made(2))

            halo(FIRST)
            soft_first(FIRST)
            tap_pair(FIRST, 0, 0)
            soft_ratio(FIRST)
            soft_square(FIRST)
            for i in range(len(SERIES) - 2, 0, -1):
                soft_term(FIRST, i)
            soft_last(FIRST)
            tap_pair(FIRST, 0, 1)
            tap_pair(FIRST, 0, 2)
            for n in range(NCONV - 1):
                tap(FIRST, 2, n)
            for n in range(NCONV - 1):
                tap_pair(FIRST, 3, n)
            scores(FIRST, 0)
            by_dt(FIRST, 0)
            decayed(FIRST, 0)

            def body(k, first, last):
                f = k.next()
                for c in range(NC):
                    q, n = following(k, c)
                    inherited(k, c)
                    if c == 0 and not last:
                        split_x(f)
                    if c or not first:
                        residual(*before(k, c))
                    outputs(k, c)
                    if c < NC - 1:
                        state(k, c)
                        gated(k, c)
                    else:
                        gated(k, c)
                        state(k, c)
                    if c or not first:
                        finish(*before(k, c))
                    if n or not last:
                        scores(q, n)
                    if c == 3 and not first:
                        ranks(k.prev())
                        slots(k.prev())
                    if c == 0 and not last:
                        halo(f)
                    if n or not last:
                        by_dt(q, n)
                        decayed(q, n)
                    if c == 3 and not first:
                        shares(k.prev())
                    if c == 0 and not last:
                        soft_first(f)
                        tap_pair(f, 0, 0)
                        tap_pair(f, 0, 1)
                        tap_pair(f, 0, 2)
                    if c == 1:
                        if not last:
                            soft_and_taps(f)
                        if not first:
                            logits(k.prev())
                        if not last:
                            soft_end(f)
                    if c == 2:
                        if not first:
                            choices(k.prev())
                        if not last:
                            for i in range(NCONV - 1):
                                tap_pair(f, 3, i)
            loop(dve, body)
            residual(LAST, NC - 1)
            finish(LAST, NC - 1)
            logits(LAST)
            choices(LAST)
            ranks(LAST)
            slots(LAST)
            shares(LAST)
            tile_table()

        @block.tensor
        def _(pe):
            start(pe, s_pf, s_XT, s_G, s_D, s_Y, s_yi, s_ds, s_YT, s_O, s_RT, s_lg, s_rk)
            pe.wait_ge(s_wlo, 1)
            mm = nc.tensor.matmul
            ident = cst[:, C_ID:C_ID + P]

            def product(dst, lhs, rhs):
                for kt in range(KT):
                    (lh, ll), (rh, rl) = lhs(kt), rhs(kt)
                    mm(dst, lh, rh, start=(kt == 0), stop=False)
                    mm(dst, lh, rl, start=False, stop=False)
                    last = mm(dst, ll, rh, start=False, stop=(kt == KT - 1))
                return last

            def x_of(kt, c):
                return x_hi[:, kt, c * Q:(c + 1) * Q], x_lo[:, kt, c * Q:(c + 1) * Q]

            def w_of(kt, lo, n):
                return w_hi[:, kt, lo:lo + n], w_lo[:, kt, lo:lo + n]

            def dt_rows(f):
                pe.wait_ge(s_xhi, count(f, 1, 1))
                pe.wait_ge(s_xlo, count(f, 1, 1))
                pe.wait_ge(s_pff, count(f, PF_USES, DT_ROWS - 1))
                product(PF[DT_ROWS % 2][0:NH, :], lambda kt: w_of(kt, DT0, NH),
                        lambda kt: (x_hi[:, kt, :], x_lo[:, kt, :])).then_inc(s_pf, 1)

            def dt_tokens(f):
                pe.wait_ge(s_pff, count(f, PF_USES, DT_TOKENS - 1))
                for c in range(NC):
                    last = mm(PF[DT_TOKENS % 2][:, c * NH:(c + 1) * NH], dtT[:, c * Q:(c + 1) * Q],
                              cst[0:NH, C_ID:C_ID + NH], start=True, stop=True)
                last.then_inc(s_pf, 1)

            def channels(f, u):
                pe.wait_ge(s_pff, count(f, PF_USES, CHANNEL_USE[u] - 1))
                product(PF[CHANNEL_USE[u] % 2][:, :], lambda kt: w_of(kt, X0 + CHANNELS[u] * P, P),
                        lambda kt: (x_hi[:, kt, :], x_lo[:, kt, :])).then_inc(s_pf, 1)

            def sums(f):
                pe.wait_ge(s_pff, count(f, PF_USES, SUMS - 1))
                pe.wait_ge(s_dt, count(f, 1, 1))
                al = a[f.par][:, :, :].rearrange("p c h -> p (c h)")
                for i, m in enumerate((C_INCL, C_GTR, C_ONE)):
                    last = mm(PF[SUMS % 2][:, i * NC * NH:(i + 1) * NC * NH], cst[:, m:m + P], al,
                              start=True, stop=True)
                last.then_inc(s_pf, 1)

            def gates(f, c):
                pe.wait_ge(s_pff, count(f, PF_USES, GATES + c - 1))
                product(PF[(GATES + c) % 2][:, :], lambda kt: x_of(kt, c),
                        lambda kt: w_of(kt, Z0, DI)).then_inc(s_pf, 1)

            def x_tokens(q, c):
                cols = slice(c * Q, (c + 1) * Q)
                if c == 0:
                    pe.wait_ge(s_sil, count(q, 3, 3))
                pe.wait_ge(s_yT, count(q, NC, max(c - 1, 0)))
                for m in range(MX):
                    last = nc.tensor.transpose(PX[:, m * P:(m + 1) * P], xch[q.par][:, m, cols], ident)
                last.then_inc(s_XT, 1)

            def scores(q, c):
                cols = slice(c * Q, (c + 1) * Q)
                if c == 0:
                    pe.wait_ge(s_sil, count(q, 3, 2))
                pe.wait_ge(s_Gm, count(q, NC, c))
                pe.wait_ge(s_Bt, count(q, NC, c))
                pe.wait_ge(s_r, count(q, NC, c - 1))
                mm(PG[:, 0:Q], BT[q.par][:, cols], CT[q.par][:, cols], start=True, stop=True)
                nc.tensor.transpose(PG[:, Q:Q + NST], BT[q.par][:, cols],
                                    cst[0:NST, C_ID:C_ID + NST]).then_inc(s_G, 1)

            def decays(q, c):
                pe.wait_ge(s_am, count(q, NC, c + 1))
                pe.wait_ge(s_E, count(q, NC, c))
                for bank, h in ((PD0, 0), (PD1, NH // 2)):
                    for am in (am_hi, am_lo):
                        last = mm(bank[:, :], after[:, :], am[:, h:h + NH // 2, :].rearrange("p h t -> p (h t)"),
                                  start=(am is am_hi), stop=(am is am_lo))
                last.then_inc(s_D, 1)

            def mix(k, c, first):
                cols = slice(c * Q, (c + 1) * Q)
                pe.wait_ge(s_S, count(k, NC, c))
                if c == 0 and first:
                    pe.wait_ge(s_S0, 1)
                mm(PI[:, :], CT[k.par][:, cols], S[:, :], start=True, stop=True).then_inc(s_yi, 1)
                pe.wait_ge(s_ya, count(k, NC, c))
                if c == 2 and not first:
                    pe.wait_ge(s_lr, count(k, 1, 0))
                if c == 0 and not first:
                    pe.wait_ge(s_rr, count(k, 1, -1))
                pe.wait_ge(s_xd, count(k, NC, c + 1))
                pe.wait_ge(s_M, count(k, NC, c + 1))
                for m in range(MX):
                    mm(PY[:, m * P:(m + 1) * P], xch[k.par][:, m, cols], Dd[:, m, :], start=True, stop=False)
                    for h in (2 * m, 2 * m + 1):
                        last = mm(PY[:, h * HD:(h + 1) * HD], M[c % 2][:, h, :],
                                  xdt[c % 2][:, h * HD:(h + 1) * HD], start=False, stop=(h % 2 == 1))
                last.then_inc(s_Y, 1)
                pe.wait_ge(s_Bt, count(k, NC, c + 1))
                pe.wait_ge(s_xw, count(k, NC, c + 1))
                pe.wait_ge(s_t1, count(k, NC, c + 1))
                mm(PI[0:NST, :], B_tok[c % 2][:, :], xw[c % 2][:, :], start=True, stop=True).then_inc(s_ds, 1)

            def turned(k, c):
                pe.wait_ge(s_xt, count(k, NC, min(c + 2, NC)))
                pe.wait_ge(s_yz, count(k, NC, c + 1))
                for m in range(MX):
                    last = nc.tensor.transpose(PX[:, m * P:(m + 1) * P], yz[c % 2][:, m * P:(m + 1) * P], ident)
                last.then_inc(s_YT, 1)

            def project(k, c, more):
                pe.wait_ge(s_yT, count(k, NC, c + 1))
                pe.wait_ge(s_Gm, count(k, NC, c + 1 + more))
                pe.wait_ge(s_Bt, count(k, NC, c + 1 + more))
                pe.wait_ge(s_r, count(k, NC, c))
                for m in range(MX):
                    last = mm(PG[:, DM:2 * DM], yT[:, m, :], wo[:, m, :], start=(m == 0), stop=(m == MX - 1))
                last.then_inc(s_O, 1)

            def router_rows(k, half):
                pe.wait_ge(s_x1, count(k, NC, 2 * half + 2))
                pe.wait_ge(s_rT, count(k, 2, half))
                for i in range(2):
                    for kt in range(KT):
                        at = (i * KT + kt) * P
                        last = nc.tensor.transpose(PY[:, at:at + P],
                                                   x1[k.par][:, 2 * half + i, kt * P:(kt + 1) * P], ident)
                last.then_inc(s_RT, 1)

            def logits(k):
                pe.wait_ge(s_rT, count(k, 2, 2))
                for c in range(NC):
                    for kt in range(KT):
                        last = mm(PY[:, c * NE:(c + 1) * NE], x1T[:, c, kt, :], wr_sb[:, kt, :],
                                  start=(kt == 0), stop=(kt == KT - 1))
                last.then_inc(s_lg, 1)

            def ranks(k):
                pe.wait_ge(s_mask, count(k, 1, 1))
                mk = mask[:, :, :].rearrange("p c e -> p (c e)")
                mm(PY[:, 0:NC * NE], cst[:, C_LESS:C_LESS + P], mk, start=True, stop=True)
                mm(PY[:, NC * NE:2 * NC * NE], cst[:, C_ONE:C_ONE + P], mk, start=True, stop=True).then_inc(s_rk, 1)

            dt_rows(FIRST)
            channels(FIRST, 0)
            pe.wait_ge(s_small, 144)
            dt_tokens(FIRST)
            for u in range(1, 5):
                channels(FIRST, u)
            sums(FIRST)
            pe.wait_ge(s_wlo, 2)
            gates(FIRST, 0)
            gates(FIRST, 1)
            pe.wait_ge(s_Dd, MX + 1)
            decays(FIRST, 0)
            scores(FIRST, 0)
            x_tokens(FIRST, 0)
            gates(FIRST, 2)
            gates(FIRST, 3)
            pe.wait_ge(s_wo, MX)

            def body(k, first, last):
                f = k.next()
                for c in range(NC):
                    q, n = following(k, c)
                    more = 0 if last and n == 0 else 1
                    if c == 3 and more:
                        decays(q, n)
                    mix(k, c, first)
                    if c == 3:
                        if more:
                            scores(q, n)
                            gates(f, 3)
                        turned(k, c)
                        if not first:
                            pe.wait_ge(s_ya, count(k, NC, NC))
                            ranks(k.prev())
                        if more:
                            x_tokens(q, n)
                        project(k, c, more)
                        continue
                    x_tokens(q, n)
                    scores(q, n)
                    decays(q, n)
                    if c == 0:
                        if not last:
                            dt_rows(f)
                            channels(f, 0)
                            dt_tokens(f)
                        turned(k, c)
                        if not last:
                            channels(f, 1)
                            channels(f, 2)
                    if c == 1:
                        if not first:
                            pe.wait_ge(s_ya, count(k, NC, 2))
                            router_rows(k.prev(), 0)
                        if not last:
                            channels(f, 3)
                        if not first:
                            router_rows(k.prev(), 1)
                        turned(k, c)
                        if not last:
                            channels(f, 4)
                        if not first:
                            logits(k.prev())
                    if c == 2:
                        if not last:
                            sums(f)
                            gates(f, 0)
                        turned(k, c)
                        if not last:
                            gates(f, 1)
                            gates(f, 2)
                    project(k, c, more)

            loop(pe, body)
            pe.wait_ge(s_ya, count(LAST, NC, NC))
            pe.wait_ge(s_rr, count(LAST, 1, 0))
            router_rows(LAST, 0)
            router_rows(LAST, 1)
            logits(LAST)
            ranks(LAST)


ROUTED, SHARED, NONE = "routed", "shared", None
PARTS = [(0, GU), (GU, 2 * GU), (2 * GU, WROW)]


def moe(nc, experts, xs, ys, out, pos_all, off_y, share_all, cst, table):
    with ExitStack() as ctx:
        def sb(name, shape, dt=F32):
            return ctx.enter_context(nc.sbuf_tensor(name, shape, dt))

        def bank(name):
            return ctx.enter_context(nc.psum_tensor(name, [P, 512], F32))

        def sem(name):
            return ctx.enter_context(nc.semaphore(name))

        def pair(name, shape, dt=F32):
            return [sb(f"{name}{i}", shape, dt) for i in range(2)]

        w_raw = sb("we_raw", [P, WROW])
        w_hi = pair("we_hi", [P, WROW], F32R)
        w_lo = pair("we_lo", [P, WROW], F32R)
        rows = pair("rows", [P, 2, DM])
        xt_hi = pair("xt_hi", [P, KT, TILE], F32R)
        xt_lo = pair("xt_lo", [P, KT, TILE], F32R)
        gate = pair("gate", [P, TILE])
        h = pair("h", [P, TILE])
        h_hi = pair("h_hi", [P, NCH, TILE], F32R)
        h_lo = pair("h_lo", [P, NCH - 1, TILE], F32R)
        y_sb = pair("y_sb", [P, 2, DM])
        x1r = pair("x1r", [P, 2, DM])
        got = pair("got", [P, 2, 2, DM])
        idx = pair("idx", [P, 4], U32)
        share = pair("share", [P, 4])
        o = pair("o", [P, 2, DM])
        st6 = sb("mst6", [P, 2, 6])
        mv = sb("mmv", [P, 2, 2])
        rstd = sb("mrstd", [P, 2])
        mhalf = sb("mmhalf", [P, 2])

        pos_y = sb("pos_y", [P, 2 * T // P], U32)
        by = sb("by", [P, 2 * T // P])
        inreg = sb("inreg", [P, 2 * T // P])
        hop = sb("hop", [P, 1])

        H = [bank(f"H{i}") for i in range(NCH)]
        PT, PY = bank("PT"), bank("PYo")

        s_part = [sem(f"s_part{i}") for i in range(3)]
        s_rows = [sem("s_rows0"), sem("s_rows1")]
        s_x1r = [sem("s_x1r0"), sem("s_x1r1")]
        s_got = [sem("s_got0"), sem("s_got1")]
        s_ys = [sem("s_ys0"), sem("s_ys1")]
        s_out = [sem("s_out0"), sem("s_out1")]
        (s_wh, s_wl, s_wlp, s_xh, s_xl, s_T, s_gu, s_dn, s_sg, s_h, s_hh, s_hl, s_y, s_yr, s_idx, s_shr,
         s_o, s_mvr, s_rstd, s_mh, s_c, s_pc, s_hold) = [sem("m_" + n) for n in (
             "wh wl wlp xh xl T gu dn sg h hh hl y yr idx shr o mvr rstd mh c pc hold").split()]
        s_v, s_posy = sem("m_v"), sem("m_posy")
        block = ctx.enter_context(nc.Block())

        def steps(eng, step, before=None):
            kind = lambda j: NONE if not 0 <= j < NTR + NTS else ROUTED if j < NTR else SHARED

            def one(j):
                step(Block(j // 2, j % 2), *[kind(j + i) for i in (-1, 0, 1, 2)])

            one(0)
            with eng.Fori(0, NTR // 2 - 2) as b:
                step(Block(b, 1), ROUTED, ROUTED, ROUTED, ROUTED)
                step(Block(b + 1, 0), ROUTED, ROUTED, ROUTED, ROUTED)
            for j in range(NTR - 3, NTR + 1):
                one(j)
            with eng.Fori(NTR // 2, (NTR + NTS) // 2 - 2) as b:
                step(Block(b, 1), SHARED, SHARED, SHARED, SHARED)
                step(Block(b + 1, 0), SHARED, SHARED, SHARED, SHARED)
            for j in range(NTR + NTS - 3, NTR + NTS + 1):
                one(j)

        def sharedno(k):
            return Block(k.b - NTR // 2, k.par)

        def is_(k, j):
            return isinstance(k.b, int) and 2 * k.b + k.par == j

        def rowsof(dram, row):
            return dram[bass.ds(row, TILE), :].rearrange("(a p) d -> p a d", p=P)

        @block.sync
        def _(sp):
            for s in s_out + s_ys:
                sp.sem_inc(s, 16)

            def tile_no(k):
                return k.b * 2 + k.par

            def entry(k, i, top):
                return sp.value_load(table[0:1, i, bass.ds(tile_no(k), 1)], min_val=0, max_val=top)

            def load_rows(k, kind):
                if kind == ROUTED:
                    src = rowsof(xs, entry(k, 1, DUMMY))
                else:
                    src = rowsof(xs, tile_no(sharedno(k)) * TILE)
                sp.dma_start(rows[k.par][:, :, :], src).then_inc(s_rows[k.par], 16)

            def load(k, kind, first_tile=False):
                sp.wait_ge(s_T, count(k, 1, -1))
                sp.sem_inc(s_hold, 1)
                if not first_tile:
                    load_rows(k, kind)
                if kind == ROUTED or is_(k, NTR):
                    expert = entry(k, 0, NE) if kind == ROUTED else 0
                    for i, (c0, c1) in enumerate(PARTS):
                        sp.wait_ge(s_wh, count(k, 3, i - 2))
                        sp.sem_inc(s_hold, 1)
                        if i < 2:
                            sp.wait_ge(s_wl, count(k, 2, i - 1))
                            sp.sem_inc(s_hold, 1)
                        else:
                            sp.wait_ge(s_wlp, count(k, 1, 0))
                            sp.sem_inc(s_hold, 1)
                        sp.dma_start(w_raw[:, c0:c1],
                                     experts[bass.ds(expert, 1), :, c0:c1].rearrange("e p n -> (e p) n")
                                     ).then_inc(s_part[i], 16)
                        if first_tile and i == 0:
                            load_rows(k, kind)

            load(Block(0, 0), ROUTED, first_tile=True)
            load(Block(0, 1), ROUTED)

            def step(k, prev, this, nxt, nxt2):
                if nxt2:
                    load(k.next().next(), nxt2)
                kp = k.prev() if prev else None
                if this == SHARED:
                    s = sharedno(k)
                    sp.wait_ge(s_o, count(s, 1, -1))
                    sp.sem_inc(s_hold, 1)
                    sp.dma_start(x1r[k.par][:, :, :], rowsof(xs, tile_no(s) * TILE)).then_inc(s_x1r[k.par], 16)
                if prev == ROUTED:
                    sp.wait_ge(s_y, count(kp, 1, 1))
                    sp.sem_inc(s_hold, 1)
                    sp.dma_start(rowsof(ys, tile_no(kp) * TILE), y_sb[kp.par][:, :, :]).then_inc(s_ys[kp.par], 16)
                if prev == SHARED:
                    s = sharedno(kp)
                    sp.wait_ge(s_o, count(s, 1, 1))
                    sp.sem_inc(s_hold, 1)
                    sp.dma_start(rowsof(out, tile_no(s) * TILE), o[kp.par][:, :, :]).then_inc(s_out[kp.par], 16)

            steps(sp, step)
            for i in range(2):
                sp.wait_ge(s_out[i], 16 * (NTS // 2) + 16)

        @block.gpsimd
        def _(pool):
            for s in (s_wlp, s_idx, s_shr, s_rstd, s_pc):
                pool.sem_inc(s, BIAS)
            nc.gpsimd.memset(mhalf[:, :], -0.5).then_inc(s_mh, 1)
            pool.wait_ge(s_mh, 1)

            def split(k):
                c0, c1 = PARTS[2]
                pool.wait_ge(s_part[2], k.count(16, 16))
                pool.wait_ge(s_wh, count(k, 3, 3))
                pool.wait_ge(s_dn, count(k, 1, -1))
                nc.gpsimd.tensor_tensor(w_lo[k.par][:, c0:c1], w_raw[:, c0:c1], w_hi[k.par][:, c0:c1].bitcast(F32),
                                        ALU.subtract).then_inc(s_wlp, 1)

            split(Block(0, 0))

            def step(k, prev, this, nxt, nxt2):
                if nxt == ROUTED or is_(k, NTR - 1):
                    split(k.next())
                if this == SHARED:
                    s = sharedno(k)
                    if is_(k, NTR):
                        pool.wait_ge(s_posy, 1)
                        for i in range(2):
                            pool.wait_ge(s_ys[i], 16 * (NTR // 2) + 16)
                    pool.wait_ge(s_o, count(s, 1, -1))
                    pool.sem_inc(s_hold, 1)
                    col = s.b * (4 * 2) + 2 * s.par
                    for i in range(2):
                        nc.gpsimd.tensor_copy(idx[k.par][:, 2 * i:2 * i + 2],
                                              pos_y[:, bass.ds(col + 4 * i, 2)]).then_inc(s_idx, 1)
                        nc.gpsimd.tensor_copy(share[k.par][:, 2 * i:2 * i + 2],
                                              share_all[:, bass.ds(col + 4 * i, 2)]).then_inc(s_shr, 1)
                    pool.wait_ge(s_idx, count(s, 2, 2))
                    pool.sem_inc(s_hold, 1)
                    for i in range(2):
                        for half in range(2):
                            pool.indirect_dma_start(
                                out=got[k.par][:, i, half, :], out_offset=None, in_=ys,
                                in_offset=bass.IndirectOffsetOnAxis(ap=idx[k.par][:, 2 * i + half:2 * i + half + 1],
                                                                    axis=0)).then_inc(s_got[k.par], 16)
                if prev == SHARED:
                    s = sharedno(k.prev())
                    pool.wait_ge(s_mvr, count(s, 1, 1))
                    pool.sem_inc(s_hold, 1)
                    nc.gpsimd.tensor_scalar(rstd[:, :], mv[:, :, 1], EPS, None, ALU.add).then_inc(s_pc, 1)
                    pool.wait_ge(s_pc, count(s, 1, 1))
                    nc.gpsimd.tensor_tensor(rstd[:, :], rstd[:, :], mhalf[:, :], ALU.pow).then_inc(s_rstd, 1)

            steps(pool, step)

        @block.scalar
        def _(act):
            for s in (s_wh, s_xh, s_sg, s_hh, s_y):
                act.sem_inc(s, BIAS)

            def split(k, i):
                c0, c1 = PARTS[i]
                act.wait_ge(s_part[i], k.count(16, 16))
                if i < 2:
                    act.wait_ge(s_gu, count(k, NCH, -NCH))
                else:
                    act.wait_ge(s_dn, count(k, 1, -1))
                nc.scalar.activation(w_hi[k.par][:, c0:c1], w_raw[:, c0:c1], ACT.Copy).then_inc(s_wh, 1)

            def split_x(k):
                act.wait_ge(s_T, count(k, 1, 1))
                act.wait_ge(s_gu, count(k, NCH, -NCH))
                nc.scalar.activation(xt_hi[k.par][:, :, :].rearrange("p a t -> p (a t)"), PT[:, :],
                                     ACT.Copy).then_inc(s_xh, 1)

            split_x(Block(0, 0))
            for i in range(3):
                split(Block(0, 0), i)

            def step(k, prev, this, nxt, nxt2):
                def silu(c):
                    act.wait_ge(s_gu, count(k, NCH, c + 1))
                    act.wait_ge(s_h, count(k, NCH, c - 1))
                    if c < NCH - 1:
                        nc.scalar.activation(gate[c % 2][:, :], H[c][:, 0:TILE], ACT.Silu).then_inc(s_sg, 1)
                    else:
                        nc.scalar.activation(gate[c % 2][64:P, :], H[c][0:64, 0:TILE], ACT.Silu).then_inc(s_sg, 1)

                def high(c):
                    lo = 0 if c < NCH - 1 else 64
                    act.wait_ge(s_h, count(k, NCH, c + 1))
                    act.wait_ge(s_dn, count(k, 1, -1))
                    nc.scalar.activation(h_hi[k.par][lo:P, c, :], h[c % 2][lo:P, :], ACT.Copy).then_inc(s_hh, 1)

                if this:
                    silu(0)
                    silu(1)
                    high(0)
                    high(1)
                if nxt == ROUTED or is_(k, NTR - 1):
                    for i in range(3):
                        split(k.next(), i)
                if prev == ROUTED:
                    kp = k.prev()
                    act.wait_ge(s_dn, count(kp, 1, 1))
                    act.wait_ge(s_ys[kp.par], sent(kp, 1))
                    nc.scalar.activation(y_sb[kp.par][:, :, :].rearrange("p a d -> p (a d)"), PY[:, :],
                                         ACT.Copy).then_inc(s_y, 1)
                if nxt:
                    split_x(k.next())
                if this:
                    silu(2)
                    silu(3)
                    high(2)
                    silu(4)
                    high(3)
                    silu(5)
                    high(4)
                    high(5)

            steps(act, step)

        @block.vector
        def _(dve):
            V = nc.vector
            for s in (s_wl, s_xl, s_h, s_hl, s_yr, s_o, s_mvr, s_c):
                dve.sem_inc(s, BIAS)
            C = Steps(9)

            def split(k, i):
                c0, c1 = PARTS[i]
                dve.wait_ge(s_part[i], k.count(16, 16))
                dve.wait_ge(s_wh, count(k, 3, i + 1))
                V.tensor_tensor(w_lo[k.par][:, c0:c1], w_raw[:, c0:c1], w_hi[k.par][:, c0:c1].bitcast(F32),
                                ALU.subtract).then_inc(s_wl, 1)

            def split_x(k):
                dve.wait_ge(s_xh, count(k, 1, 1))
                V.tensor_tensor(xt_lo[k.par][:, :, :].rearrange("p a t -> p (a t)"), PT[:, :],
                                xt_hi[k.par][:, :, :].rearrange("p a t -> p (a t)").bitcast(F32),
                                ALU.subtract).then_inc(s_xl, 1)

            split_x(Block(0, 0))
            for i in range(2):
                split(Block(0, 0), i)

            def rows_of_y():
                own = Steps()
                V.tensor_scalar(by[:, :], pos_all[:, :], off_y[:, 0:1], None, ALU.add).then_inc(s_v, 1)
                dve.wait_ge(s_v, own.made(1))
                for e in range(1, NE):
                    V.tensor_tensor(hop[:, :], off_y[:, e:e + 1], off_y[:, e - 1:e], ALU.subtract).then_inc(s_v, 1)
                    dve.wait_ge(s_v, own.made(1))
                    V.tensor_scalar(inreg[:, :], pos_all[:, :], float(R0 + e * CAP), hop[:, :], ALU.is_ge,
                                    ALU.mult).then_inc(s_v, 1)
                    dve.wait_ge(s_v, own.made(1))
                    V.tensor_tensor(by[:, :], by[:, :], inreg[:, :], ALU.add).then_inc(s_v, 1)
                    dve.wait_ge(s_v, own.made(1))
                V.tensor_copy(pos_y[:, :], by[:, :]).then_inc(s_posy, 1)

            def residual(k):
                s = sharedno(k)
                dve.wait_ge(s_dn, count(k, 1, 1))
                dve.wait_ge(s_x1r[k.par], landed(s, 1))
                dve.wait_ge(s_out[k.par], sent(s, 1))
                V.tensor_tensor(o[k.par][:, :, :].rearrange("p a d -> p (a d)"), PY[:, :],
                                x1r[k.par][:, :, :].rearrange("p a d -> p (a d)"), ALU.add).then_inc(s_yr, 1)

            def combine(k):
                s = sharedno(k)
                C.begin(s)
                dve.wait_ge(s_yr, count(s, 1, 1))
                dve.wait_ge(s_got[k.par], landed(s, 4))
                dve.wait_ge(s_shr, count(s, 2, 2))
                for i in range(2):
                    for half in range(2):
                        ins = V.scalar_tensor_tensor(
                            out=o[k.par][:, half, :], in0=got[k.par][:, i, half, :],
                            scalar=share[k.par][:, 2 * i + half:2 * i + half + 1],
                            in1=o[k.par][:, half, :], op0=ALU.mult, op1=ALU.add)
                        ins.then_inc(s_c, 1)
                        C.made(1)
                    dve.wait_ge(s_c, C.made(0))
                for half in range(2):
                    V.bn_stats(st6[:, half, :], o[k.par][:, half, :]).then_inc(s_c, 1)
                    C.made(1)
                dve.wait_ge(s_c, C.made(0))
                dve.sem_inc(s_hold, 1)
                V.bn_aggr(mv[:, 0, :], st6[:, 0, :]).then_inc(s_c, 1)
                C.made(1)
                V.bn_aggr(mv[:, 1, :], st6[:, 1, :]).then_inc(s_mvr, 1)
                dve.wait_ge(s_mvr, count(s, 1, 1))
                dve.wait_ge(s_c, C.made(0))
                dve.wait_ge(s_rstd, count(s, 1, 1))
                V.tensor_scalar(o[k.par][:, 0, :], o[k.par][:, 0, :], mv[:, 0, 0:1], rstd[:, 0:1],
                                         ALU.subtract, ALU.mult).then_inc(s_c, 1)
                C.made(1)
                V.tensor_scalar(o[k.par][:, 1, :], o[k.par][:, 1, :], mv[:, 1, 0:1], rstd[:, 1:2],
                                ALU.subtract, ALU.mult).then_inc(s_o, 1)
                V.memset(st6[0:1, 0, 0:1], 0.0).then_inc(s_c, 1)
                C.made(1)
                C.end()

            def step(k, prev, this, nxt, nxt2):
                def product(c):
                    lo = 0 if c < NCH - 1 else 64
                    up = H[c][lo:P, 0:TILE] if lo else H[c][:, TILE:2 * TILE]
                    dve.wait_ge(s_sg, count(k, NCH, c + 1))
                    dve.wait_ge(s_hh, count(k, NCH, c - 1))
                    dve.wait_ge(s_hl, count(k, NCH, c - 1))
                    V.tensor_tensor(h[c % 2][lo:P, :], gate[c % 2][lo:P, :], up, ALU.mult).then_inc(s_h, 1)

                def low(c):
                    lo = 0 if c < NCH - 1 else 64
                    dve.wait_ge(s_hh, count(k, NCH, c + 1))
                    dst = h_lo[k.par][:, c, :] if c < NCH - 1 else h_hi[k.par][0:64, c, :]
                    V.tensor_tensor(dst, h[c % 2][lo:P, :],
                                    h_hi[k.par][lo:P, c, :].bitcast(F32), ALU.subtract).then_inc(s_hl, 1)

                if this:
                    product(0)
                    product(1)
                    low(0)
                    low(1)
                if prev == SHARED:
                    residual(k.prev())
                if nxt == ROUTED or is_(k, NTR - 1):
                    for i in range(2):
                        split(k.next(), i)
                if nxt:
                    split_x(k.next())
                if this:
                    product(2)
                    product(3)
                    low(2)
                    product(4)
                    low(3)
                    product(5)
                    low(4)
                    low(5)
                if prev == SHARED:
                    combine(k.prev())
                if is_(k, NTR - 3):
                    rows_of_y()

            steps(dve, step)

        @block.tensor
        def _(pe):
            mm = nc.tensor.matmul
            for s in (s_T, s_gu, s_dn):
                pe.sem_inc(s, BIAS)

            def turn(k):
                pe.wait_ge(s_rows[k.par], landed(k, 1))
                pe.wait_ge(s_xl, count(k, 1, 0))
                for kt in range(KT):
                    for half in range(2):
                        at = kt * TILE + half * P
                        last = nc.tensor.transpose(PT[:, at:at + P], rows[k.par][:, half, kt * P:(kt + 1) * P],
                                                   cst[:, C_ID:C_ID + P])
                last.then_inc(s_T, 1)

            turn(Block(0, 0))

            def down(k, kind):
                wp = k.par if kind == ROUTED else 0
                pe.wait_ge(s_hl, count(k, NCH, NCH))
                if kind == ROUTED:
                    pe.wait_ge(s_wlp, count(k, 1, 1))
                    pe.wait_ge(s_y, count(k, 1, 0))
                else:
                    pe.wait_ge(s_wlp, count(Block(NTR // 2, 0), 1, 1))
                    pe.wait_ge(s_y, count(Block(NTR // 2, 0), 1, 0))
                    pe.wait_ge(s_yr, count(sharedno(k), 1, 0))
                for half in range(2):
                    dst = PY[:, half * DM:(half + 1) * DM]
                    hs = slice(half * P, (half + 1) * P)
                    for c in range(NCH - 1):
                        ws = slice(2 * GU + c * DM, 2 * GU + (c + 1) * DM)
                        hh, hl = h_hi[k.par][:, c, hs], h_lo[k.par][:, c, hs]
                        mm(dst, hh, w_hi[wp][:, ws], start=(c == 0), stop=False)
                        mm(dst, hh, w_lo[wp][:, ws], start=False, stop=False)
                        mm(dst, hl, w_hi[wp][:, ws], start=False, stop=False)
                    ws = slice(2 * GU + (NCH - 1) * DM, 2 * GU + NCH * DM)
                    mm(dst, h_hi[k.par][:, NCH - 1, hs], w_hi[wp][:, ws], start=False, stop=False)
                    last = mm(dst, h_hi[k.par][64:P, NCH - 1, hs], w_lo[wp][64:P, ws], start=False, stop=True)
                last.then_inc(s_dn, 1)

            def step(k, prev, this, nxt, nxt2):
                wp = k.par if this == ROUTED else 0

                def gate_up(c):
                    pe.wait_ge(s_h, count(k, NCH, c - NCH + 1))
                    for j in range(2 if c < NCH - 1 else 1):
                        dst = H[c][:, j * TILE:(j + 1) * TILE]
                        for kt in range(KT):
                            ws = slice(kt * GU + (2 * c + j) * P, kt * GU + (2 * c + j + 1) * P)
                            xh, xl = xt_hi[k.par][:, kt, :], xt_lo[k.par][:, kt, :]
                            mm(dst, w_hi[wp][:, ws], xh, start=(kt == 0), stop=False)
                            mm(dst, w_lo[wp][:, ws], xh, start=False, stop=False)
                            last = mm(dst, w_hi[wp][:, ws], xl, start=False, stop=(kt == KT - 1))
                    last.then_inc(s_gu, 1)

                if this:
                    pe.wait_ge(s_xl, count(k, 1, 1))
                    if this == ROUTED or is_(k, NTR):
                        pe.wait_ge(s_wl, count(k, 2, 2))
                for c in range(NCH):
                    if this:
                        gate_up(c)
                    if c == 1 and prev:
                        down(k.prev(), prev)
                    if c == 2 and nxt:
                        turn(k.next())

            steps(pe, step)


_OUT = ((BATCH, SEQ, DM), "float32")


def kernel(**inputs):
    import concourse.bacc as bacc
    from concourse.bass_utils import run_bass_kernel_spmd

    a = {n: np.asarray(v) for n, v in inputs.items()}

    def on_partitions(v):
        return np.ascontiguousarray(np.broadcast_to(v.reshape(1, -1), (P, v.size)))

    def in_tiles(v):
        return np.ascontiguousarray(np.moveaxis(v.reshape(-1, P, *v.shape[1:]), 0, 1))

    def expert_rows(g, u, d):
        n = g.shape[0]
        gt, ut = (np.swapaxes(w, 1, 2).reshape(n, KT, P, FF) for w in (g, u))
        full = (NCH - 1) * P
        pairs = np.stack([w[..., :full].reshape(n, KT, P, NCH - 1, P) for w in (gt, ut)], axis=4)
        gu = np.concatenate([pairs.reshape(n, KT, P, -1), gt[..., full:], ut[..., full:]], axis=3)
        dt = np.swapaxes(d, 1, 2)
        dn = np.zeros((n, NCH, P, DM), np.float32)
        dn[:, :NCH - 1] = dt[:, :full].reshape(n, NCH - 1, P, DM)
        dn[:, NCH - 1] = np.concatenate([dt[:, full:], dt[:, full:]], axis=1)
        return np.ascontiguousarray(np.concatenate(
            [np.swapaxes(gu, 1, 2).reshape(n, P, -1), np.swapaxes(dn, 1, 2).reshape(n, P, -1)], axis=2))

    x = np.ascontiguousarray(a["L0_attn_x"].reshape(T, DM))
    experts = expert_rows(*(np.concatenate([a["L0_ffn_s" + w][None], a["L0_ffn_r" + w]]) for w in "gud"))
    arrays = {
        "x": x,
        "xT": in_tiles(np.ascontiguousarray(x.T)),
        "W_in": np.ascontiguousarray(a["L0_attn_W_in"]),
        "conv_w": np.ascontiguousarray(a["L0_attn_conv_w"]),
        "conv_b": in_tiles(a["L0_attn_conv_b"]),
        "dt_bias": on_partitions(a["L0_attn_dt_bias"]),
        "A_log": on_partitions(a["L0_attn_A_log"]),
        "Dh": on_partitions(a["L0_attn_D"]),
        "norm_w": in_tiles(a["L0_attn_norm_w"]),
        "W_out": np.ascontiguousarray(a["L0_attn_W_out"]),
        "experts": experts,
        "wr": in_tiles(np.ascontiguousarray(a["L0_ffn_wr"].T)),
        "rb": on_partitions(a["L0_ffn_rb"]),
        "consts": constants(),
    }
    nc = bacc.Bacc("TRN2", target_bir_lowering=False, num_devices=1)
    args = {n: nc.dram_tensor(n, v.shape, F32, kind="ExternalInput").ap() for n, v in arrays.items()}
    args["xs"] = nc.dram_tensor("xs", (NROWS, DM), F32).ap()
    args["ys"] = nc.dram_tensor("ys", (NTR * TILE, DM), F32).ap()
    args["out"] = nc.dram_tensor("out", (T, DM), F32, kind="ExternalOutput").ap()
    program(nc, **args)
    got = run_bass_kernel_spmd(nc, [arrays], core_ids=[0]).results[0]["out"]
    return got.reshape(_OUT[0])
```
